# Optimizing a Trainium2 kernel written in Bass

```python
import numpy as np
import jax
import jax.numpy as jnp

def _softmax(x, axis=-1):
    return jax.nn.softmax(x, axis=axis)

def _gelu(x):
    return jax.nn.gelu(x, approximate=True)

def _silu(x):
    return jax.nn.silu(x)

def _sigmoid(x):
    return jax.nn.sigmoid(x)

def _layernorm(x, axis=-1, eps=1e-05):
    m = jnp.mean(x, axis=axis, keepdims=True)
    v = jnp.var(x, axis=axis, keepdims=True)
    return (x - m) / jnp.sqrt(v + eps)

def _scatter_add(tgt, idx, src, axis=0):
    return tgt.at[idx].add(src)

def _segment_sum(src, seg, n):
    return jax.ops.segment_sum(src, seg, n)
kernel_name = 'mk_xattn_ffn_d4_seqx_r8_818874'

def setup_inputs(seed: int=0):
    np.random.seed(seed)
    _w = jnp.asarray

    def _rec_inputs():
        import jax
        import jax.numpy as jnp
        _rk = jax.random.key(seed)
        x = -0.0002928 + 1 * jax.random.normal(jax.random.fold_in(_rk, 1), (4, 256, 128), jnp.float32)
        _lenS = 256 - jax.random.randint(jax.random.fold_in(_rk, 7), (4,), 0, max(1, 256 // 4) + 1, jnp.int32)
        _lenS2 = 1601 - jax.random.randint(jax.random.fold_in(_rk, 8), (4,), 0, max(1, 1601 // 4) + 1, jnp.int32)
        _ctx_512P = jax.random.normal(jax.random.fold_in(_rk, 11), (4, 16, 64), jnp.float32)
        _ctx_512c = jax.random.dirichlet(jax.random.fold_in(_rk, 511), 0.3 * jnp.ones((16,), jnp.float32), (4, 1601))
        _ctx_512t = jnp.einsum('bsk,bkd->bsd', _ctx_512c, _ctx_512P)
        _ctx_512t = _ctx_512t * jax.lax.rsqrt(jnp.mean(jnp.square(_ctx_512t)) + 1e-12) * 0.953939
        ctx_512 = 0.00222621 + 0.99962 * (_ctx_512t + 0.3 * jax.random.normal(jax.random.fold_in(_rk, 611), (4, 1601, 64), jnp.float32))
        return (x, ctx_512)
    x, ctx_512 = _rec_inputs()

    def _L0_xattn_setup():
        import jax, jax.numpy as jnp
        import numpy as np
        B, T, TC, C, CC, H = (2, 256, 64, 128, 64, 16)
        D = C // H

        def _heads(t):
            b, l, _ = t.shape
            return t.reshape(b, l, H, D).transpose(0, 2, 1, 3)
        key = jax.random.key(seed)
        ks = jax.random.split(key, 18)
        w = lambda k, i, o: jax.random.normal(k, (i, o), jnp.float32) / np.sqrt(i).astype(np.float32)
        return {'x': jax.random.normal(ks[0], (B, T, C), jnp.float32), 'cross_input': jax.random.normal(ks[1], (B, TC, CC), jnp.float32), 'Wk': w(ks[2], C, C), 'bk': jnp.zeros((C,), jnp.float32), 'Wq': w(ks[3], C, C), 'bq': jnp.zeros((C,), jnp.float32), 'Wv': w(ks[4], C, C), 'bv': jnp.zeros((C,), jnp.float32), 'Wck': w(ks[5], CC, C), 'bck': jnp.zeros((C,), jnp.float32), 'Wcq': w(ks[6], C, C), 'bcq': jnp.zeros((C,), jnp.float32), 'Wcv': w(ks[7], CC, C), 'bcv': jnp.zeros((C,), jnp.float32), 'Wp': w(ks[8], C, C), 'bp': jnp.zeros((C,), jnp.float32)}
    _L0_xattn_all = _L0_xattn_setup()
    _L0_xattn_in = {k: v for k, v in _L0_xattn_all.items() if k in ('Wk', 'bk', 'Wq', 'bq', 'Wv', 'bv', 'Wck', 'bck', 'Wcq', 'bcq', 'Wcv', 'bcv', 'Wp', 'bp')}
    del _L0_xattn_all

    def _L0_ffn_setup():
        import jax, jax.numpy as jnp
        import numpy as np
        JITTER_EPS = 0.01
        NEG_INF = -jnp.inf

        def sparsemixer_eval(scores, jitter_eps):
            m1 = jnp.max(scores, axis=-1, keepdims=True)
            ind1 = jnp.argmax(scores, axis=-1)
            factor1 = jnp.maximum(jnp.abs(scores), m1)
            mask1 = jax.lax.stop_gradient((m1 - scores) / factor1 > 2.0 * jitter_eps)
            gates1 = jax.nn.softmax(jnp.where(mask1, NEG_INF, scores), axis=-1)
            mult1 = jnp.take_along_axis(gates1, ind1[:, None], axis=-1)[:, 0]
            E = scores.shape[-1]
            onehot1 = ind1[:, None] == jnp.arange(E)[None, :]
            masked_scores = jnp.where(onehot1, NEG_INF, scores)
            m2 = jnp.max(masked_scores, axis=-1, keepdims=True)
            ind2 = jnp.argmax(masked_scores, axis=-1)
            factor2 = jnp.maximum(jnp.abs(scores), m2)
            mask2 = jax.lax.stop_gradient((m2 - scores) / factor2 > 2.0 * jitter_eps)
            gates2 = jax.nn.softmax(jnp.where(mask2, NEG_INF, masked_scores), axis=-1)
            mult2 = jnp.take_along_axis(gates2, ind2[:, None], axis=-1)[:, 0]
            multiplier = jnp.stack([mult1, mult2], axis=-1)
            selected = jnp.stack([ind1, ind2], axis=-1)
            return (multiplier, selected)
        key = jax.random.key(seed)
        k0, k1, k2, k3, k4 = jax.random.split(key, 5)
        B, S, H, F, E = (2, 128, 128, 256, 8)
        scale = 0.02
        return {'hidden_states': jax.random.normal(k0, (B, S, H), dtype=jnp.float32), 'router_w': jax.random.normal(k1, (E, H), dtype=jnp.float32) * scale, 'w_gate': jax.random.normal(k2, (E, F, H), dtype=jnp.float32) * scale, 'w_up': jax.random.normal(k3, (E, F, H), dtype=jnp.float32) * scale, 'w_down': jax.random.normal(k4, (E, H, F), dtype=jnp.float32) * scale}
    _L0_ffn_all = _L0_ffn_setup()
    _L0_ffn_in = {k: v for k, v in _L0_ffn_all.items() if k in ('router_w', 'w_gate', 'w_up', 'w_down')}
    del _L0_ffn_all

    def _L1_xattn_setup():
        import jax, jax.numpy as jnp
        import numpy as np
        B, LQ, LK = (8, 256, 256)
        QD, KD, VD = (128, 64, 64)
        key = jax.random.key(seed)
        ks = jax.random.split(key, 9)
        s = 0.02
        return {'query': jax.random.normal(ks[0], (B, LQ, QD), jnp.float32), 'key': jax.random.normal(ks[1], (B, LK, KD), jnp.float32), 'value': jax.random.normal(ks[2], (B, LK, VD), jnp.float32), 'Wq': jax.random.normal(ks[3], (QD, QD), jnp.float32) * s, 'bq': jnp.zeros((QD,), jnp.float32), 'Wk': jax.random.normal(ks[4], (KD, QD), jnp.float32) * s, 'bk': jnp.zeros((QD,), jnp.float32), 'Wv': jax.random.normal(ks[5], (VD, QD), jnp.float32) * s, 'bv': jnp.zeros((QD,), jnp.float32)}
    _L1_xattn_all = _L1_xattn_setup()
    _L1_xattn_in = {k: v for k, v in _L1_xattn_all.items() if k in ('Wq', 'bq', 'Wk', 'bk', 'Wv', 'bv')}
    del _L1_xattn_all

    def _L1_ffn_setup():
        import jax, jax.numpy as jnp
        import numpy as np
        D_MODEL = 128
        N_EXPERTS = 8
        TOP_K = 2
        BOTTLENECK = 64
        B, S = (2, 512)
        ADAPTER_SCALE = 0.5

        def _moe_forward(x, w_gate, w_noise, Wd, bd, Wu, bu):
            b, s, d = x.shape
            xf = x.reshape(-1, d)
            T = xf.shape[0]
            clean_logits = xf @ w_gate
            logits = clean_logits
            k1 = min(TOP_K + 1, N_EXPERTS)
            top_logits, top_idx = jax.lax.top_k(logits, k1)
            top_k_logits = top_logits[:, :TOP_K]
            top_k_idx = top_idx[:, :TOP_K]
            top_k_gates = jax.nn.softmax(top_k_logits, axis=-1)
            rows = jnp.arange(T)[:, None]
            gates = jnp.zeros((T, N_EXPERTS), dtype=top_k_gates.dtype)
            gates = gates.at[rows, top_k_idx].set(top_k_gates)
            h = jax.nn.relu(jnp.einsum('td,edb->teb', xf, Wd) + bd[None, :, :])
            y = jnp.einsum('teb,ebd->ted', h, Wu) + bu[None, :, :]
            y = ADAPTER_SCALE * y
            out = jnp.einsum('te,ted->td', gates, y)
            return out.reshape(b, s, d)
        key = jax.random.key(seed)
        ks = jax.random.split(key, 8)
        sd = 0.02
        x = jax.random.normal(ks[0], (B, S, D_MODEL), dtype=jnp.float32)
        w_gate = jax.random.normal(ks[1], (D_MODEL, N_EXPERTS), dtype=jnp.float32) * sd
        w_noise = jax.random.normal(ks[2], (D_MODEL, N_EXPERTS), dtype=jnp.float32) * sd
        Wd = jax.random.normal(ks[3], (N_EXPERTS, D_MODEL, BOTTLENECK), dtype=jnp.float32) * sd
        bd = jnp.zeros((N_EXPERTS, BOTTLENECK), dtype=jnp.float32)
        Wu = jax.random.normal(ks[4], (N_EXPERTS, BOTTLENECK, D_MODEL), dtype=jnp.float32) * sd
        bu = jnp.zeros((N_EXPERTS, D_MODEL), dtype=jnp.float32)
        return {'x': x, 'w_gate': w_gate, 'w_noise': w_noise, 'Wd': Wd, 'bd': bd, 'Wu': Wu, 'bu': bu}
    _L1_ffn_all = _L1_ffn_setup()
    _L1_ffn_in = {k: v for k, v in _L1_ffn_all.items() if k in ('w_gate', 'w_noise', 'Wd', 'bd', 'Wu', 'bu')}
    del _L1_ffn_all

    def _L2_xattn_setup():
        import jax, jax.numpy as jnp
        import numpy as np
        H, D, C1, C2, S, M, B, W = (16, 32, 128, 64, 256, 64, 2, 4)

        def _ln(x, g, b):
            m = jnp.mean(x, -1, keepdims=True)
            v = jnp.var(x, -1, keepdims=True)
            return (x - m) * jax.lax.rsqrt(v + 1e-05) * g + b

        def _mha(x, y, wq, wk, wv, li1_w, li1_b, lnx_g, lnx_b, lny_g, lny_b, ln3_g, ln3_b, li2_w, li2_b, li3_w, li3_b, causal):
            xn = _ln(x, lnx_g, lnx_b)
            yn = _ln(y, lny_g, lny_b)
            q = jnp.einsum('bsc,hcd->bhsd', xn, wq)
            k = jnp.einsum('btc,hcd->bhtd', yn, wk)
            v = jnp.einsum('btc,hcd->bhtd', yn, wv)
            a = jax.nn.softmax(jnp.einsum('bhsd,bhtd->bhst', q, k) * D ** (-0.5), axis=-1)
            if causal:
                s, t = (a.shape[-2], a.shape[-1])
                mask = (jnp.arange(t)[None, :] > jnp.arange(s)[:, None]).astype(a.dtype)
                a = a * mask
            o = jnp.einsum('bhst,bhtd->bhsd', a, v)
            o = o.transpose(0, 2, 1, 3).reshape(x.shape[0], x.shape[1], H * D)
            x_out = x + o @ li1_w + li1_b
            h = jax.nn.gelu(_ln(x_out, ln3_g, ln3_b) @ li2_w + li2_b, approximate=False)
            return x_out + h @ li3_w + li3_b
        key = jax.random.key(seed)
        ks = iter(jax.random.split(key, 64))

        def w(shape, scale=0.02):
            return jax.random.normal(next(ks), shape, jnp.float32) * scale
        inp = {'xx': jax.random.normal(next(ks), (B, S, C1), jnp.float32), 'ee': jax.random.normal(next(ks), (B, M, C2), jnp.float32), 'ln1_g': jnp.ones(C1, jnp.float32), 'ln1_b': jnp.zeros(C1, jnp.float32), 'ln2_g': jnp.ones(C1, jnp.float32), 'ln2_b': jnp.zeros(C1, jnp.float32)}
        for pfx, cy in (('a1', C1), ('a2', C2)):
            inp[pfx + '_wq'] = w((H, C1, D))
            inp[pfx + '_wk'] = w((H, cy, D))
            inp[pfx + '_wv'] = w((H, cy, D))
            inp[pfx + '_li1_w'] = w((H * D, C1))
            inp[pfx + '_li1_b'] = jnp.zeros(C1, jnp.float32)
            inp[pfx + '_lnx_g'] = jnp.ones(C1, jnp.float32)
            inp[pfx + '_lnx_b'] = jnp.zeros(C1, jnp.float32)
            inp[pfx + '_lny_g'] = jnp.ones(cy, jnp.float32)
            inp[pfx + '_lny_b'] = jnp.zeros(cy, jnp.float32)
            inp[pfx + '_ln3_g'] = jnp.ones(C1, jnp.float32)
            inp[pfx + '_ln3_b'] = jnp.zeros(C1, jnp.float32)
            inp[pfx + '_li2_w'] = w((C1, C1 * W))
            inp[pfx + '_li2_b'] = jnp.zeros(C1 * W, jnp.float32)
            inp[pfx + '_li3_w'] = w((C1 * W, C1))
            inp[pfx + '_li3_b'] = jnp.zeros(C1, jnp.float32)
        inp['training'] = 0
        return inp
    _L2_xattn_all = _L2_xattn_setup()
    _L2_xattn_in = {k: v for k, v in _L2_xattn_all.items() if k in ('ln1_g', 'ln1_b', 'ln2_g', 'ln2_b', 'a1_wq', 'a1_wk', 'a1_wv', 'a1_li1_w', 'a1_li1_b', 'a1_lnx_g', 'a1_lnx_b', 'a1_lny_g', 'a1_lny_b', 'a1_ln3_g', 'a1_ln3_b', 'a1_li2_w', 'a1_li2_b', 'a1_li3_w', 'a1_li3_b', 'a2_wq', 'a2_wk', 'a2_wv', 'a2_li1_w', 'a2_li1_b', 'a2_lnx_g', 'a2_lnx_b', 'a2_lny_g', 'a2_lny_b', 'a2_ln3_g', 'a2_ln3_b', 'a2_li2_w', 'a2_li2_b', 'a2_li3_w', 'a2_li3_b')}
    del _L2_xattn_all

    def _L2_ffn_setup():
        import jax, jax.numpy as jnp
        import numpy as np
        B, S, D, F, E, TOP_K = (4, 256, 128, 512, 8, 2)
        LN_EPS = 1e-05
        key = jax.random.key(seed)
        ks = jax.random.split(key, 4)
        sc = lambda fan_in: 1.0 / np.sqrt(fan_in)
        return {'x': jax.random.normal(ks[0], (B, S, D), jnp.float32), 'W1': jax.random.normal(ks[1], (E, D, F), jnp.float32) * sc(D), 'b1': jnp.zeros((E, F), jnp.float32), 'W2': jax.random.normal(ks[2], (E, F, D), jnp.float32) * sc(F), 'b2': jnp.zeros((E, D), jnp.float32), 'Wr': jax.random.normal(ks[3], (D, E), jnp.float32) * sc(D), 'br': jnp.zeros((E,), jnp.float32), 'gamma': jnp.ones((D,), jnp.float32), 'beta': jnp.zeros((D,), jnp.float32)}
    _L2_ffn_all = _L2_ffn_setup()
    _L2_ffn_in = {k: v for k, v in _L2_ffn_all.items() if k in ('W1', 'b1', 'W2', 'b2', 'Wr', 'br', 'gamma', 'beta')}
    del _L2_ffn_all

    def _L3_xattn_setup():
        import jax, jax.numpy as jnp
        import numpy as np
        NUM_HEADS = 16
        HEAD_DIM = 64
        Q_DIM = 128
        KV_DIM = 64
        INNER = NUM_HEADS * HEAD_DIM
        key = jax.random.key(seed)
        ks = jax.random.split(key, 7)
        B, N, M = (32, 128, 256)
        q = jax.random.normal(ks[0], (B, N, Q_DIM), dtype=jnp.float32)
        kv = jax.random.normal(ks[1], (B, M, KV_DIM), dtype=jnp.float32)
        Wq = jax.random.normal(ks[2], (Q_DIM, INNER), dtype=jnp.float32) / np.sqrt(Q_DIM)
        Wk = jax.random.normal(ks[3], (KV_DIM, INNER), dtype=jnp.float32) / np.sqrt(KV_DIM)
        Wv = jax.random.normal(ks[4], (KV_DIM, INNER), dtype=jnp.float32) / np.sqrt(KV_DIM)
        Wo = jax.random.normal(ks[5], (INNER, Q_DIM), dtype=jnp.float32) / np.sqrt(INNER)
        bo = jax.random.normal(ks[6], (Q_DIM,), dtype=jnp.float32) * 0.01
        return {'q': q, 'kv': kv, 'Wq': Wq, 'Wk': Wk, 'Wv': Wv, 'Wo': Wo, 'bo': bo}
    _L3_xattn_all = _L3_xattn_setup()
    _L3_xattn_in = {k: v for k, v in _L3_xattn_all.items() if k in ('Wq', 'Wk', 'Wv', 'Wo', 'bo')}
    del _L3_xattn_all

    def _L3_ffn_setup():
        import jax, jax.numpy as jnp
        import numpy as np
        NUM_EXPERTS = 8
        EXPERT_CAPACITY = 2.0
        DIM = 128
        HIDDEN_DIM = 512
        key = jax.random.key(seed)
        k_x, k_g, k_w1, k_w2 = jax.random.split(key, 4)
        n, t, d, f, e = (8, 128, DIM, HIDDEN_DIM, NUM_EXPERTS)
        x = jax.random.normal(k_x, (n, t, d), dtype=jnp.float32)
        gate_w = jax.random.normal(k_g, (e, d), dtype=jnp.float32) * 0.02
        w1 = jax.random.normal(k_w1, (e, d, f), dtype=jnp.float32) * 0.02
        w2 = jax.random.normal(k_w2, (e, f, d), dtype=jnp.float32) * 0.02
        return {'x': x, 'gate_w': gate_w, 'w1': w1, 'w2': w2}
    _L3_ffn_all = _L3_ffn_setup()
    _L3_ffn_in = {k: v for k, v in _L3_ffn_all.items() if k in ('gate_w', 'w1', 'w2')}
    del _L3_ffn_all
    return {'x': x, 'ctx_512': ctx_512, 'L0_xattn_Wk': _L0_xattn_in['Wk'], 'L0_xattn_bk': _L0_xattn_in['bk'], 'L0_xattn_Wq': _L0_xattn_in['Wq'], 'L0_xattn_bq': _L0_xattn_in['bq'], 'L0_xattn_Wv': _L0_xattn_in['Wv'], 'L0_xattn_bv': _L0_xattn_in['bv'], 'L0_xattn_Wck': _L0_xattn_in['Wck'], 'L0_xattn_bck': _L0_xattn_in['bck'], 'L0_xattn_Wcq': _L0_xattn_in['Wcq'], 'L0_xattn_bcq': _L0_xattn_in['bcq'], 'L0_xattn_Wcv': _L0_xattn_in['Wcv'], 'L0_xattn_bcv': _L0_xattn_in['bcv'], 'L0_xattn_Wp': _L0_xattn_in['Wp'], 'L0_xattn_bp': _L0_xattn_in['bp'], 'L0_ffn_router_w': _L0_ffn_in['router_w'], 'L0_ffn_w_gate': _L0_ffn_in['w_gate'], 'L0_ffn_w_up': _L0_ffn_in['w_up'], 'L0_ffn_w_down': _L0_ffn_in['w_down'], 'L1_xattn_Wq': _L1_xattn_in['Wq'], 'L1_xattn_bq': _L1_xattn_in['bq'], 'L1_xattn_Wk': _L1_xattn_in['Wk'], 'L1_xattn_bk': _L1_xattn_in['bk'], 'L1_xattn_Wv': _L1_xattn_in['Wv'], 'L1_xattn_bv': _L1_xattn_in['bv'], 'L1_ffn_w_gate': _L1_ffn_in['w_gate'], 'L1_ffn_w_noise': _L1_ffn_in['w_noise'], 'L1_ffn_Wd': _L1_ffn_in['Wd'], 'L1_ffn_bd': _L1_ffn_in['bd'], 'L1_ffn_Wu': _L1_ffn_in['Wu'], 'L1_ffn_bu': _L1_ffn_in['bu'], 'L2_xattn_ln1_g': _L2_xattn_in['ln1_g'], 'L2_xattn_ln1_b': _L2_xattn_in['ln1_b'], 'L2_xattn_ln2_g': _L2_xattn_in['ln2_g'], 'L2_xattn_ln2_b': _L2_xattn_in['ln2_b'], 'L2_xattn_a1_wq': _L2_xattn_in['a1_wq'], 'L2_xattn_a1_wk': _L2_xattn_in['a1_wk'], 'L2_xattn_a1_wv': _L2_xattn_in['a1_wv'], 'L2_xattn_a1_li1_w': _L2_xattn_in['a1_li1_w'], 'L2_xattn_a1_li1_b': _L2_xattn_in['a1_li1_b'], 'L2_xattn_a1_lnx_g': _L2_xattn_in['a1_lnx_g'], 'L2_xattn_a1_lnx_b': _L2_xattn_in['a1_lnx_b'], 'L2_xattn_a1_lny_g': _L2_xattn_in['a1_lny_g'], 'L2_xattn_a1_lny_b': _L2_xattn_in['a1_lny_b'], 'L2_xattn_a1_ln3_g': _L2_xattn_in['a1_ln3_g'], 'L2_xattn_a1_ln3_b': _L2_xattn_in['a1_ln3_b'], 'L2_xattn_a1_li2_w': _L2_xattn_in['a1_li2_w'], 'L2_xattn_a1_li2_b': _L2_xattn_in['a1_li2_b'], 'L2_xattn_a1_li3_w': _L2_xattn_in['a1_li3_w'], 'L2_xattn_a1_li3_b': _L2_xattn_in['a1_li3_b'], 'L2_xattn_a2_wq': _L2_xattn_in['a2_wq'], 'L2_xattn_a2_wk': _L2_xattn_in['a2_wk'], 'L2_xattn_a2_wv': _L2_xattn_in['a2_wv'], 'L2_xattn_a2_li1_w': _L2_xattn_in['a2_li1_w'], 'L2_xattn_a2_li1_b': _L2_xattn_in['a2_li1_b'], 'L2_xattn_a2_lnx_g': _L2_xattn_in['a2_lnx_g'], 'L2_xattn_a2_lnx_b': _L2_xattn_in['a2_lnx_b'], 'L2_xattn_a2_lny_g': _L2_xattn_in['a2_lny_g'], 'L2_xattn_a2_lny_b': _L2_xattn_in['a2_lny_b'], 'L2_xattn_a2_ln3_g': _L2_xattn_in['a2_ln3_g'], 'L2_xattn_a2_ln3_b': _L2_xattn_in['a2_ln3_b'], 'L2_xattn_a2_li2_w': _L2_xattn_in['a2_li2_w'], 'L2_xattn_a2_li2_b': _L2_xattn_in['a2_li2_b'], 'L2_xattn_a2_li3_w': _L2_xattn_in['a2_li3_w'], 'L2_xattn_a2_li3_b': _L2_xattn_in['a2_li3_b'], 'L2_ffn_W1': _L2_ffn_in['W1'], 'L2_ffn_b1': _L2_ffn_in['b1'], 'L2_ffn_W2': _L2_ffn_in['W2'], 'L2_ffn_b2': _L2_ffn_in['b2'], 'L2_ffn_Wr': _L2_ffn_in['Wr'], 'L2_ffn_br': _L2_ffn_in['br'], 'L2_ffn_gamma': _L2_ffn_in['gamma'], 'L2_ffn_beta': _L2_ffn_in['beta'], 'L3_xattn_Wq': _L3_xattn_in['Wq'], 'L3_xattn_Wk': _L3_xattn_in['Wk'], 'L3_xattn_Wv': _L3_xattn_in['Wv'], 'L3_xattn_Wo': _L3_xattn_in['Wo'], 'L3_xattn_bo': _L3_xattn_in['bo'], 'L3_ffn_gate_w': _L3_ffn_in['gate_w'], 'L3_ffn_w1': _L3_ffn_in['w1'], 'L3_ffn_w2': _L3_ffn_in['w2']}

def reference(x, ctx_512, L0_xattn_Wk, L0_xattn_bk, L0_xattn_Wq, L0_xattn_bq, L0_xattn_Wv, L0_xattn_bv, L0_xattn_Wck, L0_xattn_bck, L0_xattn_Wcq, L0_xattn_bcq, L0_xattn_Wcv, L0_xattn_bcv, L0_xattn_Wp, L0_xattn_bp, L0_ffn_router_w, L0_ffn_w_gate, L0_ffn_w_up, L0_ffn_w_down, L1_xattn_Wq, L1_xattn_bq, L1_xattn_Wk, L1_xattn_bk, L1_xattn_Wv, L1_xattn_bv, L1_ffn_w_gate, L1_ffn_w_noise, L1_ffn_Wd, L1_ffn_bd, L1_ffn_Wu, L1_ffn_bu, L2_xattn_ln1_g, L2_xattn_ln1_b, L2_xattn_ln2_g, L2_xattn_ln2_b, L2_xattn_a1_wq, L2_xattn_a1_wk, L2_xattn_a1_wv, L2_xattn_a1_li1_w, L2_xattn_a1_li1_b, L2_xattn_a1_lnx_g, L2_xattn_a1_lnx_b, L2_xattn_a1_lny_g, L2_xattn_a1_lny_b, L2_xattn_a1_ln3_g, L2_xattn_a1_ln3_b, L2_xattn_a1_li2_w, L2_xattn_a1_li2_b, L2_xattn_a1_li3_w, L2_xattn_a1_li3_b, L2_xattn_a2_wq, L2_xattn_a2_wk, L2_xattn_a2_wv, L2_xattn_a2_li1_w, L2_xattn_a2_li1_b, L2_xattn_a2_lnx_g, L2_xattn_a2_lnx_b, L2_xattn_a2_lny_g, L2_xattn_a2_lny_b, L2_xattn_a2_ln3_g, L2_xattn_a2_ln3_b, L2_xattn_a2_li2_w, L2_xattn_a2_li2_b, L2_xattn_a2_li3_w, L2_xattn_a2_li3_b, L2_ffn_W1, L2_ffn_b1, L2_ffn_W2, L2_ffn_b2, L2_ffn_Wr, L2_ffn_br, L2_ffn_gamma, L2_ffn_beta, L3_xattn_Wq, L3_xattn_Wk, L3_xattn_Wv, L3_xattn_Wo, L3_xattn_bo, L3_ffn_gate_w, L3_ffn_w1, L3_ffn_w2):
    import jax
    import jax.numpy as jnp

    def _L0_xattn_ref(x, cross_input, Wk, bk, Wq, bq, Wv, bv, Wck, bck, Wcq, bcq, Wcv, bcv, Wp, bp):
        import jax, jax.numpy as jnp
        import numpy as np
        B, T, TC, C, CC, H = (2, 256, 64, 128, 64, 16)
        D = C // H

        def _heads(t):
            b, l, _ = t.shape
            return t.reshape(b, l, H, D).transpose(0, 2, 1, 3)
        scale = np.float32(1.0 / np.sqrt(D))
        q = _heads(x @ Wq + bq)
        k = _heads(x @ Wk + bk)
        v = _heads(x @ Wv + bv)
        att = jnp.einsum('bhqd,bhkd->bhqk', q, k) * scale
        causal = jnp.tril(jnp.ones((T, T), bool))
        att = jnp.where(causal[None, None], att, -jnp.inf)
        y = jnp.einsum('bhqk,bhkd->bhqd', jax.nn.softmax(att, axis=-1), v)
        qc = _heads(x @ Wcq + bcq)
        kc = _heads(cross_input @ Wck + bck)
        vc = _heads(cross_input @ Wcv + bcv)
        attc = jnp.einsum('bhqd,bhkd->bhqk', qc, kc) * scale
        y = y + jnp.einsum('bhqk,bhkd->bhqd', jax.nn.softmax(attc, axis=-1), vc)
        y = y.transpose(0, 2, 1, 3).reshape(x.shape[0], T, C)
        return y @ Wp + bp

    def _L0_ffn_ref(hidden_states, router_w, w_gate, w_up, w_down):
        import jax, jax.numpy as jnp
        import numpy as np
        JITTER_EPS = 0.01
        NEG_INF = -jnp.inf

        def sparsemixer_eval(scores, jitter_eps):
            m1 = jnp.max(scores, axis=-1, keepdims=True)
            ind1 = jnp.argmax(scores, axis=-1)
            factor1 = jnp.maximum(jnp.abs(scores), m1)
            mask1 = jax.lax.stop_gradient((m1 - scores) / factor1 > 2.0 * jitter_eps)
            gates1 = jax.nn.softmax(jnp.where(mask1, NEG_INF, scores), axis=-1)
            mult1 = jnp.take_along_axis(gates1, ind1[:, None], axis=-1)[:, 0]
            E = scores.shape[-1]
            onehot1 = ind1[:, None] == jnp.arange(E)[None, :]
            masked_scores = jnp.where(onehot1, NEG_INF, scores)
            m2 = jnp.max(masked_scores, axis=-1, keepdims=True)
            ind2 = jnp.argmax(masked_scores, axis=-1)
            factor2 = jnp.maximum(jnp.abs(scores), m2)
            mask2 = jax.lax.stop_gradient((m2 - scores) / factor2 > 2.0 * jitter_eps)
            gates2 = jax.nn.softmax(jnp.where(mask2, NEG_INF, masked_scores), axis=-1)
            mult2 = jnp.take_along_axis(gates2, ind2[:, None], axis=-1)[:, 0]
            multiplier = jnp.stack([mult1, mult2], axis=-1)
            selected = jnp.stack([ind1, ind2], axis=-1)
            return (multiplier, selected)
        B, S, H = hidden_states.shape
        E = router_w.shape[0]
        x = hidden_states.reshape(-1, H)
        T = x.shape[0]
        logits = x @ router_w.T
        routing_weights, selected = sparsemixer_eval(logits, JITTER_EPS)
        tok = jnp.arange(T)
        dense_w = jnp.zeros((T, E), dtype=x.dtype)
        dense_w = dense_w.at[tok, selected[:, 0]].add(routing_weights[:, 0])
        dense_w = dense_w.at[tok, selected[:, 1]].add(routing_weights[:, 1])
        out = jnp.zeros_like(x)
        for e in range(E):
            h = jax.nn.silu(x @ w_gate[e].T) * (x @ w_up[e].T)
            out = out + dense_w[:, e:e + 1] * (h @ w_down[e].T)
        return out.reshape(B, S, H)

    def _L1_xattn_ref(query, key, value, Wq, bq, Wk, bk, Wv, bv):
        import jax, jax.numpy as jnp
        import numpy as np
        B, LQ, LK = (8, 256, 256)
        QD, KD, VD = (128, 64, 64)
        q = jnp.einsum('bld,de->ble', query, Wq) + bq
        k = jnp.einsum('bld,de->ble', key, Wk) + bk
        v = jnp.einsum('bld,de->ble', value, Wv) + bv
        scores = jnp.einsum('bqe,bke->bqk', q, k)
        attn = jax.nn.softmax(scores, axis=-1)
        out = jnp.einsum('bqk,bke->bqe', attn, v)
        return out

    def _L1_ffn_ref(x, w_gate, w_noise, Wd, bd, Wu, bu):
        import jax, jax.numpy as jnp
        import numpy as np
        D_MODEL = 128
        N_EXPERTS = 8
        TOP_K = 2
        BOTTLENECK = 64
        B, S = (2, 512)
        ADAPTER_SCALE = 0.5

        def _moe_forward(x, w_gate, w_noise, Wd, bd, Wu, bu):
            b, s, d = x.shape
            xf = x.reshape(-1, d)
            T = xf.shape[0]
            clean_logits = xf @ w_gate
            logits = clean_logits
            k1 = min(TOP_K + 1, N_EXPERTS)
            top_logits, top_idx = jax.lax.top_k(logits, k1)
            top_k_logits = top_logits[:, :TOP_K]
            top_k_idx = top_idx[:, :TOP_K]
            top_k_gates = jax.nn.softmax(top_k_logits, axis=-1)
            rows = jnp.arange(T)[:, None]
            gates = jnp.zeros((T, N_EXPERTS), dtype=top_k_gates.dtype)
            gates = gates.at[rows, top_k_idx].set(top_k_gates)
            h = jax.nn.relu(jnp.einsum('td,edb->teb', xf, Wd) + bd[None, :, :])
            y = jnp.einsum('teb,ebd->ted', h, Wu) + bu[None, :, :]
            y = ADAPTER_SCALE * y
            out = jnp.einsum('te,ted->td', gates, y)
            return out.reshape(b, s, d)
        return _moe_forward(x, w_gate, w_noise, Wd, bd, Wu, bu)

    def _L2_xattn_ref(xx, ee, ln1_g, ln1_b, ln2_g, ln2_b, a1_wq, a1_wk, a1_wv, a1_li1_w, a1_li1_b, a1_lnx_g, a1_lnx_b, a1_lny_g, a1_lny_b, a1_ln3_g, a1_ln3_b, a1_li2_w, a1_li2_b, a1_li3_w, a1_li3_b, a2_wq, a2_wk, a2_wv, a2_li1_w, a2_li1_b, a2_lnx_g, a2_lnx_b, a2_lny_g, a2_lny_b, a2_ln3_g, a2_ln3_b, a2_li2_w, a2_li2_b, a2_li3_w, a2_li3_b, training):
        import jax, jax.numpy as jnp
        import numpy as np
        H, D, C1, C2, S, M, B, W = (16, 32, 128, 64, 256, 64, 2, 4)

        def _ln(x, g, b):
            m = jnp.mean(x, -1, keepdims=True)
            v = jnp.var(x, -1, keepdims=True)
            return (x - m) * jax.lax.rsqrt(v + 1e-05) * g + b

        def _mha(x, y, wq, wk, wv, li1_w, li1_b, lnx_g, lnx_b, lny_g, lny_b, ln3_g, ln3_b, li2_w, li2_b, li3_w, li3_b, causal):
            xn = _ln(x, lnx_g, lnx_b)
            yn = _ln(y, lny_g, lny_b)
            q = jnp.einsum('bsc,hcd->bhsd', xn, wq)
            k = jnp.einsum('btc,hcd->bhtd', yn, wk)
            v = jnp.einsum('btc,hcd->bhtd', yn, wv)
            a = jax.nn.softmax(jnp.einsum('bhsd,bhtd->bhst', q, k) * D ** (-0.5), axis=-1)
            if causal:
                s, t = (a.shape[-2], a.shape[-1])
                mask = (jnp.arange(t)[None, :] > jnp.arange(s)[:, None]).astype(a.dtype)
                a = a * mask
            o = jnp.einsum('bhst,bhtd->bhsd', a, v)
            o = o.transpose(0, 2, 1, 3).reshape(x.shape[0], x.shape[1], H * D)
            x_out = x + o @ li1_w + li1_b
            h = jax.nn.gelu(_ln(x_out, ln3_g, ln3_b) @ li2_w + li2_b, approximate=False)
            return x_out + h @ li3_w + li3_b
        x = _ln(xx, ln1_g, ln1_b)
        x = x + _mha(x, x, a1_wq, a1_wk, a1_wv, a1_li1_w, a1_li1_b, a1_lnx_g, a1_lnx_b, a1_lny_g, a1_lny_b, a1_ln3_g, a1_ln3_b, a1_li2_w, a1_li2_b, a1_li3_w, a1_li3_b, causal=True)
        x = _ln(x, ln2_g, ln2_b)
        return x + _mha(x, ee, a2_wq, a2_wk, a2_wv, a2_li1_w, a2_li1_b, a2_lnx_g, a2_lnx_b, a2_lny_g, a2_lny_b, a2_ln3_g, a2_ln3_b, a2_li2_w, a2_li2_b, a2_li3_w, a2_li3_b, causal=False)

    def _L2_ffn_ref(x, W1, b1, W2, b2, Wr, br, gamma, beta):
        import jax, jax.numpy as jnp
        import numpy as np
        B, S, D, F, E, TOP_K = (4, 256, 128, 512, 8, 2)
        LN_EPS = 1e-05
        b, s, d = x.shape
        e = Wr.shape[1]
        rw = jax.nn.softmax(x.mean(axis=1) @ Wr + br, axis=-1)
        x_flat = x.reshape(-1, d)
        rw_tok = jnp.repeat(rw, s, axis=0)
        tk_w, tk_i = jax.lax.top_k(rw_tok, TOP_K)
        tk_w = jax.nn.softmax(tk_w, axis=-1)
        h = jax.nn.gelu(jnp.einsum('nd,edf->enf', x_flat, W1) + b1[:, None, :], approximate=False)
        expert_out = jnp.einsum('enf,efd->end', h, W2) + b2[:, None, :]
        onehot = jax.nn.one_hot(tk_i, e, dtype=x.dtype)
        cw = jnp.einsum('nk,nke->ne', tk_w, onehot)
        out = jnp.einsum('ne,end->nd', cw, expert_out).reshape(b, s, d)
        y = out + x
        mu = y.mean(axis=-1, keepdims=True)
        var = y.var(axis=-1, keepdims=True)
        return (y - mu) / jnp.sqrt(var + LN_EPS) * gamma + beta

    def _L3_xattn_ref(q, kv, Wq, Wk, Wv, Wo, bo):
        import jax, jax.numpy as jnp
        import numpy as np
        NUM_HEADS = 16
        HEAD_DIM = 64
        Q_DIM = 128
        KV_DIM = 64
        INNER = NUM_HEADS * HEAD_DIM
        B, N, _ = q.shape
        M = kv.shape[1]
        scale = HEAD_DIM ** (-0.5)
        qh = (q @ Wq).reshape(B, N, NUM_HEADS, HEAD_DIM).transpose(0, 2, 1, 3)
        kh = (kv @ Wk).reshape(B, M, NUM_HEADS, HEAD_DIM).transpose(0, 2, 1, 3)
        vh = (kv @ Wv).reshape(B, M, NUM_HEADS, HEAD_DIM).transpose(0, 2, 1, 3)
        scores = jnp.einsum('bhnd,bhmd->bhnm', qh, kh) * scale
        attn = jax.nn.softmax(scores, axis=-1)
        out = jnp.einsum('bhnm,bhmd->bhnd', attn, vh)
        out = out.transpose(0, 2, 1, 3).reshape(B, N, INNER)
        return out @ Wo + bo

    def _L3_ffn_ref(x, gate_w, w1, w2):
        import jax, jax.numpy as jnp
        import numpy as np
        NUM_EXPERTS = 8
        EXPERT_CAPACITY = 2.0
        DIM = 128
        HIDDEN_DIM = 512
        n, t, d = x.shape
        e = gate_w.shape[0]
        k = int(EXPERT_CAPACITY * t / e)
        scores = jnp.einsum('ntd,ed->nte', x, gate_w)
        probs = jax.nn.softmax(scores, axis=-1)
        g, m = jax.lax.top_k(probs.transpose(0, 2, 1), k)
        batch_idx = jnp.arange(n)[:, None, None]
        xin = x[batch_idx, m]
        h = jnp.einsum('nekd,edf->nekf', xin, w1)
        h = jax.nn.gelu(h, approximate=False)
        h = jnp.einsum('nekf,efd->nekd', h, w2)
        out_tok = g[..., None] * h
        out = jnp.zeros((n, t, d), dtype=x.dtype).at[batch_idx, m].add(out_tok)
        return out
    x = x + _L0_xattn_ref(_layernorm(x, axis=-1), ctx_512, L0_xattn_Wk, L0_xattn_bk, L0_xattn_Wq, L0_xattn_bq, L0_xattn_Wv, L0_xattn_bv, L0_xattn_Wck, L0_xattn_bck, L0_xattn_Wcq, L0_xattn_bcq, L0_xattn_Wcv, L0_xattn_bcv, L0_xattn_Wp, L0_xattn_bp)
    x = x + _L0_ffn_ref(_layernorm(x, axis=-1), L0_ffn_router_w, L0_ffn_w_gate, L0_ffn_w_up, L0_ffn_w_down)
    x = x + _L1_xattn_ref(_layernorm(x, axis=-1), ctx_512, ctx_512, L1_xattn_Wq, L1_xattn_bq, L1_xattn_Wk, L1_xattn_bk, L1_xattn_Wv, L1_xattn_bv)
    x = x + _L1_ffn_ref(_layernorm(x, axis=-1), L1_ffn_w_gate, L1_ffn_w_noise, L1_ffn_Wd, L1_ffn_bd, L1_ffn_Wu, L1_ffn_bu)
    x = x + _L2_xattn_ref(_layernorm(x, axis=-1), ctx_512, L2_xattn_ln1_g, L2_xattn_ln1_b, L2_xattn_ln2_g, L2_xattn_ln2_b, L2_xattn_a1_wq, L2_xattn_a1_wk, L2_xattn_a1_wv, L2_xattn_a1_li1_w, L2_xattn_a1_li1_b, L2_xattn_a1_lnx_g, L2_xattn_a1_lnx_b, L2_xattn_a1_lny_g, L2_xattn_a1_lny_b, L2_xattn_a1_ln3_g, L2_xattn_a1_ln3_b, L2_xattn_a1_li2_w, L2_xattn_a1_li2_b, L2_xattn_a1_li3_w, L2_xattn_a1_li3_b, L2_xattn_a2_wq, L2_xattn_a2_wk, L2_xattn_a2_wv, L2_xattn_a2_li1_w, L2_xattn_a2_li1_b, L2_xattn_a2_lnx_g, L2_xattn_a2_lnx_b, L2_xattn_a2_lny_g, L2_xattn_a2_lny_b, L2_xattn_a2_ln3_g, L2_xattn_a2_ln3_b, L2_xattn_a2_li2_w, L2_xattn_a2_li2_b, L2_xattn_a2_li3_w, L2_xattn_a2_li3_b, 0)
    x = x + _L2_ffn_ref(_layernorm(x, axis=-1), L2_ffn_W1, L2_ffn_b1, L2_ffn_W2, L2_ffn_b2, L2_ffn_Wr, L2_ffn_br, L2_ffn_gamma, L2_ffn_beta)
    x = x + _L3_xattn_ref(_layernorm(x, axis=-1), ctx_512, L3_xattn_Wq, L3_xattn_Wk, L3_xattn_Wv, L3_xattn_Wo, L3_xattn_bo)
    x = x + _L3_ffn_ref(_layernorm(x, axis=-1), L3_ffn_gate_w, L3_ffn_w1, L3_ffn_w2)
    return x

_drawn_inputs = setup_inputs


def setup_inputs(seed=0):
    import zlib

    import numpy as np

    out = dict(_drawn_inputs(seed))
    spreads = {'L0_xattn_bk': (0.0, 2.0),
     'L0_xattn_bq': (0.0, 0.447),
     'L0_xattn_bv': (0.0, 0.1),
     'L0_xattn_bck': (0.0, 2.0),
     'L0_xattn_bcq': (0.0, 0.395),
     'L0_xattn_bcv': (0.0, 0.1),
     'L0_xattn_bp': (0.0, 0.1),
     'L1_xattn_bq': (0.0, 0.8),
     'L1_xattn_bk': (0.0, 2.0),
     'L1_xattn_bv': (0.0, 0.1),
     'L1_ffn_bd': (0.0, 0.8),
     'L1_ffn_bu': (0.0, 0.268),
     'L2_xattn_ln1_g': (1.0, 0.2),
     'L2_xattn_ln1_b': (0.0, 0.1),
     'L2_xattn_ln2_g': (1.0, 0.2),
     'L2_xattn_ln2_b': (0.0, 0.1),
     'L2_xattn_a1_li1_b': (0.0, 0.311),
     'L2_xattn_a1_lnx_g': (1.0, 0.6),
     'L2_xattn_a1_lnx_b': (0.0, 0.8),
     'L2_xattn_a1_lny_g': (1.0, 0.6),
     'L2_xattn_a1_lny_b': (0.0, 0.8),
     'L2_xattn_a1_ln3_g': (1.0, 0.6),
     'L2_xattn_a1_ln3_b': (0.0, 0.8),
     'L2_xattn_a1_li2_b': (0.0, 0.8),
     'L2_xattn_a1_li3_b': (0.0, 0.369),
     'L2_xattn_a2_li1_b': (0.0, 0.1),
     'L2_xattn_a2_lnx_g': (1.0, 0.6),
     'L2_xattn_a2_lnx_b': (0.0, 0.8),
     'L2_xattn_a2_lny_g': (1.0, 0.6),
     'L2_xattn_a2_lny_b': (0.0, 0.8),
     'L2_xattn_a2_ln3_g': (1.0, 0.6),
     'L2_xattn_a2_ln3_b': (0.0, 0.8),
     'L2_xattn_a2_li2_b': (0.0, 0.8),
     'L2_xattn_a2_li3_b': (0.0, 0.1),
     'L2_ffn_b1': (0.0, 0.797),
     'L2_ffn_b2': (0.0, 0.488),
     'L2_ffn_br': (0.0, 0.8),
     'L2_ffn_gamma': (1.0, 0.2),
     'L2_ffn_beta': (0.0, 0.342)}
    factors = {'L0_ffn_router_w': 6.262,
     'L0_ffn_w_gate': 5.63,
     'L0_ffn_w_up': 5.586,
     'L0_ffn_w_down': 5.6,
     'L1_xattn_Wq': 4.809,
     'L1_xattn_Wk': 4.934,
     'L1_ffn_Wd': 8.0,
     'L1_ffn_Wu': 6.822,
     'L2_xattn_a1_wq': 8.0,
     'L2_xattn_a1_wk': 8.0,
     'L2_xattn_a1_wv': 5.594,
     'L2_xattn_a1_li1_w': 5.568,
     'L2_xattn_a1_li2_w': 3.308,
     'L2_xattn_a1_li3_w': 2.898,
     'L2_xattn_a2_wq': 8.0,
     'L2_xattn_a2_wk': 8.0,
     'L2_xattn_a2_wv': 4.402,
     'L2_xattn_a2_li1_w': 4.542,
     'L2_xattn_a2_li2_w': 3.271,
     'L2_xattn_a2_li3_w': 3.035,
     'L3_xattn_bo': 8.0,
     'L3_ffn_gate_w': 8.0,
     'L3_ffn_w1': 8.0,
     'L3_ffn_w2': 8.0}
    for name, (base, spread) in spreads.items():
        noise = np.random.default_rng([zlib.crc32(name.encode()), seed]).standard_normal(out[name].shape)
        drawn = base * np.exp(spread * noise) if base else spread * noise
        out[name] = jnp.asarray(drawn.astype(out[name].dtype))
    for name, factor in factors.items():
        out[name] = (out[name] * factor).astype(out[name].dtype)
    return out
```

```python
from contextlib import ExitStack, contextmanager

import concourse.bass as bass
from concourse import mybir

F32 = mybir.dt.float32
ALU = mybir.AluOpType
ACT = mybir.ActivationFunctionType
AX = mybir.AxisListType

P = 128
B, T, C = 4, 256, 128
TC, CC = 1601, 64
KA = CC + 1
NT = B * T // P
QT = T // P
H = 16
E = 8
CT = -(-TC // P)
LAST = TC - (CT - 1) * P
EPS = 1e-5
LOWEST = -3.0e38


@contextmanager
def stage(nc, name, *signals):
    with ExitStack() as es:
        sems = [es.enter_context(nc.semaphore(f"{name}_{s}")) for s in signals]
        with nc.Block() as block:
            yield (block, *sems)
        for s in sems:
            nc.sync.sem_clear(s)
        nc.all_engine_barrier(sem_only=True)


class Link:

    def __init__(self, eng, sem, base=0):
        self.eng, self.sem, self.base, self.n = eng, sem, base, 0

    def __call__(self, ins):
        ins.then_inc(self.sem, 1)
        self.n += 1
        self.eng.wait_ge(self.sem, self.base + self.n)


class Space:

    def __init__(self, nc, name):
        self.nc, self.name, self.es = nc, name, ExitStack()

    def __enter__(self):
        return self

    def __exit__(self, *a):
        self.es.close()

    def __call__(self, name, shape, dt=F32):
        return self.es.enter_context(self.nc.sbuf_tensor(f"{self.name}_{name}", shape, dt))


def bcast(ap, shape):
    return ap.to_broadcast(shape)


def rows(dram, n=P):
    return dram.rearrange("(a n) -> a n", a=1).to_broadcast([n, dram.shape[0]])


def layernorm(nc, name, src, dst, gain=None, shift=None, tiles=NT, width=C, last=P):
    with Space(nc, name) as sb:
        stats = sb("stats", [P, tiles, 6])
        mv = sb("mv", [P, tiles, 2])
        std = sb("std", [P, tiles])
        rstd = sb("rstd", [P, tiles])
        gb = sb("gb", [P, 2, width]) if gain is not None else None
        parts = [(slice(0, tiles), P)] if last == P else [(slice(0, tiles - 1), P), (slice(tiles - 1, tiles), last)]
        with stage(nc, name, "moments", "std", "step", "affine_in") as (block, moments, std_done, step, affine_in):
            @block.sync
            def _(sp):
                if gain is not None:
                    sp.dma_start(gb[:, 0, :], rows(gain)).then_inc(affine_in, 16)
                    sp.dma_start(gb[:, 1, :], rows(shift)).then_inc(affine_in, 16)

            @block.vector
            def _(dve):
                link = Link(dve, step)
                for n in range(tiles):
                    r = P if n < tiles - 1 else last
                    link(nc.vector.bn_stats(stats[0:r, n, :], src[0:r, n, :]))
                    link(nc.vector.bn_aggr(mv[0:r, n, :], stats[0:r, n, :]))
                for s, r in parts:
                    nc.vector.tensor_scalar(rstd[0:r, s], mv[0:r, s, 1], EPS, None, ALU.add).then_inc(moments, 1)
                dve.wait_ge(std_done, len(parts))
                for s, r in parts:
                    link(nc.vector.reciprocal(rstd[0:r, s], std[0:r, s]))
                for n in range(tiles):
                    r = P if n < tiles - 1 else last
                    link(nc.vector.tensor_scalar(dst[0:r, n, :], src[0:r, n, :], mv[0:r, n, 0:1],
                                                 rstd[0:r, n:n + 1], ALU.subtract, ALU.mult))
                if gain is not None:
                    dve.wait_ge(affine_in, 32)
                    link(nc.vector.tensor_tensor(dst[:], dst[:], gb[:, 0:1, :].to_broadcast([P, tiles, width]), ALU.mult))
                    link(nc.vector.tensor_tensor(dst[:], dst[:], gb[:, 1:2, :].to_broadcast([P, tiles, width]), ALU.add))

            @block.scalar
            def _(act):
                act.wait_ge(moments, len(parts))
                for s, r in parts:
                    nc.scalar.activation(std[0:r, s], rstd[0:r, s], ACT.Sqrt).then_inc(std_done, 1)


def transpose_tokens(nc, name, g, src, outs, width=C):
    kc = width // P
    with Space(nc, name) as sb:
        cols = sb("cols", [P, 2 * len(outs)])
        with stage(nc, name, "turned", "kept", "cols_in") as (block, turned, kept, cols_in):
            n_cols = sum(gain is not None for _, gain, _ in outs)

            @block.sync
            def _(sp):
                for k, (_, gain, shift) in enumerate(outs):
                    if gain is not None:
                        sp.dma_start(cols[:, 2 * k:2 * k + 1], gain.rearrange("(n a) -> n a", a=1)).then_inc(cols_in, 16)
                        sp.dma_start(cols[:, 2 * k + 1:2 * k + 2], shift.rearrange("(n a) -> n a", a=1)).then_inc(cols_in, 16)

            @block.tensor
            def _(pe):
                for i in range(kc * 2):
                    c, half = i // 2, i % 2
                    if i >= 2:
                        pe.wait_ge(kept, i - 1)
                    for n in range(4):
                        mm = nc.tensor.transpose(g.bank[i % 2][:, n * P:(n + 1) * P],
                                                 src[:, half * 4 + n, c * P:(c + 1) * P], g.ident[:])
                    mm.then_inc(turned, 1)

            @block.vector
            def _(dve):
                if n_cols:
                    dve.wait_ge(cols_in, 32 * n_cols)
                for i in range(kc * 2):
                    c, half = i // 2, i % 2
                    dve.wait_ge(turned, i + 1)
                    for k, (dst, gain, _) in enumerate(outs):
                        o = dst[:, c, half * 512:half * 512 + 512]
                        if gain is None:
                            ins = nc.vector.tensor_copy(o, g.bank[i % 2][:])
                        else:
                            ins = nc.vector.tensor_scalar(o, g.bank[i % 2][:], cols[:, 2 * k:2 * k + 1],
                                                          cols[:, 2 * k + 1:2 * k + 2], ALU.mult, ALU.add)
                    ins.then_inc(kept, 1)


def cross_attention(nc, name, g, kvT, wq, wkT, bq, wv, normT, y, heads, D, scale, add):
    D1 = D + 1
    NC = -(-heads * D // 512)
    CH = heads // NC
    NV = CT * NC
    VA, VD = (NV + 1) // 2, NV // 2
    NG = (CT + 1) // 2
    CW = [401, 400, 400, 400]
    C0 = [0, 401, 801, 1201]
    NJ = QT * len(CW)
    NS = min(heads, 2)
    with Space(nc, name) as sb:
        ctxT = sb("ctxT", [KA, TC])
        wvs = sb("wv", [KA, heads * D])
        V = sb("V", [P, CT, heads, D1])
        wqs = [sb(f"wq{s}", [C, D]) for s in range(NS)]
        wks = [sb(f"wk{s}", [D, KA]) for s in range(NS)]
        bqs = [sb(f"bq{s}", [D, 1]) for s in range(NS)]
        qT = [sb(f"qT{s}", [D, T]) for s in range(NS)]
        qk = [sb(f"qk{s}", [KA, T]) for s in range(NS)]
        mx = [sb(f"mx{s}", [P, NJ]) for s in range(NS)]
        negm = [sb(f"negm{s}", [P, QT]) for s in range(NS)]
        PT = [sb(f"PT{s}", [P, CT, T]) for s in range(NS)]
        rl = [sb(f"rl{s}", [P, QT]) for s in range(NS)]
        p_q = g.bank[0][:, 0:T]
        p_qk = g.bank[0][:, T:2 * T]
        p_m = g.bank[1]
        p_s = [g.bank[2], g.bank[3]]
        p_st = [g.bank[4], g.bank[5]]
        p_o = [g.bank[6], g.bank[7]]
        p_v = [g.bank[2], g.bank[3], g.bank[4], g.bank[5]]
        names = ["wv_in", "ctx_in", "head_in0", "head_in1", "ones_set", "v_mm", "v_act", "v_dve", "q_mm", "q_sb",
                 "qk_mm", "qk_sb", "s_mm", "max_done", "negm_done", "m_mm", "qk_final", "st_mm", "exp_done",
                 "pv_mm", "recip_done", "out_free", "head_begun"]
        with stage(nc, name, *names) as (
                block, wv_in, ctx_in, head_in0, head_in1, ones_set, v_mm, v_act, v_dve, q_mm, q_sb, qk_mm, qk_sb,
                s_mm, max_done, negm_done, m_mm, qk_final, st_mm, exp_done, pv_mm, recip_done, out_free, head_begun):
            head_in = [head_in0, head_in1]

            def pipeline(eng, step):
                step(-1, 1, 0)
                step(0, 0, 0)
                if heads > 1:
                    with eng.Fori(0, (heads - 2) // 2) as k:
                        step(k * 2 + 1, 1, k + 1, True)
                        step(k * 2 + 2, 0, k + 1, True)
                    step(heads - 1, 1, heads // 2)
                step(heads, heads % 2, (heads + 1) // 2)

            def fronts(h, inner):
                return inner or h + 1 < heads

            def mids(h, inner):
                return inner or 0 <= h < heads

            def backs(h, inner):
                return inner or 1 <= h

            @block.sync
            def _(sp):
                sp.dma_start(wvs[:], wv).then_inc(wv_in, 16)
                with sp.Fori(0, B) as b:
                    sp.wait_ge(st_mm, b * (heads * NG))
                    sp.dma_start(ctxT[:], kvT[bass.ds(b, 1), :, :].rearrange("a k t -> (a k) t")).then_inc(ctx_in, 16)

                    def load(h, u):
                        s = u % NS
                        i = b * heads + h
                        if isinstance(h, int) and h < 2:
                            sp.wait_ge(qk_mm, b * heads)
                        else:
                            sp.wait_ge(qk_mm, i - 1)
                        for dst, src in ((wqs[s], wq), (wks[s], wkT), (bqs[s], bq)):
                            sp.dma_start(dst[:], src[bass.ds(h, 1), :, :].rearrange("a k t -> (a k) t")).then_inc(head_in[s], 16)
                    load(0, 0)
                    if heads > 1:
                        load(1, 1)
                        with sp.Fori(0, (heads - 2) // 2) as k:
                            load(k * 2 + 2, 0)
                            load(k * 2 + 3, 1)

            @block.tensor
            def _(pe):
                with pe.Fori(0, B) as b:
                    pe.wait_ge(wv_in, 16)
                    pe.wait_ge(ctx_in, b * 16 + 16)
                    pe.wait_ge(exp_done, b * (heads * NG))
                    pe.wait_ge(max_done, b * (heads * NJ))
                    for n in range(NV):
                        t, c = n // NC, n % NC
                        r = P if t < CT - 1 else LAST
                        if n >= 4:
                            pe.wait_ge((v_act, v_dve)[n % 2], b * (VA, VD)[n % 2] + (n - 4) // 2 + 1)
                        nc.tensor.matmul(p_v[n % 4][0:r, 0:CH * D], ctxT[:, t * P:t * P + r],
                                         wvs[:, c * CH * D:(c + 1) * CH * D], start=True, stop=True).then_inc(v_mm, 1)
                    pe.wait_ge(v_act, b * VA + VA)
                    pe.wait_ge(v_dve, b * VD + VD)

                    def step(h, u, pair, inner=False):
                        i = b * heads + h
                        sf, sm = (u + 1) % NS, u % NS
                        front, mid, back = fronts(h, inner), mids(h, inner), backs(h, inner)
                        if front:
                            f = i + 1
                            pe.wait_ge(head_in[sf], (b * (heads // NS) + pair + 1) * 48)
                            if not (isinstance(h, int) and h < 0):
                                pe.wait_ge(qk_sb, f)
                            else:
                                pe.wait_ge(qk_sb, b * heads)
                            pe.sem_inc(head_begun, 1)
                            nc.tensor.matmul(p_q[0:D, :], wqs[sf][:], normT[:, 0, bass.ds(b * T, T)],
                                             start=True, stop=True).then_inc(q_mm, 1)

                        def scores(j):
                            a, c = j // len(CW), j % len(CW)
                            if j >= 2 or inner or h >= 0:
                                pe.wait_ge(max_done, f * NJ + j - 1)
                            nc.tensor.matmul(p_s[j % 2][:, 0:CW[c]], qk[sf][:, a * P:(a + 1) * P],
                                             ctxT[:, C0[c]:C0[c] + CW[c]], start=True, stop=True).then_inc(s_mm, 1)

                        def scores_t(n):
                            if n == 0:
                                pe.wait_ge(qk_final, i + 1)
                            if n >= 2:
                                pe.wait_ge(exp_done, i * NG + n - 1)
                            elif inner or h > 0:
                                pe.wait_ge(exp_done, i * NG if n == 0 else i * NG - 1)
                            for t in range(2 * n, min(2 * n + 2, CT)):
                                r = P if t < CT - 1 else LAST
                                mm = nc.tensor.matmul(p_st[n % 2][0:r, (t % 2) * T:(t % 2 + 1) * T],
                                                      ctxT[:, t * P:t * P + r], qk[sm][:], start=True, stop=True)
                            mm.then_inc(st_mm, 1)

                        def values(t):
                            k = i - 1
                            hk = h - 1
                            if t == 0:
                                pe.wait_ge(out_free, k + 3 - NS)
                            if t % 2 == 0:
                                pe.wait_ge(exp_done, k * NG + t // 2 + 1)
                            r = P if t < CT - 1 else LAST
                            for a in range(QT):
                                mm = nc.tensor.matmul(p_o[sf][:, a * D1:(a + 1) * D1], PT[sf][0:r, t, a * P:(a + 1) * P],
                                                      V[0:r, t, bass.ds(hk, 1), :].rearrange("p a d -> p (a d)"),
                                                      start=(t == 0 and a == 0), stop=(t == CT - 1),
                                                      skip_group_check=True)
                            if t == CT - 1:
                                mm.then_inc(pv_mm, 1)

                        if mid:
                            scores_t(0)
                        if front:
                            pe.wait_ge(q_sb, f + 1)
                            nc.tensor.matmul(p_qk[0:KA, :], wks[sf][:], qT[sf][:], start=True, stop=True).then_inc(qk_mm, 1)
                        if mid:
                            scores_t(1)
                        if front:
                            pe.wait_ge(qk_sb, f + 1)
                        for j in range(NJ):
                            if front:
                                scores(j)
                            if mid and j + 2 < NG:
                                scores_t(j + 2)
                            if back:
                                values(j)
                        if back:
                            values(8)
                            values(9)
                        if front:
                            pe.wait_ge(negm_done, f + 1)
                            for a in range(QT):
                                mm = nc.tensor.matmul(p_m[CC:KA, a * P:(a + 1) * P], negm[sf][:, a:a + 1], g.ident[:],
                                                      start=True, stop=True)
                            mm.then_inc(m_mm, 1)
                        if back:
                            for t in range(10, CT):
                                values(t)

                    pipeline(pe, step)

            @block.scalar
            def _(act):
                with act.Fori(0, B) as b:
                    act.wait_ge(pv_mm, b * heads)
                    for n in range(0, NV, 2):
                        t, c = n // NC, n % NC
                        r = P if t < CT - 1 else LAST
                        act.wait_ge(v_mm, b * NV + n + 1)
                        nc.scalar.copy(V[0:r, t, c * CH:(c + 1) * CH, 0:D],
                                       p_v[n % 4][0:r, 0:CH * D].rearrange("p (h d) -> p h d", d=D)).then_inc(v_act, 1)

                    def step(h, u, pair, inner=False):
                        i = b * heads + h
                        sm = u % NS
                        if not mids(h, inner):
                            return
                        if inner or h >= 2:
                            act.wait_ge(pv_mm, i - 1)
                        for n in range(NG):
                            act.wait_ge(st_mm, i * NG + n + 1)
                            m = min(2, CT - 2 * n)
                            r = P if m == 2 else LAST
                            nc.scalar.activation(PT[sm][0:r, 2 * n:2 * n + m, :].rearrange("p t q -> p (t q)"),
                                                 p_st[n % 2][0:r, 0:m * T], ACT.Exp, scale=scale).then_inc(exp_done, 1)
                    pipeline(act, step)

            @block.vector
            def _(dve):
                nc.vector.memset(V[:, :, :, D:D1], 1.0).then_inc(ones_set, 1)
                dve.wait_ge(ones_set, 1)
                dve.sem_inc(out_free, 2)
                with dve.Fori(0, B) as b:
                    dve.wait_ge(pv_mm, b * heads)
                    for n in range(1, NV, 2):
                        t, c = n // NC, n % NC
                        r = P if t < CT - 1 else LAST
                        dve.wait_ge(v_mm, b * NV + n + 1)
                        nc.vector.tensor_copy(V[0:r, t, c * CH:(c + 1) * CH, 0:D],
                                              p_v[n % 4][0:r, 0:CH * D].rearrange("p (h d) -> p h d", d=D)).then_inc(v_dve, 1)

                    def step(h, u, pair, inner=False):
                        i = b * heads + h
                        sf = (u + 1) % NS
                        if fronts(h, inner):
                            f = i + 1
                            dve.wait_ge(q_mm, f + 1)
                            nc.vector.tensor_scalar(qT[sf][:], p_q[0:D, :], bqs[sf][:, 0:1], None, ALU.add).then_inc(q_sb, 1)
                            dve.wait_ge(qk_mm, f + 1)
                            if inner or h >= 1:
                                dve.wait_ge(st_mm, (f - 1) * NG)
                            nc.vector.tensor_copy(qk[sf][:], p_qk[0:KA, :]).then_inc(qk_sb, 1)
                            for j in range(NJ):
                                dve.wait_ge(s_mm, f * NJ + j + 1)
                                nc.vector.tensor_reduce(mx[sf][:, j:j + 1], p_s[j % 2][:, 0:CW[j % len(CW)]], AX.X,
                                                        ALU.max).then_inc(max_done, 1)
                            dve.wait_ge(max_done, f * NJ + NJ)
                            nc.vector.tensor_reduce(negm[sf][:], mx[sf][:].rearrange("p (a c) -> p a c", a=QT), AX.X,
                                                    ALU.max, negate=True).then_inc(negm_done, 1)
                            dve.wait_ge(m_mm, f + 1)
                            nc.vector.tensor_tensor(qk[sf][CC:KA, :], qk[sf][CC:KA, :], p_m[CC:KA, 0:T],
                                                    ALU.add).then_inc(qk_final, 1)
                        if backs(h, inner):
                            k, hk = i - 1, h - 1
                            o = p_o[sf][:, 0:QT * D1].rearrange("p (a d) -> p a d", d=D1)
                            dve.wait_ge(pv_mm, k + 1)
                            nc.vector.reciprocal(rl[sf][:], o[:, :, D]).then_inc(recip_done, 1)
                            dve.wait_ge(recip_done, k + 1)
                            for a in range(QT):
                                dst = y[:, bass.ds(b * QT + a, 1), bass.ds(hk * D, D)].rearrange("p a d -> p (a d)")
                                if add:
                                    ins = nc.vector.scalar_tensor_tensor(out=dst, in0=o[:, a, 0:D], scalar=rl[sf][:, a:a + 1],
                                                                         in1=dst, op0=ALU.mult, op1=ALU.add)
                                else:
                                    ins = nc.vector.tensor_scalar(dst, o[:, a, 0:D], rl[sf][:, a:a + 1], None, ALU.mult)
                            ins.then_inc(out_free, 1)
                    pipeline(dve, step)


def self_attention(nc, name, g, wq, wk, bq, bk, wv, bv, qsrcT, kvsrcT, y, D, scale, causal):
    D1 = D + 1
    DP = 32
    KM = DP + 1
    NHEAD = 64 if bq is not None else 32
    with Space(nc, name) as sb:
        wvs = sb("wv", [C, H * D])
        bvs = sb("bv", [P, H * D]) if bv is not None else None
        V = sb("V", [P, NT, H, D1])
        ones = sb("ones", [P, 1])
        mask = sb("mask", [P, QT, T]) if causal else None
        sm = sb("masked", [P, QT, T]) if causal else None
        wqs = [sb(f"wq{s}", [C, DP]) for s in range(2)]
        wks = [sb(f"wk{s}", [C, DP]) for s in range(2)]
        bs = [sb(f"b{s}", [DP, 2]) for s in range(2)] if bq is not None else None
        qT = [sb(f"qT{s}", [KM, T]) for s in range(2)]
        kT = [sb(f"kT{s}", [KM, T]) for s in range(2)]
        negm = [sb(f"negm{s}", [P, QT]) for s in range(2)]
        PT = [sb(f"PT{s}", [P, QT, T]) for s in range(2)]
        PD = [sb(f"PD{s}", [P, QT, P]) for s in range(2)]
        rl = [sb(f"rl{s}", [P, QT]) for s in range(2)]
        p_qk, p_m = g.bank[0], g.bank[1]
        p_s, p_st, p_o = [g.bank[2], g.bank[3]], [g.bank[4], g.bank[5]], [g.bank[6], g.bank[7]]
        names = ["wv_in", "head_in0", "head_in1", "consts", "select_begun", "v_mm", "v_sb", "qk_mm", "qk_sb", "s_mm", "masked", "s_read",
                 "negm_done", "m_mm", "q_final", "st_mm", "exp_done", "diag_done", "pv_mm", "recip_done", "out_free", "head_begun"]
        with stage(nc, name, *names) as (
                block, wv_in, head_in0, head_in1, consts, select_begun, v_mm, v_sb, qk_mm, qk_sb, s_mm, masked, s_read, negm_done,
                m_mm, q_final, st_mm, exp_done, diag_done, pv_mm, recip_done, out_free, head_begun):
            head_in = [head_in0, head_in1]

            def pipeline(eng, step):
                step(-1, 1, 0)
                step(0, 0, 0)
                with eng.Fori(0, (H - 2) // 2) as k:
                    step(k * 2 + 1, 1, k + 1, True)
                    step(k * 2 + 2, 0, k + 1, True)
                step(H - 1, 1, H // 2)
                step(H, 0, (H + 1) // 2)

            def fronts(h, inner):
                return inner or h + 1 < H

            def mids(h, inner):
                return inner or 0 <= h < H

            def backs(h, inner):
                return inner or 1 <= h

            @block.sync
            def _(sp):
                sp.dma_start(wvs[:], wv).then_inc(wv_in, 16)
                if bv is not None:
                    sp.dma_start(bvs[:], rows(bv)).then_inc(wv_in, 16)
                with sp.Fori(0, B) as b:
                    def load(h, u):
                        i = b * H + h
                        if isinstance(h, int) and h < 2:
                            sp.wait_ge(qk_sb, b * H)
                        else:
                            sp.wait_ge(qk_sb, i - 1)
                        sp.dma_start(wqs[u][:], wq[bass.ds(h, 1), :, :].rearrange("a k t -> (a k) t")).then_inc(head_in[u], 16)
                        sp.dma_start(wks[u][:], wk[bass.ds(h, 1), :, :].rearrange("a k t -> (a k) t")).then_inc(head_in[u], 16)
                        if bq is not None:
                            sp.dma_start(bs[u][:, 0:1], bq[bass.ds(h, 1), :, :].rearrange("a k t -> (a k) t")).then_inc(head_in[u], 16)
                            sp.dma_start(bs[u][:, 1:2], bk[bass.ds(h, 1), :, :].rearrange("a k t -> (a k) t")).then_inc(head_in[u], 16)
                    load(0, 0)
                    load(1, 1)
                    with sp.Fori(0, (H - 2) // 2) as k:
                        load(k * 2 + 2, 0)
                        load(k * 2 + 3, 1)

            @block.gpsimd
            def _(pool):
                if causal:
                    nc.gpsimd.memset(mask[:], 0.0).then_inc(masked, 1)
                    pool.wait_ge(masked, 1)
                    nc.gpsimd.affine_select(out=mask[:], in_=mask[:], compare_op=ALU.is_ge, fill=LOWEST, base=0,
                                            pattern=[[P, QT], [-1, T]], channel_multiplier=1).then_inc(consts, 1)
                with pool.Fori(0, B) as b:
                    def step(h, u, pair, inner=False):
                        if not mids(h, inner):
                            return
                        i = b * H + h
                        pool.wait_ge(exp_done, i + 1)
                        if inner or h >= 2:
                            pool.wait_ge(pv_mm, i - 1)
                        pool.sem_inc(select_begun, 1)
                        for a in range(QT):
                            ins = nc.gpsimd.affine_select(out=PD[u][:, a, :], in_=PT[u][:, a, a * P:(a + 1) * P],
                                                          compare_op=ALU.is_ge if causal else ALU.is_gt, fill=0.0, base=0,
                                                          pattern=[[1 if causal else -1, P]],
                                                          channel_multiplier=-1 if causal else 1)
                        ins.then_inc(diag_done, 1)
                    pipeline(pool, step)

            @block.tensor
            def _(pe):
                pe.wait_ge(wv_in, 16 if bv is None else 32)
                for n in range(NT):
                    if n >= 2:
                        pe.wait_ge(v_sb, n - 1)
                    nc.tensor.matmul(p_s[n % 2][:, 0:H * D], kvsrcT[:, 0, n * P:(n + 1) * P], wvs[:],
                                     start=True, stop=True).then_inc(v_mm, 1)
                pe.wait_ge(v_sb, NT)
                pe.wait_ge(consts, 4 if causal else 3)
                with pe.Fori(0, B) as b:
                    def step(h, u, pair, inner=False):
                        i = b * H + h
                        sf, f = (u + 1) % 2, i + 1
                        front, mid, back = fronts(h, inner), mids(h, inner), backs(h, inner)
                        if front:
                            pe.wait_ge(head_in[sf], (b * (H // 2) + pair + 1) * NHEAD)
                            pe.wait_ge(qk_sb, f if inner or h >= 0 else b * H)
                            pe.sem_inc(head_begun, 1)
                            nc.tensor.matmul(p_qk[0:DP, 0:T], wqs[sf][:], qsrcT[:, 0, bass.ds(b * T, T)], start=True, stop=True)
                            nc.tensor.matmul(p_qk[0:DP, T:2 * T], wks[sf][:], kvsrcT[:, 0, bass.ds(b * T, T)],
                                             start=True, stop=True).then_inc(qk_mm, 1)
                        if mid:
                            pe.wait_ge(q_final, i + 1)
                            if inner or h >= 2:
                                pe.wait_ge(exp_done, i - 1)
                            for t in range(QT):
                                q0 = t * P if causal else 0
                                mm = nc.tensor.matmul(p_st[u][:, t * T + q0:(t + 1) * T], kT[u][:, t * P:(t + 1) * P],
                                                      qT[u][:, q0:T], start=True, stop=True)
                            mm.then_inc(st_mm, 1)
                        if front:
                            pe.wait_ge(qk_sb, f + 1)
                            if inner or h >= 1:
                                pe.wait_ge(s_read, f - 1)
                            for a in range(QT):
                                mm = nc.tensor.matmul(p_s[sf][:, a * T:(a + 1) * T], qT[sf][0:DP, a * P:(a + 1) * P],
                                                      kT[sf][0:DP, :], start=True, stop=True)
                            mm.then_inc(s_mm, 1)
                        if back:
                            k, hk = i - 1, h - 1
                            pe.wait_ge(diag_done, k + 1)
                            pe.wait_ge(exp_done, k + 1)
                            pe.wait_ge(out_free, k + 1)

                            def block_(a, lhsT, t, first=False, last=False):
                                w = D1 if causal else D
                                return nc.tensor.matmul(p_o[sf][:, a * D1:a * D1 + w], lhsT,
                                                        V[:, bass.ds(b * QT + t, 1), bass.ds(hk, 1), 0:w].rearrange("p a h d -> p (a h d)"),
                                                        start=first, stop=last, skip_group_check=True)
                            if causal:
                                block_(0, PD[sf][:, 0, :], 0, first=True, last=True)
                                block_(1, PT[sf][:, 0, P:T], 0)
                                mm = block_(1, PD[sf][:, 1, :], 1, last=True)
                            else:
                                block_(0, PD[sf][:, 0, :], 0, first=True)
                                block_(0, PT[sf][:, 1, 0:P], 1, last=True)
                                block_(1, PD[sf][:, 1, :], 1, last=True)
                                for a in range(QT):
                                    for t in range(QT):
                                        mm = nc.tensor.matmul(p_o[sf][:, a * D1 + D:(a + 1) * D1], PT[sf][:, t, a * P:(a + 1) * P],
                                                              ones[:], start=False, stop=(t == QT - 1), skip_group_check=True)
                            mm.then_inc(pv_mm, 1)
                        if front:
                            pe.wait_ge(negm_done, f + 1)
                            for a in range(QT):
                                mm = nc.tensor.matmul(p_m[DP:KM, a * P:(a + 1) * P], negm[sf][:, a:a + 1], g.ident[:],
                                                      start=True, stop=True)
                            mm.then_inc(m_mm, 1)
                    pipeline(pe, step)

            @block.scalar
            def _(act):
                with act.Fori(0, B) as b:
                    def step(h, u, pair, inner=False):
                        i = b * H + h
                        if not mids(h, inner):
                            return
                        if inner or h >= 2:
                            act.wait_ge(pv_mm, i - 1)
                        act.wait_ge(st_mm, i + 1)
                        if causal:
                            nc.scalar.activation(PT[u][:, 0, :], p_st[u][:, 0:T], ACT.Exp, scale=scale)
                            ins = nc.scalar.activation(PT[u][:, 1, P:T], p_st[u][:, T + P:2 * T], ACT.Exp, scale=scale)
                        else:
                            ins = nc.scalar.activation(PT[u][:].rearrange("p t q -> p (t q)"), p_st[u][:], ACT.Exp, scale=scale)
                        ins.then_inc(exp_done, 1)
                    pipeline(act, step)

            @block.vector
            def _(dve):
                for s in range(2):
                    nc.vector.memset(kT[s][DP:KM, :], 1.0).then_inc(consts, 1)
                nc.vector.memset(V[:, :, :, D:D1], 1.0)
                nc.vector.memset(ones[:], 1.0).then_inc(consts, 1)
                dve.sem_inc(out_free, 2)
                dve.wait_ge(consts, 4 if causal else 3)
                dve.wait_ge(wv_in, 16 if bv is None else 32)
                for n in range(NT):
                    dve.wait_ge(v_mm, n + 1)
                    o = V[:, n, :, 0:D]
                    i_ = p_s[n % 2][:, 0:H * D].rearrange("p (h d) -> p h d", d=D)
                    if bv is None:
                        nc.vector.tensor_copy(o, i_).then_inc(v_sb, 1)
                    else:
                        nc.vector.tensor_tensor(o, i_, bvs[:].rearrange("p (h d) -> p h d", d=D), ALU.add).then_inc(v_sb, 1)
                with dve.Fori(0, B) as b:
                    def step(h, u, pair, inner=False):
                        i = b * H + h
                        sf, f = (u + 1) % 2, i + 1
                        if fronts(h, inner):
                            dve.wait_ge(qk_mm, f + 1)
                            if inner or h >= 1:
                                dve.wait_ge(st_mm, f - 1)
                            if bq is None:
                                nc.vector.tensor_copy(qT[sf][0:DP, :], p_qk[0:DP, 0:T])
                                nc.vector.tensor_copy(kT[sf][0:DP, :], p_qk[0:DP, T:2 * T]).then_inc(qk_sb, 1)
                            else:
                                nc.vector.tensor_scalar(qT[sf][0:DP, :], p_qk[0:DP, 0:T], bs[sf][:, 0:1], None, ALU.add)
                                nc.vector.tensor_scalar(kT[sf][0:DP, :], p_qk[0:DP, T:2 * T], bs[sf][:, 1:2], None,
                                                        ALU.add).then_inc(qk_sb, 1)
                            dve.wait_ge(s_mm, f + 1)
                            if causal:
                                nc.vector.tensor_tensor(sm[:], p_s[sf][:].rearrange("p (a t) -> p a t", t=T), mask[:],
                                                        ALU.add).then_inc(s_read, 1)
                                dve.wait_ge(s_read, f + 1)
                                nc.vector.tensor_reduce(negm[sf][:], sm[:], AX.X, ALU.max, negate=True).then_inc(negm_done, 1)
                            else:
                                nc.vector.tensor_reduce(negm[sf][:], p_s[sf][:].rearrange("p (a t) -> p a t", t=T), AX.X,
                                                        ALU.max, negate=True).then_inc(negm_done, 1)
                                dve.wait_ge(negm_done, f + 1)
                                dve.sem_inc(s_read, 1)
                            dve.wait_ge(m_mm, f + 1)
                            nc.vector.tensor_copy(qT[sf][DP:KM, :], p_m[DP:KM, 0:T]).then_inc(q_final, 1)
                        if backs(h, inner):
                            k, hk = i - 1, h - 1
                            o = p_o[sf][:, 0:QT * D1].rearrange("p (a d) -> p a d", d=D1)
                            dve.wait_ge(pv_mm, k + 1)
                            nc.vector.reciprocal(rl[sf][:], o[:, :, D]).then_inc(recip_done, 1)
                            dve.wait_ge(recip_done, k + 1)
                            for a in range(QT):
                                dst = y[:, bass.ds(b * QT + a, 1), bass.ds(hk * D, D)].rearrange("p a d -> p (a d)")
                                ins = nc.vector.tensor_scalar(dst, o[:, a, 0:D], rl[sf][:, a:a + 1], None, ALU.mult)
                            ins.then_inc(out_free, 1)
                    pipeline(dve, step)


def add_tokens(nc, name, dst, src):
    with stage(nc, name, "added") as (block, added):
        @block.vector
        def _(dve):
            nc.vector.tensor_tensor(dst[:], dst[:], src[:], ALU.add).then_inc(added, 1)
            dve.wait_ge(added, 1)


def linear(nc, name, g, srcT, kc, w, bias, dst):
    with Space(nc, name) as sb:
        ws = sb("w", [P, kc, C])
        bs = sb("b", [P, C])
        with stage(nc, name, "in_", "product", "used", "step") as (block, in_, product, used, step):
            @block.sync
            def _(sp):
                sp.dma_start(ws[:], w.rearrange("(k p) c -> p k c", p=P)).then_inc(in_, 16)
                sp.dma_start(bs[:], rows(bias)).then_inc(in_, 16)

            @block.tensor
            def _(pe):
                pe.wait_ge(in_, 32)
                for n in range(NT):
                    for k in range(kc):
                        mm = nc.tensor.matmul(g.bank[n // 4][:, n % 4 * P:(n % 4 + 1) * P], srcT[:, k, n * P:(n + 1) * P],
                                              ws[:, k, :], start=(k == 0), stop=(k == kc - 1))
                    if n % 4 == 3:
                        mm.then_inc(product, 1)

            @block.vector
            def _(dve):
                link = Link(dve, step)
                dve.wait_ge(in_, 32)
                link(nc.vector.tensor_tensor(dst[:], dst[:], bs[:].rearrange("p (a c) -> p a c", a=1).to_broadcast([P, NT, C]), ALU.add))
                for n in range(2):
                    dve.wait_ge(product, n + 1)
                    o = dst[:, 4 * n:4 * n + 4, :]
                    link(nc.vector.tensor_tensor(o, o, g.bank[n][:].rearrange("p (a c) -> p a c", c=C), ALU.add))


def hidden(nc, name, g, srcT, w, bias, dstT, fc):
    with Space(nc, name) as sb:
        ws = sb("w", [P, fc * P])
        bs = sb("b", [P, fc])
        with stage(nc, name, "in_", "product", "done") as (block, in_, product, done):
            @block.sync
            def _(sp):
                sp.dma_start(ws[:], w).then_inc(in_, 16)
                sp.dma_start(bs[:], bias).then_inc(in_, 16)

            @block.tensor
            def _(pe):
                pe.wait_ge(in_, 32)
                for n in range(2 * fc):
                    f, half = n // 2, n % 2
                    if n >= 4:
                        pe.wait_ge(done, n - 3)
                    nc.tensor.matmul(g.bank[n % 4][:], ws[:, f * P:(f + 1) * P], srcT[:, 0, half * 512:half * 512 + 512],
                                     start=True, stop=True).then_inc(product, 1)

            @block.scalar
            def _(act):
                for n in range(2 * fc):
                    f, half = n // 2, n % 2
                    act.wait_ge(product, n + 1)
                    nc.scalar.activation(dstT[:, f, half * 512:half * 512 + 512], g.bank[n % 4][:], ACT.Gelu,
                                         bias=bs[:, f:f + 1]).then_inc(done, 1)


def experts(nc, name, g, srcT, w1, b1, w2, wts, dst, kind, FC, FP=P):
    gated = kind == "silu"
    func = {"silu": ACT.Silu, "relu": ACT.Relu, "gelu": ACT.Gelu}[kind]
    W1 = FC * FP * (2 if gated else 1)
    NW = 32 if b1 is None else 48
    NB = 2 if gated else 4
    with Space(nc, name) as sb:
        w1s = [sb(f"w1_{s}", [P, W1]) for s in range(2)]
        w2s = [sb(f"w2_{s}", [FP, FC * C]) for s in range(2)]
        b1s = [sb(f"b1_{s}", [FP, FC]) for s in range(2)] if b1 is not None else None
        hT = sb("hT", [FP, FC, B * T])
        sg = [sb(f"sg{s}", [FP, 512]) for s in range(2)] if gated else None
        p_up = [g.bank[s] for s in range(4)]
        p_dn = [g.bank[4], g.bank[5]]
        with stage(nc, name, "w_in0", "w_in1", "up_mm", "up_free", "gate_done", "h_done", "down_mm", "down_free") as (
                block, w_in0, w_in1, up_mm, up_free, gate_done, h_done, down_mm, down_free):
            w_in = [w_in0, w_in1]
            NH = 2 * FC

            @block.sync
            def _(sp):
                with sp.Fori(0, E // 2) as k:
                    for u in range(2):
                        sp.wait_ge(down_mm, k * 4 + 2 * u)
                        e = bass.ds(k * 2 + u, 1)
                        sp.dma_start(w1s[u][:], w1[e, :, :].rearrange("a k t -> (a k) t")).then_inc(w_in[u], 16)
                        sp.dma_start(w2s[u][:], w2[e, :, :].rearrange("a k t -> (a k) t")).then_inc(w_in[u], 16)
                        if b1 is not None:
                            sp.dma_start(b1s[u][:], b1[e, :, :].rearrange("a k t -> (a k) t")).then_inc(w_in[u], 16)

            @block.tensor
            def _(pe):
                pe.sem_inc(down_mm, 2)
                with pe.Fori(0, E // 2) as k:
                    for u in range(2):
                        e = k * 2 + u
                        pe.wait_ge(w_in[u], (k + 1) * NW)
                        for n in range(NH):
                            half, f = n // FC, n % FC
                            x = srcT[:, 0, half * 512:half * 512 + 512]
                            pe.wait_ge(up_free, e * NH + n + 1)
                            s = n % NB
                            mm = nc.tensor.matmul(p_up[s][0:FP, :], w1s[u][:, f * FP:(f + 1) * FP], x, start=True, stop=True)
                            if gated:
                                mm = nc.tensor.matmul(p_up[2 + s][0:FP, :], w1s[u][:, (FC + f) * FP:(FC + f + 1) * FP], x,
                                                      start=True, stop=True)
                            mm.then_inc(up_mm, 1)
                        for half in range(2):
                            pe.wait_ge(h_done, e * NH + (half + 1) * FC)
                            pe.wait_ge(down_free, e * 2 + half + 1)
                            for n in range(4):
                                for f in range(FC):
                                    t = (half * 4 + n) * P
                                    mm = nc.tensor.matmul(p_dn[half][:, n * P:(n + 1) * P], hT[:, f, t:t + P],
                                                          w2s[u][:, f * C:(f + 1) * C], start=(f == 0), stop=(f == FC - 1))
                            mm.then_inc(down_mm, 1)

            @block.scalar
            def _(act):
                if not gated:
                    act.sem_inc(up_free, NB)
                with act.Fori(0, E // 2) as k:
                    for u in range(2):
                        e = k * 2 + u
                        for n in range(NH):
                            half, f = n // FC, n % FC
                            o = hT[:, f, half * 512:half * 512 + 512]
                            act.wait_ge(up_mm, e * NH + n + 1)
                            if gated:
                                if n < 2:
                                    act.wait_ge(h_done, e * NH)
                                else:
                                    act.wait_ge(h_done, e * NH + n - 1)
                                nc.scalar.activation(sg[n % 2][:], p_up[n % NB][0:FP, :], func).then_inc(gate_done, 1)
                            else:
                                if f == 0:
                                    act.wait_ge(down_mm, e * 2 + half + 1)
                                bias = b1s[u][:, f:f + 1] if b1 is not None else 0.0
                                nc.scalar.activation(o, p_up[n % NB][0:FP, :], func, bias=bias).then_inc(h_done, 1)
                                act.wait_ge(h_done, e * NH + n + 1)
                                act.sem_inc(up_free, 1)

            @block.vector
            def _(dve):
                dve.sem_inc(down_free, 2)
                if gated:
                    dve.sem_inc(up_free, NB)
                with dve.Fori(0, E // 2) as k:
                    for u in range(2):
                        e = k * 2 + u
                        if gated:
                            for n in range(NH):
                                half, f = n // FC, n % FC
                                o = hT[:, f, half * 512:half * 512 + 512]
                                dve.wait_ge(gate_done, e * NH + n + 1)
                                if f == 0:
                                    dve.wait_ge(down_mm, e * 2 + half + 1)
                                nc.vector.tensor_tensor(o, sg[n % 2][:], p_up[2 + n % NB][0:FP, :], ALU.mult).then_inc(h_done, 1)
                                dve.wait_ge(h_done, e * NH + n + 1)
                                dve.sem_inc(up_free, 1)
                        for half in range(2):
                            dve.wait_ge(down_mm, e * 2 + half + 3)
                            dve.wait_ge(down_free, e * 2 + half + 1)
                            for n in range(4):
                                t = half * 4 + n
                                ins = nc.vector.scalar_tensor_tensor(out=dst[:, t, :], in0=p_dn[half][:, n * P:(n + 1) * P],
                                                                     scalar=wts[:, t, bass.ds(e, 1)], in1=dst[:, t, :],
                                                                     op0=ALU.mult, op1=ALU.add)
                            ins.then_inc(down_free, 1)


def expert_biases(nc, name, g, wts, b2, dst):
    with Space(nc, name) as sb:
        wT = sb("wT", [E, B * T])
        b2s = sb("b2", [E, C])
        with stage(nc, name, "in_", "turned", "kept", "product", "step") as (block, in_, turned, kept, product, step):
            @block.sync
            def _(sp):
                sp.dma_start(b2s[:], b2).then_inc(in_, 16)

            @block.tensor
            def _(pe):
                for n in range(NT):
                    mm = nc.tensor.transpose(g.bank[n // 4][0:E, n % 4 * P:(n % 4 + 1) * P], wts[:, n, :], g.ident[:])
                    mm.then_inc(turned, 1)
                pe.wait_ge(kept, 2)
                pe.wait_ge(in_, 16)
                for n in range(NT):
                    nc.tensor.matmul(g.bank[2 + n // 4][:, n % 4 * P:(n % 4 + 1) * P], wT[:, n * P:(n + 1) * P], b2s[:],
                                     start=True, stop=True).then_inc(product, 1)

            @block.vector
            def _(dve):
                link = Link(dve, step)
                for n in range(2):
                    dve.wait_ge(turned, 4 * n + 4)
                    nc.vector.tensor_copy(wT[:, n * 512:(n + 1) * 512], g.bank[n][0:E, :]).then_inc(kept, 1)
                for n in range(2):
                    dve.wait_ge(product, 4 * n + 4)
                    o = dst[:, 4 * n:4 * n + 4, :]
                    link(nc.vector.tensor_tensor(o, o, g.bank[2 + n][:].rearrange("p (a c) -> p a c", c=C), ALU.add))


class Picks:

    def __init__(self, nc, sb, link, n):
        self.nc, self.link, self.n = nc, link, n
        self.rev = sb("rev", [P, 1, E])
        self.r = sb("r", [P, n, E])
        self.rm = sb("rm", [P, n, 1])
        for e in range(E):
            link(nc.vector.memset(self.rev[:, :, e:e + 1], float(E - e)))

    def wide(self, ap):
        return ap[:].to_broadcast([P, self.n, E])

    def first(self, onehot, top, s):
        nc, link = self.nc, self.link
        link(nc.vector.tensor_reduce(top[:], s[:], AX.X, ALU.max))
        link(nc.vector.tensor_tensor(self.r[:], s[:], self.wide(top), ALU.is_equal))
        link(nc.vector.tensor_tensor(self.r[:], self.r[:], self.wide(self.rev), ALU.mult))
        link(nc.vector.tensor_reduce(self.rm[:], self.r[:], AX.X, ALU.max))
        link(nc.vector.tensor_tensor(onehot[:], self.r[:], self.wide(self.rm), ALU.is_equal))

    def without(self, out, s, onehot):
        nc, link = self.nc, self.link
        link(nc.vector.tensor_scalar(self.r[:], onehot[:], -1.0, 1.0, ALU.mult, ALU.add))
        link(nc.vector.tensor_tensor(out[:], s[:], self.r[:], ALU.mult))
        link(nc.vector.scalar_tensor_tensor(out=out[:], in0=onehot[:], scalar=LOWEST, in1=out[:], op0=ALU.mult, op1=ALU.add))


def router(nc, name, g, kind, srcT, wr, wts, br=None):
    n = B if kind == "batch" else NT
    with Space(nc, name) as sb:
        wrs = sb("wr", [C, E])
        brs = sb("br", [P, 1, E])
        s = sb("s", [P, n, E])
        s2 = sb("s2", [P, n, E])
        oh1, oh2 = sb("oh1", [P, n, E]), sb("oh2", [P, n, E])
        m1, m2 = sb("m1", [P, n, 1]), sb("m2", [P, n, 1])
        d, ex = sb("d", [P, 2, n, E]), sb("ex", [P, 2, n, E])
        t = sb("t", [P, n, E])
        u1, u2 = sb("u1", [P, n, 1]), sb("u2", [P, n, 1])
        mean = sb("mean", [P, B])
        meanw = sb("meanw", [P, B, P])
        with stage(nc, name, "in_", "mean_done", "logits", "exp_in", "exp_out", "step") as (
                block, in_, mean_done, logits, exp_in, exp_out, step):
            @block.sync
            def _(sp):
                sp.dma_start(wrs[:], wr).then_inc(in_, 16)
                if br is not None:
                    sp.dma_start(brs[:].rearrange("p a e -> p (a e)"), rows(br)).then_inc(in_, 16)

            @block.tensor
            def _(pe):
                pe.wait_ge(in_, 16 if br is None else 32)
                if kind == "batch":
                    pe.wait_ge(mean_done, 1)
                for i in range(n):
                    lhsT = meanw[:, i, :] if kind == "batch" else srcT[:, 0, i * P:(i + 1) * P]
                    nc.tensor.matmul(g.bank[0][:, i * E:(i + 1) * E], lhsT, wrs[:], start=True, stop=True).then_inc(logits, 1)

            @block.scalar
            def _(act):
                for k in range({"mixer": 2, "top2": 1, "batch": 2}[kind]):
                    act.wait_ge(exp_in, k + 1)
                    i_, o = (d[:, k], ex[:, k])
                    if kind == "mixer" or (kind == "batch" and k == 0):
                        nc.scalar.activation(o, i_, ACT.Exp).then_inc(exp_out, 1)
                    else:
                        nc.scalar.activation(u2[:], u1[:], ACT.Exp).then_inc(exp_out, 1)

            @block.vector
            def _(dve):
                link = Link(dve, step)
                v = nc.vector
                pick = Picks(nc, sb, link, n)
                wide = pick.wide
                if kind == "batch":
                    link(v.tensor_reduce(mean[:], srcT[:].rearrange("p a (b t) -> p (a b) t", b=B), AX.X, ALU.add))
                    link(v.tensor_scalar(mean[:], mean[:], 1.0 / T, None, ALU.mult))
                    link(v.tensor_copy(meanw[:], mean[:].rearrange("p (b a) -> p b a", a=1).to_broadcast([P, B, P])))
                    dve.sem_inc(mean_done, 1)
                dve.wait_ge(logits, n)
                link(v.tensor_copy(s[:], g.bank[0][:, 0:n * E].rearrange("p (n e) -> p n e", e=E)))
                if kind == "mixer":
                    def near(k, sc, top):
                        link(v.tensor_tensor(d[:, k], sc[:], wide(top), ALU.subtract))
                        dve.sem_inc(exp_in, 1)
                        link(v.scalar_tensor_tensor(out=t[:], in0=s[:], scalar=-1.0, in1=s[:], op0=ALU.mult, op1=ALU.max))
                        link(v.tensor_tensor(t[:], t[:], wide(top), ALU.max))
                        link(v.tensor_scalar(t[:], t[:], 2.0 * 0.01, None, ALU.mult))
                        link(v.tensor_tensor(s2[:], wide(top), s[:], ALU.subtract))
                        link(v.tensor_tensor(t[:], s2[:], t[:], ALU.is_le))

                    def gate(k, u):
                        dve.wait_ge(exp_out, k + 1)
                        link(v.tensor_tensor(t[:], t[:], ex[:, k], ALU.mult))
                        link(v.tensor_reduce(u[:], t[:], AX.X, ALU.add))
                        link(v.reciprocal(u[:], u[:]))
                    pick.first(oh1, m1, s)
                    near(0, s, m1)
                    gate(0, u1)
                    pick.without(s2, s, oh1)
                    pick.first(oh2, m2, s2)
                    near(1, s2, m2)
                    gate(1, u2)
                    link(v.tensor_tensor(oh1[:], oh1[:], wide(u1), ALU.mult))
                    link(v.tensor_tensor(oh2[:], oh2[:], wide(u2), ALU.mult))
                    link(v.tensor_tensor(wts[:], oh1[:], oh2[:], ALU.add))
                    return
                if kind == "batch":
                    link(v.tensor_tensor(s[:], s[:], wide(brs), ALU.add))
                    link(v.tensor_reduce(m1[:], s[:], AX.X, ALU.max))
                    link(v.tensor_tensor(d[:, 0], s[:], wide(m1), ALU.subtract))
                    dve.sem_inc(exp_in, 1)
                    dve.wait_ge(exp_out, 1)
                    link(v.tensor_reduce(u1[:], ex[:, 0], AX.X, ALU.add))
                    link(v.reciprocal(u1[:], u1[:]))
                    link(v.tensor_tensor(s[:], ex[:, 0], wide(u1), ALU.mult))
                pick.first(oh1, m1, s)
                pick.without(s2, s, oh1)
                pick.first(oh2, m2, s2)
                link(v.tensor_tensor(u1[:], m2[:], m1[:], ALU.subtract))
                dve.sem_inc(exp_in, 1)
                dve.wait_ge(exp_out, 2 if kind == "batch" else 1)
                link(v.tensor_scalar(u1[:], u2[:], 1.0, None, ALU.add))
                link(v.reciprocal(u1[:], u1[:]))
                link(v.tensor_tensor(u2[:], u2[:], u1[:], ALU.mult))
                if kind == "top2":
                    link(v.tensor_scalar(u1[:], u1[:], 0.5, None, ALU.mult))
                    link(v.tensor_scalar(u2[:], u2[:], 0.5, None, ALU.mult))
                link(v.tensor_tensor(oh1[:], oh1[:], wide(u1), ALU.mult))
                link(v.tensor_tensor(oh2[:], oh2[:], wide(u2), ALU.mult))
                if kind == "batch":
                    for a in range(QT):
                        link(v.tensor_tensor(wts[:].rearrange("p (b a) e -> p b a e", a=QT)[:, :, a, :], oh1[:], oh2[:], ALU.add))
                else:
                    link(v.tensor_tensor(wts[:], oh1[:], oh2[:], ALU.add))


def expert_choice(nc, name, g, srcT, wr, wts, keep):
    with Space(nc, name) as sb:
        wrs = sb("wr", [C, E])
        s = sb("s", [P, NT, E])
        top = sb("top", [P, NT, 1])
        pr = sb("pr", [P, NT, E])
        prw = sb("prw", [P, 2, E, QT, P])
        prt = sb("prt", [P, 2, E, T])
        before = sb("before", [P, QT, T])
        cmp_ = sb("cmp", [P, 2, T])
        ahead = sb("ahead", [P, 2, E, T])
        rank = sb("rank", [P, NT, E])
        with stage(nc, name, "in_", "logits", "exp_in", "exp_out", "made", "wide", "spread", "compared", "step") as (
                block, in_, logits, exp_in, exp_out, made, wide_done, spread, compared, step):
            @block.sync
            def _(sp):
                sp.dma_start(wrs[:], wr).then_inc(in_, 16)

            @block.gpsimd
            def _(pool):
                nc.gpsimd.memset(before[:], 1.0).then_inc(made, 1)
                pool.wait_ge(made, 1)
                nc.gpsimd.affine_select(out=before[:], in_=before[:], compare_op=ALU.is_gt, fill=0.0, base=0,
                                        pattern=[[P, QT], [-1, T]], channel_multiplier=1).then_inc(made, 1)

            @block.tensor
            def _(pe):
                pe.wait_ge(in_, 16)
                for i in range(NT):
                    nc.tensor.matmul(g.bank[0][:, i * E:(i + 1) * E], srcT[:, 0, i * P:(i + 1) * P], wrs[:],
                                     start=True, stop=True).then_inc(logits, 1)
                for b in range(B):
                    pe.wait_ge(wide_done, b + 1)
                    for e in range(E):
                        i = b * E + e
                        if i >= 4:
                            pe.wait_ge(spread, i - 3)
                        for a in range(QT):
                            mm = nc.tensor.matmul(g.bank[1 + i % 4][:, a * P:(a + 1) * P], prw[:, b % 2, e, a, :], g.ident[:],
                                                  start=True, stop=True)
                        mm.then_inc(compared, 1)

            @block.scalar
            def _(act):
                act.wait_ge(exp_in, 1)
                nc.scalar.activation(pr[:], s[:], ACT.Exp).then_inc(exp_out, 1)
                for i in range(B * E):
                    b, e = i // E, i % E
                    act.wait_ge(compared, i + 1)
                    if b >= 2 and e == 0:
                        act.wait_ge(made, 2 + b - 1)
                    nc.scalar.copy(prt[:, b % 2, e, :], g.bank[1 + i % 4][:, 0:T]).then_inc(spread, 1)

            @block.vector
            def _(dve):
                link = Link(dve, step)
                v = nc.vector
                dve.wait_ge(logits, NT)
                link(v.tensor_copy(s[:], g.bank[0][:, 0:NT * E].rearrange("p (n e) -> p n e", e=E)))
                link(v.tensor_reduce(top[:], s[:], AX.X, ALU.max))
                link(v.tensor_tensor(s[:], s[:], top[:].to_broadcast([P, NT, E]), ALU.subtract))
                dve.sem_inc(exp_in, 1)
                dve.wait_ge(exp_out, 1)
                link(v.tensor_reduce(top[:], pr[:], AX.X, ALU.add))
                link(v.reciprocal(top[:], top[:]))
                link(v.tensor_tensor(pr[:], pr[:], top[:].to_broadcast([P, NT, E]), ALU.mult))
                dve.wait_ge(made, 2)

                def widen(b):
                    for a in range(QT):
                        link(v.tensor_copy(prw[:, b % 2, :, a, :],
                                           pr[:, b * QT + a, :].rearrange("p (e a) -> p e a", a=1).to_broadcast([P, E, P])))
                    dve.sem_inc(wide_done, 1)
                widen(0)
                for b in range(B):
                    if b + 1 < B:
                        widen(b + 1)
                    for a in range(QT):
                        for e in range(E):
                            dve.wait_ge(spread, b * E + e + 1)
                            pc = pr[:, b * QT + a, e:e + 1]
                            link(v.scalar_tensor_tensor(out=cmp_[:, e % 2, :], in0=prt[:, b % 2, e, :], scalar=pc,
                                                        in1=before[:, a, :], op0=ALU.is_equal, op1=ALU.mult))
                            link(v.scalar_tensor_tensor(out=ahead[:, a, e, :], in0=prt[:, b % 2, e, :], scalar=pc,
                                                        in1=cmp_[:, e % 2, :], op0=ALU.is_gt, op1=ALU.add))
                        link(v.tensor_reduce(rank[:, b * QT + a, :], ahead[:, a], AX.X, ALU.add))
                    dve.sem_inc(made, 1)
                link(v.tensor_scalar(rank[:], rank[:], float(keep), None, ALU.is_lt))
                link(v.tensor_tensor(wts[:], rank[:], pr[:], ALU.mult))


def context_norm(nc, name, g, ctx, gain, shift, kvT):
    for b in range(B):
        with Space(nc, f"{name}{b}") as sb:
            c = sb("c", [P, CT, CC])
            z = sb("z", [P, CT, CC])
            zT = sb("zT", [KA, TC])
            cols = sb("cols", [CC, 2])
            with stage(nc, f"{name}{b}_load", "in_") as (block, in_):
                @block.sync
                def _(sp):
                    sp.dma_start(c[:, 0:CT - 1, :], ctx[b, 0:(CT - 1) * P, :].rearrange("(t p) c -> p t c", p=P)).then_inc(in_, 16)
                    sp.dma_start(c[0:LAST, CT - 1, :], ctx[b, (CT - 1) * P:TC, :]).then_inc(in_, 16)
                    sp.wait_ge(in_, 32)
            layernorm(nc, f"{name}{b}_ln", c, z, tiles=CT, width=CC, last=LAST)
            with stage(nc, f"{name}{b}_turn", "in_", "turned", "kept", "stored") as (block, in_, turned, kept, stored):
                @block.sync
                def _(sp):
                    sp.dma_start(cols[:, 0:1], gain.rearrange("(n a) -> n a", a=1)).then_inc(in_, 16)
                    sp.dma_start(cols[:, 1:2], shift.rearrange("(n a) -> n a", a=1)).then_inc(in_, 16)
                    sp.wait_ge(kept, CT + 1)
                    sp.dma_start(kvT[b, :, :], zT[:]).then_inc(stored, 16)
                    sp.wait_ge(stored, 16)

                @block.tensor
                def _(pe):
                    for t in range(CT):
                        r = P if t < CT - 1 else LAST
                        if t >= 4:
                            pe.wait_ge(kept, t - 3 + 1)
                        nc.tensor.transpose(g.bank[t % 4][0:CC, 0:r], z[0:r, t, :], g.ident[0:r, 0:r]).then_inc(turned, 1)

                @block.vector
                def _(dve):
                    nc.vector.memset(zT[CC:KA, :], 1.0).then_inc(kept, 1)
                    dve.wait_ge(in_, 32)
                    for t in range(CT):
                        r = P if t < CT - 1 else LAST
                        dve.wait_ge(turned, t + 1)
                        nc.vector.tensor_scalar(zT[0:CC, t * P:t * P + r], g.bank[t % 4][0:CC, 0:r], cols[:, 0:1], cols[:, 1:2],
                                                ALU.mult, ALU.add).then_inc(kept, 1)


class Global:
    pass


def build(nc, a, out, sublayers=8):
    with ExitStack() as es:
        def sb(name, shape):
            return es.enter_context(nc.sbuf_tensor(name, shape, F32))
        g = Global()
        g.bank = [es.enter_context(nc.psum_tensor(f"bank{i}", [P, 512], F32)) for i in range(8)]
        g.ident = sb("ident", [P, P])
        x = sb("x", [P, NT, C])
        xn = sb("xn", [P, NT, C])
        xnT = sb("xnT", [P, 1, B * T])
        wts = sb("wts", [P, NT, E])
        xv = lambda t: t.rearrange("b (a p) c -> p (b a) c", p=P)

        with stage(nc, "start", "in_", "made") as (block, in_, made):
            @block.sync
            def _(sp):
                sp.dma_start(x[:], xv(a["x"])).then_inc(in_, 16)
                sp.wait_ge(in_, 16)

            @block.gpsimd
            def _(pool):
                nc.gpsimd.memset(g.ident[:], 0.0).then_inc(made, 1)
                pool.wait_ge(made, 1)
                nc.gpsimd.affine_select(out=g.ident[:], in_=g.ident[:], compare_op=ALU.not_equal, fill=1.0, base=0,
                                        pattern=[[-1, P]], channel_multiplier=1).then_inc(made, 1)
                pool.wait_ge(made, 2)

        def normed(name):
            layernorm(nc, name + "_ln", x, xn)
            transpose_tokens(nc, name + "_xnT", g, xn, [(xnT, None, None)])

        def l0_attention():
            normed("l0a")
            with Space(nc, "l0a") as s:
                y = s("y", [P, NT, C])
                yT = s("yT", [P, 1, B * T])
                self_attention(nc, "l0self", g, a["l0_wq"], a["l0_wk"], a["l0_bq"], a["l0_bk"], a["L0_xattn_Wv"], a["L0_xattn_bv"],
                               xnT, xnT, y, C // H, (C // H) ** -0.5, True)
                cross_attention(nc, "l0cross", g, a["kvT"], a["l0_wcq"], a["l0_wckT"], a["l0_bcq"], a["l0_wcv"], xnT, y, H, C // H,
                                (C // H) ** -0.5, True)
                transpose_tokens(nc, "l0yT", g, y, [(yT, None, None)])
                linear(nc, "l0out", g, yT, 1, a["L0_xattn_Wp"], a["L0_xattn_bp"], x)

        def l0_ffn():
            normed("l0f")
            router(nc, "l0router", g, "mixer", xnT, a["l0_wr"], wts)
            experts(nc, "l0experts", g, xnT, a["l0_w1"], None, a["l0_w2"], wts, x, "silu", 2)

        def l1_attention():
            normed("l1a")
            cross_attention(nc, "l1cross", g, a["kvT"], a["l1_wq"], a["l1_wkT"], a["l1_bq"], a["l1_wv"], xnT, x, 1, C, 1.0, True)

        def l1_ffn():
            normed("l1f")
            router(nc, "l1router", g, "top2", xnT, a["L1_ffn_w_gate"], wts)
            expert_biases(nc, "l1bias", g, wts, a["L1_ffn_bu"], x)
            experts(nc, "l1experts", g, xnT, a["L1_ffn_Wd"], a["l1_b1"], a["L1_ffn_Wu"], wts, x, "relu", 1, 64)

        def mlp(name, s, r, pre):
            hT = s(name + "hT", [P, 4, B * T])
            layernorm(nc, name + "_ln3", r, xn)
            transpose_tokens(nc, name + "_ln3T", g, xn, [(xnT, a[pre + "ln3_g"], a[pre + "ln3_b"])])
            hidden(nc, name + "_h", g, xnT, a[pre + "li2_w"], a[pre + "li2_bT"], hT, 4)
            linear(nc, name + "_o", g, hT, 4, a[pre + "li3_w"], a[pre + "li3_b"], r)

        def l2_attention():
            W = H * 32
            with Space(nc, "l2a") as s:
                x1 = s("x1", [P, NT, C])
                r = s("r", [P, NT, C])
                layernorm(nc, "l2_ln0", x, xn)
                layernorm(nc, "l2_ln1", xn, x1, a["L2_xattn_ln1_g"], a["L2_xattn_ln1_b"])
                layernorm(nc, "l2_a1ln", x1, xn)
                with Space(nc, "l2a1") as s1:
                    kvn = s1("kvn", [P, 1, B * T])
                    y = s1("y", [P, NT, W])
                    transpose_tokens(nc, "l2_a1T", g, xn, [(xnT, a["L2_xattn_a1_lnx_g"], a["L2_xattn_a1_lnx_b"]),
                                                           (kvn, a["L2_xattn_a1_lny_g"], a["L2_xattn_a1_lny_b"])])
                    self_attention(nc, "l2self", g, a["L2_xattn_a1_wq"], a["L2_xattn_a1_wk"], None, None, a["l2_a1_wv"], None,
                                   xnT, kvn, y, 32, 32 ** -0.5, False)
                    after_attention("l2a1o", s1, x1, r, y, "L2_xattn_a1_")
                add_tokens(nc, "l2_add1", r, x1)
                layernorm(nc, "l2_ln2", r, x1, a["L2_xattn_ln2_g"], a["L2_xattn_ln2_b"])
                layernorm(nc, "l2_a2ln", x1, xn)
                transpose_tokens(nc, "l2_a2T", g, xn, [(xnT, a["L2_xattn_a2_lnx_g"], a["L2_xattn_a2_lnx_b"])])
                context_norm(nc, "l2ctx", g, a["ctx_512"], a["L2_xattn_a2_lny_g"], a["L2_xattn_a2_lny_b"], g.kvT2)
                with Space(nc, "l2a2") as s1:
                    y = s1("y", [P, NT, W])
                    cross_attention(nc, "l2cross", g, g.kvT2, a["L2_xattn_a2_wq"], a["l2_a2_wkT"], a["l2_bq0"], a["l2_a2_wv"],
                                    xnT, y, H, 32, 32 ** -0.5, False)
                    after_attention("l2a2o", s1, x1, r, y, "L2_xattn_a2_")
                add_tokens(nc, "l2_add2", x, x1)
                add_tokens(nc, "l2_add3", x, r)

        def after_attention(name, s, x1, r, y, pre):
            with Space(nc, name) as s2:
                yT = s2("yT", [P, 4, B * T])
                with stage(nc, name + "_copy", "copied") as (block, copied):
                    @block.vector
                    def _(dve):
                        nc.vector.tensor_copy(r[:], x1[:]).then_inc(copied, 1)
                        dve.wait_ge(copied, 1)
                transpose_tokens(nc, name + "_yT", g, y, [(yT, None, None)], width=512)
                linear(nc, name + "_lin", g, yT, 4, a[pre + "li1_w"], a[pre + "li1_b"], r)
            with Space(nc, name + "m") as s2:
                mlp(name, s2, r, pre)

        def l2_ffn():
            normed("l2f")
            router(nc, "l2router", g, "batch", xnT, a["L2_ffn_Wr"], wts, a["L2_ffn_br"])
            expert_biases(nc, "l2bias", g, wts, a["L2_ffn_b2"], xn)
            experts(nc, "l2experts", g, xnT, a["L2_ffn_W1"], a["l2_b1"], a["l2_w2"], wts, xn, "gelu", 4)
            with Space(nc, "l2f") as s:
                z = s("z", [P, NT, C])
                layernorm(nc, "l2f_out", xn, z, a["L2_ffn_gamma"], a["L2_ffn_beta"])
                add_tokens(nc, "l2f_add", x, z)

        def l3_attention():
            normed("l3a")
            with Space(nc, "l3a") as s:
                y = s("y", [P, NT, H * 64])
                cross_attention(nc, "l3cross", g, a["kvT"], a["l3_wq"], a["l3_wkT"], a["l3_bq0"], a["l3_wv"], xnT, y, H, 64,
                                64 ** -0.5, False)
                yT = s("yT", [P, 8, B * T])
                transpose_tokens(nc, "l3yT", g, y, [(yT, None, None)], width=H * 64)
                linear(nc, "l3out", g, yT, 8, a["L3_xattn_Wo"], a["L3_xattn_bo"], x)

        def l3_ffn():
            normed("l3f")
            expert_choice(nc, "l3router", g, xnT, a["l3_wr"], wts, int(2.0 * T / E))
            experts(nc, "l3experts", g, xnT, a["L3_ffn_w1"], None, a["l3_w2"], wts, x, "gelu", 4)

        g.kvT2 = nc.dram_tensor("kvT2", [B, KA, TC], F32).ap()
        for f in (l0_attention, l0_ffn, l1_attention, l1_ffn, l2_attention, l2_ffn, l3_attention, l3_ffn)[:sublayers]:
            f()

        with stage(nc, "end", "stored") as (block, stored):
            @block.sync
            def _(sp):
                sp.dma_start(xv(out), x[:]).then_inc(stored, 16)
                sp.wait_ge(stored, 16)


def layout(v, np):
    def f(n):
        return np.asarray(v[n], np.float32)

    def heads(w, D, pad=None):
        w = w.reshape(w.shape[0], -1, D).transpose(1, 0, 2)
        return np.pad(w, ((0, 0), (0, 0), (0, (pad or D) - D)))

    def col(b, D, pad=None):
        b = b.reshape(-1, D, 1)
        return np.pad(b, ((0, 0), (0, (pad or D) - D), (0, 0)))

    def keyT(w, b, D):
        n = w.shape[1] // D
        return np.concatenate([w.T.reshape(n, D, CC), b.reshape(n, D, 1)], 2)

    def value(w, b):
        return np.concatenate([w, b[None]], 0)

    def down(w, FP):
        return w.reshape(E, -1, FP, C).transpose(0, 2, 1, 3).reshape(E, FP, -1)

    zero = lambda n: np.zeros(n, np.float32)
    a = {n: f(n) for n in v if v[n] is not None}
    a["kvT"] = np.concatenate([f("ctx_512").transpose(0, 2, 1), np.ones((B, 1, TC), np.float32)], 1)
    D = C // H
    a["l0_wq"], a["l0_wk"] = heads(f("L0_xattn_Wq"), D, 32), heads(f("L0_xattn_Wk"), D, 32)
    a["l0_bq"], a["l0_bk"] = col(f("L0_xattn_bq"), D, 32), col(f("L0_xattn_bk"), D, 32)
    a["l0_wcq"], a["l0_bcq"] = heads(f("L0_xattn_Wcq"), D), col(f("L0_xattn_bcq"), D)
    a["l0_wckT"] = keyT(f("L0_xattn_Wck"), f("L0_xattn_bck"), D)
    a["l0_wcv"] = value(f("L0_xattn_Wcv"), f("L0_xattn_bcv"))
    a["l0_wr"] = f("L0_ffn_router_w").T
    a["l0_w1"] = np.concatenate([f("L0_ffn_w_gate").transpose(0, 2, 1), f("L0_ffn_w_up").transpose(0, 2, 1)], 2)
    a["l0_w2"] = down(f("L0_ffn_w_down").transpose(0, 2, 1), P)
    a["l1_wq"], a["l1_bq"] = heads(f("L1_xattn_Wq"), C), col(f("L1_xattn_bq"), C)
    a["l1_wkT"] = keyT(f("L1_xattn_Wk"), f("L1_xattn_bk"), C)
    a["l1_wv"] = value(f("L1_xattn_Wv"), f("L1_xattn_bv"))
    a["l1_b1"] = f("L1_ffn_bd").reshape(E, 64, 1)
    a["l2_a1_wv"] = f("L2_xattn_a1_wv").transpose(1, 0, 2).reshape(C, -1)
    a["l2_a2_wkT"] = np.concatenate([f("L2_xattn_a2_wk").transpose(0, 2, 1), zero((H, 32, 1))], 2)
    a["l2_bq0"] = zero((H, 32, 1))
    a["l2_a2_wv"] = value(f("L2_xattn_a2_wv").transpose(1, 0, 2).reshape(CC, -1), zero(H * 32))
    for p in ("L2_xattn_a1_", "L2_xattn_a2_"):
        a[p + "li2_bT"] = f(p + "li2_b").reshape(4, P).T
    a["l2_b1"] = f("L2_ffn_b1").reshape(E, 4, P).transpose(0, 2, 1)
    a["l2_w2"] = down(f("L2_ffn_W2"), P)
    a["l3_wq"], a["l3_bq0"] = heads(f("L3_xattn_Wq"), 64), zero((H, 64, 1))
    a["l3_wkT"] = keyT(f("L3_xattn_Wk"), zero(H * 64), 64)
    a["l3_wv"] = value(f("L3_xattn_Wv"), zero(H * 64))
    a["l3_wr"] = f("L3_ffn_gate_w").T
    a["l3_w2"] = down(f("L3_ffn_w2"), P)
    return {n: np.ascontiguousarray(w) for n, w in a.items()}


SUBLAYERS = 8


def kernel(**inputs):
    import numpy as np
    import concourse.bacc as bacc
    from concourse.bass_utils import run_bass_kernel_spmd

    nc = bacc.Bacc("TRN2", target_bir_lowering=False, num_devices=1)
    arrays = layout(inputs, np)
    a = {n: nc.dram_tensor(f"in_{n}", list(w.shape), F32, kind="ExternalInput").ap() for n, w in arrays.items()}
    out = nc.dram_tensor("out", [B, T, C], F32, kind="ExternalOutput").ap()
    build(nc, a, out, SUBLAYERS)
    r = run_bass_kernel_spmd(nc, [{f"in_{n}": w for n, w in arrays.items()}], core_ids=[0])
    return r.results[0]["out"]
```

```python
from contextlib import ExitStack, contextmanager

import concourse.bass as bass
from concourse import mybir

F32 = mybir.dt.float32
F32R = mybir.dt.float32r
ALU = mybir.AluOpType
ACT = mybir.ActivationFunctionType
AX = mybir.AxisListType

P = 128
B, T, C = 4, 256, 128
TC, CC = 1601, 64
KA = CC + 1
TCE = TC + 1
NT = B * T // P
QT = T // P
H = 16
E = 8
CT = -(-TC // P)
LAST = TC - (CT - 1) * P
EPS = 1e-5
LOWEST = -3.0e38


@contextmanager
def stage(nc, name, *signals):
    with ExitStack() as es:
        sems = [es.enter_context(nc.semaphore(f"{name}_{s}")) for s in signals]
        with nc.Block() as block:
            yield (block, *sems)
        for s in sems:
            nc.sync.sem_clear(s)
        nc.all_engine_barrier(sem_only=True)


class Link:

    def __init__(self, eng, sem, base=0):
        self.eng, self.sem, self.base, self.n = eng, sem, base, 0

    def __call__(self, ins):
        ins.then_inc(self.sem, 1)
        self.n += 1
        self.eng.wait_ge(self.sem, self.base + self.n)


class Space:

    def __init__(self, nc, name):
        self.nc, self.name, self.es = nc, name, ExitStack()

    def __enter__(self):
        return self

    def __exit__(self, *a):
        self.es.close()

    def __call__(self, name, shape, dt=F32):
        return self.es.enter_context(self.nc.sbuf_tensor(f"{self.name}_{name}", shape, dt))


def bcast(ap, shape):
    return ap.to_broadcast(shape)


def rows(dram, n=P):
    return dram.rearrange("(a n) -> a n", a=1).to_broadcast([n, dram.shape[0]])


def layernorm(nc, name, src, dst, gain=None, shift=None, tiles=NT, width=C, last=P):
    with Space(nc, name) as sb:
        stats = sb("stats", [P, tiles, 6])
        mv = sb("mv", [P, tiles, 2])
        std = sb("std", [P, tiles])
        rstd = sb("rstd", [P, tiles])
        gb = sb("gb", [P, 2, width]) if gain is not None else None
        parts = [(slice(0, tiles), P)] if last == P else [(slice(0, tiles - 1), P), (slice(tiles - 1, tiles), last)]
        with stage(nc, name, "moments", "std", "step", "affine_in") as (block, moments, std_done, step, affine_in):
            @block.sync
            def _(sp):
                if gain is not None:
                    sp.dma_start(gb[:, 0, :], rows(gain)).then_inc(affine_in, 16)
                    sp.dma_start(gb[:, 1, :], rows(shift)).then_inc(affine_in, 16)

            @block.vector
            def _(dve):
                link = Link(dve, step)
                for n in range(tiles):
                    r = P if n < tiles - 1 else last
                    link(nc.vector.bn_stats(stats[0:r, n, :], src[0:r, n, :]))
                    link(nc.vector.bn_aggr(mv[0:r, n, :], stats[0:r, n, :]))
                for s, r in parts:
                    nc.vector.tensor_scalar(rstd[0:r, s], mv[0:r, s, 1], EPS, None, ALU.add).then_inc(moments, 1)
                dve.wait_ge(std_done, len(parts))
                for s, r in parts:
                    link(nc.vector.reciprocal(rstd[0:r, s], std[0:r, s]))
                for n in range(tiles):
                    r = P if n < tiles - 1 else last
                    link(nc.vector.tensor_scalar(dst[0:r, n, :], src[0:r, n, :], mv[0:r, n, 0:1],
                                                 rstd[0:r, n:n + 1], ALU.subtract, ALU.mult))
                if gain is not None:
                    dve.wait_ge(affine_in, 32)
                    link(nc.vector.tensor_tensor(dst[:], dst[:], gb[:, 0:1, :].to_broadcast([P, tiles, width]), ALU.mult))
                    link(nc.vector.tensor_tensor(dst[:], dst[:], gb[:, 1:2, :].to_broadcast([P, tiles, width]), ALU.add))

            @block.scalar
            def _(act):
                act.wait_ge(moments, len(parts))
                for s, r in parts:
                    nc.scalar.activation(std[0:r, s], rstd[0:r, s], ACT.Sqrt).then_inc(std_done, 1)


def transpose_tokens(nc, name, g, src, outs, width=C):
    kc = width // P
    with Space(nc, name) as sb:
        cols = sb("cols", [P, 2 * len(outs)])
        with stage(nc, name, "turned", "kept", "cols_in") as (block, turned, kept, cols_in):
            n_cols = sum(gain is not None for _, gain, _ in outs)

            @block.sync
            def _(sp):
                for k, (_, gain, shift) in enumerate(outs):
                    if gain is not None:
                        sp.dma_start(cols[:, 2 * k:2 * k + 1], gain.rearrange("(n a) -> n a", a=1)).then_inc(cols_in, 16)
                        sp.dma_start(cols[:, 2 * k + 1:2 * k + 2], shift.rearrange("(n a) -> n a", a=1)).then_inc(cols_in, 16)

            @block.tensor
            def _(pe):
                for i in range(kc * 2):
                    c, half = i // 2, i % 2
                    if i >= 2:
                        pe.wait_ge(kept, i - 1)
                    for n in range(4):
                        mm = nc.tensor.transpose(g.bank[i % 2][:, n * P:(n + 1) * P],
                                                 src[:, half * 4 + n, c * P:(c + 1) * P], g.ident[:])
                    mm.then_inc(turned, 1)

            @block.vector
            def _(dve):
                if n_cols:
                    dve.wait_ge(cols_in, 32 * n_cols)
                for i in range(kc * 2):
                    c, half = i // 2, i % 2
                    dve.wait_ge(turned, i + 1)
                    for k, (dst, gain, _) in enumerate(outs):
                        o = dst[:, c, half * 512:half * 512 + 512]
                        if gain is None:
                            ins = nc.vector.tensor_copy(o, g.bank[i % 2][:])
                        else:
                            ins = nc.vector.tensor_scalar(o, g.bank[i % 2][:], cols[:, 2 * k:2 * k + 1],
                                                          cols[:, 2 * k + 1:2 * k + 2], ALU.mult, ALU.add)
                    ins.then_inc(kept, 1)


class Context:

    def __init__(self, sb):
        self.hi_lo = sb("hi_lo", [P, B, TCE], F32R)
        self.hi_one = sb("hi_one", [KA, B, TCE], F32R)


def split_context(nc, name, ctx, cT):
    with Space(nc, name) as sb:
        c = [sb(f"c{s}", [CC, TCE]) for s in range(2)]
        with stage(nc, name, "in_0", "in_1", "widened", "hi_done", "lo_done", "one_set") as (
                block, in_0, in_1, widened, hi_done, lo_done, one_set):
            in_ = [in_0, in_1]

            @block.sync
            def _(sp):
                for b in range(B):
                    if b >= 2:
                        sp.wait_ge(lo_done, b - 1)
                        sp.wait_ge(hi_done, 2 * (b - 1))
                    sp.dma_start(c[b % 2][:, 0:TC], cT[b, :, :]).then_inc(in_[b % 2], 16)

            @block.scalar
            def _(act):
                for b in range(B):
                    act.wait_ge(widened, b + 1)
                    nc.scalar.copy(ctx.hi_lo[0:CC, b, :], c[b % 2][:]).then_inc(hi_done, 1)
                    nc.scalar.copy(ctx.hi_one[0:CC, b, :], c[b % 2][:]).then_inc(hi_done, 1)

            @block.vector
            def _(dve):
                nc.vector.memset(ctx.hi_one[CC:KA, :, :].bitcast(F32), 1.0).then_inc(one_set, 1)
                dve.wait_ge(one_set, 1)
                for b in range(B):
                    dve.wait_ge(in_[b % 2], 16 * (b // 2 + 1))
                    nc.vector.tensor_copy(c[b % 2][:, TC:TCE], c[b % 2][:, TC - 1:TC]).then_inc(widened, 1)
                    dve.wait_ge(hi_done, 2 * b + 1)
                    dve.wait_ge(widened, b + 1)
                    nc.vector.tensor_tensor(ctx.hi_lo[CC:2 * CC, b, :], c[b % 2][:], ctx.hi_lo[0:CC, b, :].bitcast(F32),
                                            ALU.subtract).then_inc(lo_done, 1)
                dve.wait_ge(lo_done, B)


def project_values(nc, name, g, ctx, wv, heads, D, V):
    D1 = D + 1
    U = min(heads, 8)
    N = U * D
    NU = heads // U
    with Space(nc, name) as sb:
        w = sb("w", [CC, heads * D])
        w_hi = sb("w_hi", [P, heads * D], F32R)
        w_lo = sb("w_lo", [CC, heads * D], F32R)
        out = [sb(f"out{s}", [P, U, CT, D1]) for s in range(2)]
        with stage(nc, name, "w_in", "w_split", "ones_set", "v_mm", "v_act", "v_dve", "stored0", "stored1") as (
                block, w_in, w_split, ones_set, v_mm, v_act, v_dve, stored0, stored1):
            stored = [stored0, stored1]

            @block.sync
            def _(sp):
                sp.dma_start(w[:], wv).then_inc(w_in, 16)
                for n in range(B * NU):
                    b, c = n // NU, n % NU
                    sp.wait_ge(v_act, 7 * (n + 1))
                    sp.wait_ge(v_dve, 6 * (n + 1))
                    sp.dma_start(V[b, c * U:(c + 1) * U, :, :].rearrange("h p x -> p h x"),
                                 out[n % 2][:].rearrange("p h t d -> p h (t d)")).then_inc(stored[n % 2], 16)
                for s in range(2):
                    sp.wait_ge(stored[s], 16 * (B * NU // 2))

            @block.tensor
            def _(pe):
                pe.wait_ge(w_split, 3)
                for n in range(B * NU):
                    b, c = n // NU, n % NU
                    for t in range(CT):
                        r = P if t < CT - 1 else LAST
                        m = n * CT + t
                        if m >= 4:
                            k = m - 4
                            tk, nk = k % CT, k // CT
                            pe.wait_ge((v_act, v_dve)[tk % 2], (7, 6)[tk % 2] * nk + tk // 2 + 1)
                        o = g.bank[m % 4][0:r, 0:N]
                        cols = slice(c * N, (c + 1) * N)
                        nc.tensor.matmul(o, ctx.hi_lo[:, b, t * P:t * P + r], w_hi[:, cols], start=True, stop=False)
                        nc.tensor.matmul(o, ctx.hi_one[0:CC, b, t * P:t * P + r], w_lo[:, cols],
                                         start=False, stop=True).then_inc(v_mm, 1)

            def keep(eng, parity, copy, done):
                for n in range(B * NU):
                    if n >= 2:
                        eng.wait_ge(stored[n % 2], 16 * (n // 2))
                    for t in range(parity, CT, 2):
                        r = P if t < CT - 1 else LAST
                        m = n * CT + t
                        eng.wait_ge(v_mm, m + 1)
                        copy(out[n % 2][0:r, :, t, 0:D], g.bank[m % 4][0:r, 0:N].rearrange("p (h d) -> p h d", d=D)).then_inc(done, 1)

            @block.scalar
            def _(act):
                act.wait_ge(w_in, 16)
                nc.scalar.copy(w_hi[0:CC, :], w[:]).then_inc(w_split, 1)
                nc.scalar.copy(w_hi[CC:2 * CC, :], w[:]).then_inc(w_split, 1)
                act.wait_ge(ones_set, 2)
                keep(act, 0, nc.scalar.copy, v_act)

            @block.vector
            def _(dve):
                for s in range(2):
                    nc.vector.memset(out[s][:], 1.0).then_inc(ones_set, 1)
                dve.wait_ge(w_split, 2)
                nc.vector.tensor_tensor(w_lo[:], w[:], w_hi[0:CC, :].bitcast(F32), ALU.subtract).then_inc(w_split, 1)
                dve.wait_ge(ones_set, 2)
                keep(dve, 1, nc.vector.tensor_copy, v_dve)


class Head:

    def __init__(self, b, h, i, turn, u):
        self.b, self.h, self.i, self.turn, self.u = b, h, i, turn, u


def run_heads(eng, heads, step):
    def fixed(b, c):
        def at(d):
            i = b * heads + c + d
            return Head(i // heads, i % heads, i, i // 2, i % 2) if 0 <= i < B * heads else None
        return at

    def looped(b, k, c):
        def at(d):
            return Head(b, k * 2 + c + d, k * 2 + b * heads + c + d, k + (b * heads + c + d) // 2, (c + d) % 2)
        return at

    step(fixed(0, -1))
    for b in range(B):
        for c in range(min(heads, 2)):
            step(fixed(b, c))
        if heads > 2:
            with eng.Fori(0, (heads - 4) // 2) as k:
                step(looped(b, k, 2))
                step(looped(b, k, 3))
            step(fixed(b, heads - 2))
            step(fixed(b, heads - 1))
    for c in range(2):
        step(fixed(B, c))


def after(eng, sem, n):
    if not isinstance(n, int) or n > 0:
        eng.wait_ge(sem, n)


def cross_attention(nc, name, g, ctx, wq, wkT, bq, V, normT, y, heads, D, scale, add, key_bias, bv=None):
    D1 = D + 1
    DM = min(D1, P)
    KR = CC + 1 if key_bias else CC
    NG = (CT + 1) // 2
    CW = [402, 400, 400, 400]
    C0 = [0, 402, 802, 1202]
    NJ = QT * len(CW)
    NW = 32 if bq is None else 48
    with Space(nc, name) as sb:
        wqs = [sb(f"wq{s}", [C, D]) for s in range(2)]
        wks = [sb(f"wk{s}", [D, KA]) for s in range(2)]
        bqs = [sb(f"bq{s}", [D, 1]) for s in range(2)]
        bvs = sb("bv", [P, heads * D]) if bv is not None else None
        Vs = [sb(f"V{s}", [P, CT, D1]) for s in range(2)]
        qT = [sb(f"qT{s}", [D, T]) for s in range(2)]
        q_hi = [sb(f"q_hi{s}", [P, T], F32R) for s in range(2)]
        q_lo = [sb(f"q_lo{s}", [KA, T], F32R) for s in range(2)]
        top = sb("top", [KA, T]) if key_bias else None
        mx = [sb(f"mx{s}", [P, NJ]) for s in range(2)]
        negm = [sb(f"negm{s}", [P, QT]) for s in range(2)]
        PT = [sb(f"PT{s}", [P, CT, T]) for s in range(2)]
        oT = [sb(f"oT{s}", [DM, T]) for s in range(2)]
        lT = [sb(f"lT{s}", [1, T]) for s in range(2)] if D1 > P else None
        rl = [sb(f"rl{s}", [P, QT]) for s in range(2)]
        p_q, p_qk = g.bank[0][:, 0:T], g.bank[0][:, T:2 * T]
        p_m = g.bank[0][CC:KA, 0:T]
        p_s, p_st = [g.bank[2], g.bank[3]], [g.bank[4], g.bank[5]]
        p_oT = [g.bank[6 + s][0:DM, 0:T] for s in range(2)]
        p_l = [g.bank[6 + s][0:1, T:2 * T] for s in range(2)]
        p_o = g.bank[1][:, 0:QT * D1].rearrange("p (a d) -> p a d", d=D1)
        names = ["w_in0", "w_in1", "v_in0", "v_in1", "bv_in", "waits_taken", "q_mm", "q_sb", "qk_mm", "q_hi_done", "q_lo_done",
                 "s_mm", "max_done", "negm_done", "m_mm", "top_done", "m_done", "st_mm", "exp_done", "pv_mm", "o_sb",
                 "turned", "recip_done", "y_done"]
        with stage(nc, name, *names) as (
                block, w_in0, w_in1, v_in0, v_in1, bv_in, waits_taken, q_mm, q_sb, qk_mm, q_hi_done, q_lo_done, s_mm,
                max_done, negm_done, m_mm, top_done, m_done, st_mm, exp_done, pv_mm, o_sb, turned, recip_done, y_done):
            w_in, v_in = [w_in0, w_in1], [v_in0, v_in1]

            @block.sync
            def _(sp):
                if bv is not None:
                    sp.dma_start(bvs[:], rows(bv)).then_inc(bv_in, 16)

                def step(at):
                    f = at(1)
                    if not f:
                        return
                    h = bass.ds(f.h, 1)
                    after(sp, qk_mm, f.i - 1)
                    sp.dma_start(wqs[f.u][:], wq[h, :, :].rearrange("a k t -> (a k) t")).then_inc(w_in[f.u], 16)
                    sp.dma_start(wks[f.u][:], wkT[h, :, :].rearrange("a k t -> (a k) t")).then_inc(w_in[f.u], 16)
                    if bq is not None:
                        sp.dma_start(bqs[f.u][:], bq[h, :, :].rearrange("a k t -> (a k) t")).then_inc(w_in[f.u], 16)
                    after(sp, pv_mm, f.i - 1)
                    sp.dma_start(Vs[f.u][:].rearrange("p t d -> p (t d)"), V[f.b, h, :, :].rearrange("h p x -> (h p) x"))\
                        .then_inc(v_in[f.u], 16)
                run_heads(sp, heads, step)

            @block.tensor
            def _(pe):
                def step(at):
                    f, m, v, o = at(1), at(0), at(-1), at(-2)

                    def scores(j):
                        a, c = j // len(CW), j % len(CW)
                        after(pe, max_done, f.i * NJ + j - 1)
                        nc.tensor.matmul(p_s[j % 2][:, 0:CW[c]], q_hi[f.u][:, a * P:(a + 1) * P],
                                         ctx.hi_lo[:, f.b, C0[c]:C0[c] + CW[c]], start=True, stop=True).then_inc(s_mm, 1)

                    def scores_t(n):
                        if n == 0:
                            pe.wait_ge(m_done, m.i + 1)
                        after(pe, exp_done, m.i * NG + (n - 1 if n >= 2 else -n))
                        for t in range(2 * n, min(2 * n + 2, CT)):
                            r = P if t < CT - 1 else LAST
                            out = p_st[n % 2][0:r, (t % 2) * T:(t % 2 + 1) * T]
                            nc.tensor.matmul(out, ctx.hi_lo[:, m.b, t * P:t * P + r], q_hi[m.u][:], start=True, stop=False)
                            mm = nc.tensor.matmul(out, ctx.hi_one[:, m.b, t * P:t * P + r], q_lo[m.u][:], start=False, stop=True)
                        mm.then_inc(st_mm, 1)

                    def values(t):
                        if t == 0:
                            pe.wait_ge(v_in[v.u], v.turn * 16 + 16)
                            after(pe, o_sb, v.i - 1)
                        if t % 2 == 0:
                            pe.wait_ge(exp_done, v.i * NG + t // 2 + 1)
                        r = P if t < CT - 1 else LAST
                        mm = nc.tensor.matmul(p_oT[v.u], Vs[v.u][0:r, t, 0:DM], PT[v.u][0:r, t, :],
                                              start=(t == 0), stop=(t == CT - 1), skip_group_check=True)
                        if D1 > P:
                            mm = nc.tensor.matmul(p_l[v.u], Vs[v.u][0:r, t, D:D1], PT[v.u][0:r, t, :],
                                                  start=False, stop=(t == CT - 1), skip_group_check=True)
                        if t == CT - 1:
                            mm.then_inc(pv_mm, 1)

                    if m:
                        scores_t(0)
                    if f:
                        pe.wait_ge(w_in[f.u], f.turn * NW + NW)
                        after(pe, q_sb, f.i)
                        pe.sem_inc(waits_taken, 1)
                        nc.tensor.matmul(p_q[0:D, :], wqs[f.u][:], normT[:, 0, f.b * T:(f.b + 1) * T],
                                         start=True, stop=True).then_inc(q_mm, 1)
                    if v:
                        values(0)
                    if m:
                        scores_t(1)
                    if f:
                        pe.wait_ge(q_sb, f.i + 1)
                        after(pe, q_lo_done, f.i)
                        after(pe, m_done, f.i)
                        pe.sem_inc(waits_taken, 1)
                        nc.tensor.matmul(p_qk[0:KR, :], wks[f.u][:, 0:KR], qT[f.u][:], start=True, stop=True).then_inc(qk_mm, 1)
                    if v:
                        values(1)
                        values(2)
                    if o:
                        pe.wait_ge(o_sb, o.i + 1)
                        after(pe, y_done, o.i)
                        pe.sem_inc(waits_taken, 1)
                        for a in range(QT):
                            mm = nc.tensor.transpose(p_o[:, a, 0:DM], oT[o.u][:, a * P:(a + 1) * P], g.ident[0:DM, 0:DM])
                            if D1 > P:
                                mm = nc.tensor.transpose(p_o[:, a, D:D1], lT[o.u][:, a * P:(a + 1) * P], g.ident[0:1, 0:1])
                        mm.then_inc(turned, 1)
                    if f:
                        pe.wait_ge(q_hi_done, 2 * f.i + 2)
                    for j in range(NJ):
                        if f:
                            scores(j)
                        if m and j + 2 < NG:
                            scores_t(j + 2)
                        if v:
                            values(3 + j)
                    if f:
                        pe.wait_ge(negm_done, f.i + 1)
                        for a in range(QT):
                            mm = nc.tensor.matmul(p_m[:, a * P:(a + 1) * P], negm[f.u][:, a:a + 1], g.ident[:], start=True, stop=True)
                        mm.then_inc(m_mm, 1)
                    if v:
                        values(11)
                        values(12)
                run_heads(pe, heads, step)

            @block.scalar
            def _(act):
                def step(at):
                    f, m = at(1), at(0)

                    def exps(n):
                        act.wait_ge(st_mm, m.i * NG + n + 1)
                        k = min(2, CT - 2 * n)
                        r = P if k == 2 else LAST
                        nc.scalar.activation(PT[m.u][0:r, 2 * n:2 * n + k, :].rearrange("p t q -> p (t q)"),
                                             p_st[n % 2][0:r, 0:k * T], ACT.Exp, scale=scale).then_inc(exp_done, 1)
                    if m:
                        after(act, pv_mm, m.i - 1)
                        exps(0)
                        exps(1)
                    if f:
                        act.wait_ge(qk_mm, f.i + 1)
                        after(act, st_mm, (f.i - 1) * NG)
                        for s in range(2):
                            nc.scalar.copy(q_hi[f.u][s * CC:(s + 1) * CC, :], p_qk[0:CC, :]).then_inc(q_hi_done, 1)
                    if m:
                        for n in range(2, NG):
                            exps(n)
                run_heads(act, heads, step)

            @block.vector
            def _(dve):
                def step(at):
                    f, v, o = at(1), at(-1), at(-2)
                    if f:
                        dve.wait_ge(q_mm, f.i + 1)
                        if bq is not None:
                            nc.vector.tensor_scalar(qT[f.u][:], p_q[0:D, :], bqs[f.u][:, 0:1], None, ALU.add).then_inc(q_sb, 1)
                        else:
                            nc.vector.tensor_copy(qT[f.u][:], p_q[0:D, :]).then_inc(q_sb, 1)
                        dve.wait_ge(q_hi_done, 2 * f.i + 2)
                        nc.vector.tensor_tensor(q_lo[f.u][0:CC, :], p_qk[0:CC, :], q_hi[f.u][0:CC, :].bitcast(F32),
                                                ALU.subtract).then_inc(q_lo_done, 1)
                    if o:
                        dve.wait_ge(turned, o.i + 1)
                        nc.vector.reciprocal(rl[o.u][:], p_o[:, :, D]).then_inc(recip_done, 1)
                        dve.wait_ge(recip_done, o.i + 1)
                        for a in range(QT):
                            dst = y[:, o.b * QT + a, bass.ds(o.h * D, D)]
                            if add:
                                ins = nc.vector.scalar_tensor_tensor(out=dst, in0=p_o[:, a, 0:D], scalar=rl[o.u][:, a:a + 1],
                                                                     in1=dst, op0=ALU.mult, op1=ALU.add)
                            else:
                                ins = nc.vector.tensor_scalar(dst, p_o[:, a, 0:D], rl[o.u][:, a:a + 1], None, ALU.mult)
                        ins.then_inc(y_done, 1)
                    if f:
                        for j in range(NJ):
                            dve.wait_ge(s_mm, f.i * NJ + j + 1)
                            nc.vector.tensor_reduce(mx[f.u][:, j:j + 1], p_s[j % 2][:, 0:CW[j % len(CW)]], AX.X,
                                                    ALU.max).then_inc(max_done, 1)
                        dve.wait_ge(max_done, f.i * NJ + NJ)
                        nc.vector.tensor_reduce(negm[f.u][:], mx[f.u][:].rearrange("p (a c) -> p a c", a=QT), AX.X,
                                                ALU.max, negate=True).then_inc(negm_done, 1)
                        dve.wait_ge(m_mm, f.i + 1)
                        row = q_lo[f.u][CC:KA, :]
                        if key_bias:
                            nc.vector.tensor_copy(top[CC:KA, :], p_qk[CC:KA, :]).then_inc(top_done, 1)
                            dve.wait_ge(top_done, 2 * f.i + 1)
                            nc.vector.tensor_tensor(top[CC:KA, :], p_m, top[CC:KA, :], ALU.subtract).then_inc(top_done, 1)
                            dve.wait_ge(top_done, 2 * f.i + 2)
                            nc.vector.tensor_tensor(row, top[CC:KA, :], p_qk[CC:KA, :], ALU.add).then_inc(m_done, 1)
                        else:
                            nc.vector.tensor_copy(row, p_m).then_inc(m_done, 1)
                    if v:
                        dve.wait_ge(pv_mm, v.i + 1)
                        after(dve, turned, v.i - 1)
                        if D1 > P:
                            nc.vector.tensor_copy(lT[v.u][:], p_l[v.u])
                        nc.vector.tensor_copy(oT[v.u][:], p_oT[v.u]).then_inc(o_sb, 1)
                run_heads(dve, heads, step)
                if bv is not None:
                    dve.wait_ge(bv_in, 16)
                    dve.wait_ge(y_done, B * heads)
                    nc.vector.tensor_tensor(y[:], y[:], bvs[:].rearrange("p (a c) -> p a c", a=1).to_broadcast([P, NT, heads * D]),
                                            ALU.add).then_inc(y_done, 1)
                    dve.wait_ge(y_done, B * heads + 1)


def self_attention(nc, name, g, wq, wk, bq, bk, wv, bv, qsrcT, kvsrcT, y, D, scale, causal):
    D1 = D + 1
    DP = 32
    KM = DP + 1
    NHEAD = 64 if bq is not None else 32
    with Space(nc, name) as sb:
        wvs = sb("wv", [C, H * D])
        bvs = sb("bv", [P, H * D]) if bv is not None else None
        V = sb("V", [P, NT, H, D1])
        ones = sb("ones", [P, 1])
        mask = sb("mask", [P, QT, T]) if causal else None
        sm = sb("masked", [P, QT, T]) if causal else None
        wqs = [sb(f"wq{s}", [C, DP]) for s in range(2)]
        wks = [sb(f"wk{s}", [C, DP]) for s in range(2)]
        bs = [sb(f"b{s}", [DP, 2]) for s in range(2)] if bq is not None else None
        qT = [sb(f"qT{s}", [KM, T]) for s in range(2)]
        kT = [sb(f"kT{s}", [KM, T]) for s in range(2)]
        negm = [sb(f"negm{s}", [P, QT]) for s in range(2)]
        PT = [sb(f"PT{s}", [P, QT, T]) for s in range(2)]
        PD = [sb(f"PD{s}", [P, QT, P]) for s in range(2)]
        rl = [sb(f"rl{s}", [P, QT]) for s in range(2)]
        p_qk, p_m = g.bank[0], g.bank[1]
        p_s, p_st, p_o = [g.bank[2], g.bank[3]], [g.bank[4], g.bank[5]], [g.bank[6], g.bank[7]]
        names = ["wv_in", "head_in0", "head_in1", "consts", "select_begun", "v_mm", "v_sb", "qk_mm", "qk_sb", "s_mm", "masked", "s_read",
                 "negm_done", "m_mm", "q_final", "st_mm", "exp_done", "diag_done", "pv_mm", "recip_done", "out_free", "head_begun"]
        with stage(nc, name, *names) as (
                block, wv_in, head_in0, head_in1, consts, select_begun, v_mm, v_sb, qk_mm, qk_sb, s_mm, masked, s_read, negm_done,
                m_mm, q_final, st_mm, exp_done, diag_done, pv_mm, recip_done, out_free, head_begun):
            head_in = [head_in0, head_in1]

            def pipeline(eng, step):
                step(-1, 1, 0)
                step(0, 0, 0)
                with eng.Fori(0, (H - 2) // 2) as k:
                    step(k * 2 + 1, 1, k + 1, True)
                    step(k * 2 + 2, 0, k + 1, True)
                step(H - 1, 1, H // 2)
                step(H, 0, (H + 1) // 2)

            def fronts(h, inner):
                return inner or h + 1 < H

            def mids(h, inner):
                return inner or 0 <= h < H

            def backs(h, inner):
                return inner or 1 <= h

            @block.sync
            def _(sp):
                sp.dma_start(wvs[:], wv).then_inc(wv_in, 16)
                if bv is not None:
                    sp.dma_start(bvs[:], rows(bv)).then_inc(wv_in, 16)
                with sp.Fori(0, B) as b:
                    def load(h, u):
                        i = b * H + h
                        if isinstance(h, int) and h < 2:
                            sp.wait_ge(qk_sb, b * H)
                        else:
                            sp.wait_ge(qk_sb, i - 1)
                        sp.dma_start(wqs[u][:], wq[bass.ds(h, 1), :, :].rearrange("a k t -> (a k) t")).then_inc(head_in[u], 16)
                        sp.dma_start(wks[u][:], wk[bass.ds(h, 1), :, :].rearrange("a k t -> (a k) t")).then_inc(head_in[u], 16)
                        if bq is not None:
                            sp.dma_start(bs[u][:, 0:1], bq[bass.ds(h, 1), :, :].rearrange("a k t -> (a k) t")).then_inc(head_in[u], 16)
                            sp.dma_start(bs[u][:, 1:2], bk[bass.ds(h, 1), :, :].rearrange("a k t -> (a k) t")).then_inc(head_in[u], 16)
                    load(0, 0)
                    load(1, 1)
                    with sp.Fori(0, (H - 2) // 2) as k:
                        load(k * 2 + 2, 0)
                        load(k * 2 + 3, 1)

            @block.gpsimd
            def _(pool):
                if causal:
                    nc.gpsimd.memset(mask[:], 0.0).then_inc(masked, 1)
                    pool.wait_ge(masked, 1)
                    nc.gpsimd.affine_select(out=mask[:], in_=mask[:], compare_op=ALU.is_ge, fill=LOWEST, base=0,
                                            pattern=[[P, QT], [-1, T]], channel_multiplier=1).then_inc(consts, 1)
                with pool.Fori(0, B) as b:
                    def step(h, u, pair, inner=False):
                        if not mids(h, inner):
                            return
                        i = b * H + h
                        pool.wait_ge(exp_done, i + 1)
                        if inner or h >= 2:
                            pool.wait_ge(pv_mm, i - 1)
                        pool.sem_inc(select_begun, 1)
                        for a in range(QT):
                            ins = nc.gpsimd.affine_select(out=PD[u][:, a, :], in_=PT[u][:, a, a * P:(a + 1) * P],
                                                          compare_op=ALU.is_ge if causal else ALU.is_gt, fill=0.0, base=0,
                                                          pattern=[[1 if causal else -1, P]],
                                                          channel_multiplier=-1 if causal else 1)
                        ins.then_inc(diag_done, 1)
                    pipeline(pool, step)

            @block.tensor
            def _(pe):
                pe.wait_ge(wv_in, 16 if bv is None else 32)
                for n in range(NT):
                    if n >= 2:
                        pe.wait_ge(v_sb, n - 1)
                    nc.tensor.matmul(p_s[n % 2][:, 0:H * D], kvsrcT[:, 0, n * P:(n + 1) * P], wvs[:],
                                     start=True, stop=True).then_inc(v_mm, 1)
                pe.wait_ge(v_sb, NT)
                pe.wait_ge(consts, 4 if causal else 3)
                with pe.Fori(0, B) as b:
                    def step(h, u, pair, inner=False):
                        i = b * H + h
                        sf, f = (u + 1) % 2, i + 1
                        front, mid, back = fronts(h, inner), mids(h, inner), backs(h, inner)
                        if front:
                            pe.wait_ge(head_in[sf], (b * (H // 2) + pair + 1) * NHEAD)
                            pe.wait_ge(qk_sb, f if inner or h >= 0 else b * H)
                            pe.sem_inc(head_begun, 1)
                            nc.tensor.matmul(p_qk[0:DP, 0:T], wqs[sf][:], qsrcT[:, 0, bass.ds(b * T, T)], start=True, stop=True)
                            nc.tensor.matmul(p_qk[0:DP, T:2 * T], wks[sf][:], kvsrcT[:, 0, bass.ds(b * T, T)],
                                             start=True, stop=True).then_inc(qk_mm, 1)
                        if mid:
                            pe.wait_ge(q_final, i + 1)
                            if inner or h >= 2:
                                pe.wait_ge(exp_done, i - 1)
                            for t in range(QT):
                                q0 = t * P if causal else 0
                                mm = nc.tensor.matmul(p_st[u][:, t * T + q0:(t + 1) * T], kT[u][:, t * P:(t + 1) * P],
                                                      qT[u][:, q0:T], start=True, stop=True)
                            mm.then_inc(st_mm, 1)
                        if front:
                            pe.wait_ge(qk_sb, f + 1)
                            if inner or h >= 1:
                                pe.wait_ge(s_read, f - 1)
                            for a in range(QT):
                                mm = nc.tensor.matmul(p_s[sf][:, a * T:(a + 1) * T], qT[sf][0:DP, a * P:(a + 1) * P],
                                                      kT[sf][0:DP, :], start=True, stop=True)
                            mm.then_inc(s_mm, 1)
                        if back:
                            k, hk = i - 1, h - 1
                            pe.wait_ge(diag_done, k + 1)
                            pe.wait_ge(exp_done, k + 1)
                            pe.wait_ge(out_free, k + 1)

                            def block_(a, lhsT, t, first=False, last=False):
                                w = D1 if causal else D
                                return nc.tensor.matmul(p_o[sf][:, a * D1:a * D1 + w], lhsT,
                                                        V[:, bass.ds(b * QT + t, 1), bass.ds(hk, 1), 0:w].rearrange("p a h d -> p (a h d)"),
                                                        start=first, stop=last, skip_group_check=True)
                            if causal:
                                block_(0, PD[sf][:, 0, :], 0, first=True, last=True)
                                block_(1, PT[sf][:, 0, P:T], 0)
                                mm = block_(1, PD[sf][:, 1, :], 1, last=True)
                            else:
                                block_(0, PD[sf][:, 0, :], 0, first=True)
                                block_(0, PT[sf][:, 1, 0:P], 1, last=True)
                                block_(1, PD[sf][:, 1, :], 1, last=True)
                                for a in range(QT):
                                    for t in range(QT):
                                        mm = nc.tensor.matmul(p_o[sf][:, a * D1 + D:(a + 1) * D1], PT[sf][:, t, a * P:(a + 1) * P],
                                                              ones[:], start=False, stop=(t == QT - 1), skip_group_check=True)
                            mm.then_inc(pv_mm, 1)
                        if front:
                            pe.wait_ge(negm_done, f + 1)
                            for a in range(QT):
                                mm = nc.tensor.matmul(p_m[DP:KM, a * P:(a + 1) * P], negm[sf][:, a:a + 1], g.ident[:],
                                                      start=True, stop=True)
                            mm.then_inc(m_mm, 1)
                    pipeline(pe, step)

            @block.scalar
            def _(act):
                with act.Fori(0, B) as b:
                    def step(h, u, pair, inner=False):
                        i = b * H + h
                        if not mids(h, inner):
                            return
                        if inner or h >= 2:
                            act.wait_ge(pv_mm, i - 1)
                        act.wait_ge(st_mm, i + 1)
                        if causal:
                            nc.scalar.activation(PT[u][:, 0, :], p_st[u][:, 0:T], ACT.Exp, scale=scale)
                            ins = nc.scalar.activation(PT[u][:, 1, P:T], p_st[u][:, T + P:2 * T], ACT.Exp, scale=scale)
                        else:
                            ins = nc.scalar.activation(PT[u][:].rearrange("p t q -> p (t q)"), p_st[u][:], ACT.Exp, scale=scale)
                        ins.then_inc(exp_done, 1)
                    pipeline(act, step)

            @block.vector
            def _(dve):
                for s in range(2):
                    nc.vector.memset(kT[s][DP:KM, :], 1.0).then_inc(consts, 1)
                nc.vector.memset(V[:, :, :, D:D1], 1.0)
                nc.vector.memset(ones[:], 1.0).then_inc(consts, 1)
                dve.sem_inc(out_free, 2)
                dve.wait_ge(consts, 4 if causal else 3)
                dve.wait_ge(wv_in, 16 if bv is None else 32)
                for n in range(NT):
                    dve.wait_ge(v_mm, n + 1)
                    o = V[:, n, :, 0:D]
                    i_ = p_s[n % 2][:, 0:H * D].rearrange("p (h d) -> p h d", d=D)
                    if bv is None:
                        nc.vector.tensor_copy(o, i_).then_inc(v_sb, 1)
                    else:
                        nc.vector.tensor_tensor(o, i_, bvs[:].rearrange("p (h d) -> p h d", d=D), ALU.add).then_inc(v_sb, 1)
                with dve.Fori(0, B) as b:
                    def step(h, u, pair, inner=False):
                        i = b * H + h
                        sf, f = (u + 1) % 2, i + 1
                        if fronts(h, inner):
                            dve.wait_ge(qk_mm, f + 1)
                            if inner or h >= 1:
                                dve.wait_ge(st_mm, f - 1)
                            if bq is None:
                                nc.vector.tensor_copy(qT[sf][0:DP, :], p_qk[0:DP, 0:T])
                                nc.vector.tensor_copy(kT[sf][0:DP, :], p_qk[0:DP, T:2 * T]).then_inc(qk_sb, 1)
                            else:
                                nc.vector.tensor_scalar(qT[sf][0:DP, :], p_qk[0:DP, 0:T], bs[sf][:, 0:1], None, ALU.add)
                                nc.vector.tensor_scalar(kT[sf][0:DP, :], p_qk[0:DP, T:2 * T], bs[sf][:, 1:2], None,
                                                        ALU.add).then_inc(qk_sb, 1)
                            dve.wait_ge(s_mm, f + 1)
                            if causal:
                                nc.vector.tensor_tensor(sm[:], p_s[sf][:].rearrange("p (a t) -> p a t", t=T), mask[:],
                                                        ALU.add).then_inc(s_read, 1)
                                dve.wait_ge(s_read, f + 1)
                                nc.vector.tensor_reduce(negm[sf][:], sm[:], AX.X, ALU.max, negate=True).then_inc(negm_done, 1)
                            else:
                                nc.vector.tensor_reduce(negm[sf][:], p_s[sf][:].rearrange("p (a t) -> p a t", t=T), AX.X,
                                                        ALU.max, negate=True).then_inc(negm_done, 1)
                                dve.wait_ge(negm_done, f + 1)
                                dve.sem_inc(s_read, 1)
                            dve.wait_ge(m_mm, f + 1)
                            nc.vector.tensor_copy(qT[sf][DP:KM, :], p_m[DP:KM, 0:T]).then_inc(q_final, 1)
                        if backs(h, inner):
                            k, hk = i - 1, h - 1
                            o = p_o[sf][:, 0:QT * D1].rearrange("p (a d) -> p a d", d=D1)
                            dve.wait_ge(pv_mm, k + 1)
                            nc.vector.reciprocal(rl[sf][:], o[:, :, D]).then_inc(recip_done, 1)
                            dve.wait_ge(recip_done, k + 1)
                            for a in range(QT):
                                dst = y[:, bass.ds(b * QT + a, 1), bass.ds(hk * D, D)].rearrange("p a d -> p (a d)")
                                ins = nc.vector.tensor_scalar(dst, o[:, a, 0:D], rl[sf][:, a:a + 1], None, ALU.mult)
                            ins.then_inc(out_free, 1)
                    pipeline(dve, step)


def add_tokens(nc, name, dst, src):
    with stage(nc, name, "added") as (block, added):
        @block.vector
        def _(dve):
            nc.vector.tensor_tensor(dst[:], dst[:], src[:], ALU.add).then_inc(added, 1)
            dve.wait_ge(added, 1)


def linear(nc, name, g, srcT, kc, w, bias, dst):
    with Space(nc, name) as sb:
        ws = sb("w", [P, kc, C])
        bs = sb("b", [P, C])
        with stage(nc, name, "in_", "product", "used", "step") as (block, in_, product, used, step):
            @block.sync
            def _(sp):
                sp.dma_start(ws[:], w.rearrange("(k p) c -> p k c", p=P)).then_inc(in_, 16)
                sp.dma_start(bs[:], rows(bias)).then_inc(in_, 16)

            @block.tensor
            def _(pe):
                pe.wait_ge(in_, 32)
                for n in range(NT):
                    for k in range(kc):
                        mm = nc.tensor.matmul(g.bank[n // 4][:, n % 4 * P:(n % 4 + 1) * P], srcT[:, k, n * P:(n + 1) * P],
                                              ws[:, k, :], start=(k == 0), stop=(k == kc - 1))
                    if n % 4 == 3:
                        mm.then_inc(product, 1)

            @block.vector
            def _(dve):
                link = Link(dve, step)
                dve.wait_ge(in_, 32)
                link(nc.vector.tensor_tensor(dst[:], dst[:], bs[:].rearrange("p (a c) -> p a c", a=1).to_broadcast([P, NT, C]), ALU.add))
                for n in range(2):
                    dve.wait_ge(product, n + 1)
                    o = dst[:, 4 * n:4 * n + 4, :]
                    link(nc.vector.tensor_tensor(o, o, g.bank[n][:].rearrange("p (a c) -> p a c", c=C), ALU.add))


def hidden(nc, name, g, srcT, w, bias, dstT, fc):
    with Space(nc, name) as sb:
        ws = sb("w", [P, fc * P])
        bs = sb("b", [P, fc])
        with stage(nc, name, "in_", "product", "done") as (block, in_, product, done):
            @block.sync
            def _(sp):
                sp.dma_start(ws[:], w).then_inc(in_, 16)
                sp.dma_start(bs[:], bias).then_inc(in_, 16)

            @block.tensor
            def _(pe):
                pe.wait_ge(in_, 32)
                for n in range(2 * fc):
                    f, half = n // 2, n % 2
                    if n >= 4:
                        pe.wait_ge(done, n - 3)
                    nc.tensor.matmul(g.bank[n % 4][:], ws[:, f * P:(f + 1) * P], srcT[:, 0, half * 512:half * 512 + 512],
                                     start=True, stop=True).then_inc(product, 1)

            @block.scalar
            def _(act):
                for n in range(2 * fc):
                    f, half = n // 2, n % 2
                    act.wait_ge(product, n + 1)
                    nc.scalar.activation(dstT[:, f, half * 512:half * 512 + 512], g.bank[n % 4][:], ACT.Gelu,
                                         bias=bs[:, f:f + 1]).then_inc(done, 1)


def experts(nc, name, g, srcT, w1, b1, w2, wts, dst, kind, FC, FP=P):
    gated = kind == "silu"
    func = {"silu": ACT.Silu, "relu": ACT.Relu, "gelu": ACT.Gelu}[kind]
    W1 = FC * FP * (2 if gated else 1)
    NW = 32 if b1 is None else 48
    NB = 2 if gated else 4
    with Space(nc, name) as sb:
        w1s = [sb(f"w1_{s}", [P, W1]) for s in range(2)]
        w2s = [sb(f"w2_{s}", [FP, FC * C]) for s in range(2)]
        b1s = [sb(f"b1_{s}", [FP, FC]) for s in range(2)] if b1 is not None else None
        hT = sb("hT", [FP, FC, B * T])
        sg = [sb(f"sg{s}", [FP, 512]) for s in range(2)] if gated else None
        p_up = [g.bank[s] for s in range(4)]
        p_dn = [g.bank[4], g.bank[5]]
        with stage(nc, name, "w_in0", "w_in1", "up_mm", "up_free", "gate_done", "h_done", "down_mm", "down_free") as (
                block, w_in0, w_in1, up_mm, up_free, gate_done, h_done, down_mm, down_free):
            w_in = [w_in0, w_in1]
            NH = 2 * FC

            @block.sync
            def _(sp):
                with sp.Fori(0, E // 2) as k:
                    for u in range(2):
                        sp.wait_ge(down_mm, k * 4 + 2 * u)
                        e = bass.ds(k * 2 + u, 1)
                        sp.dma_start(w1s[u][:], w1[e, :, :].rearrange("a k t -> (a k) t")).then_inc(w_in[u], 16)
                        sp.dma_start(w2s[u][:], w2[e, :, :].rearrange("a k t -> (a k) t")).then_inc(w_in[u], 16)
                        if b1 is not None:
                            sp.dma_start(b1s[u][:], b1[e, :, :].rearrange("a k t -> (a k) t")).then_inc(w_in[u], 16)

            @block.tensor
            def _(pe):
                pe.sem_inc(down_mm, 2)
                with pe.Fori(0, E // 2) as k:
                    for u in range(2):
                        e = k * 2 + u
                        pe.wait_ge(w_in[u], (k + 1) * NW)
                        for n in range(NH):
                            half, f = n // FC, n % FC
                            x = srcT[:, 0, half * 512:half * 512 + 512]
                            pe.wait_ge(up_free, e * NH + n + 1)
                            s = n % NB
                            mm = nc.tensor.matmul(p_up[s][0:FP, :], w1s[u][:, f * FP:(f + 1) * FP], x, start=True, stop=True)
                            if gated:
                                mm = nc.tensor.matmul(p_up[2 + s][0:FP, :], w1s[u][:, (FC + f) * FP:(FC + f + 1) * FP], x,
                                                      start=True, stop=True)
                            mm.then_inc(up_mm, 1)
                        for half in range(2):
                            pe.wait_ge(h_done, e * NH + (half + 1) * FC)
                            pe.wait_ge(down_free, e * 2 + half + 1)
                            for n in range(4):
                                for f in range(FC):
                                    t = (half * 4 + n) * P
                                    mm = nc.tensor.matmul(p_dn[half][:, n * P:(n + 1) * P], hT[:, f, t:t + P],
                                                          w2s[u][:, f * C:(f + 1) * C], start=(f == 0), stop=(f == FC - 1))
                            mm.then_inc(down_mm, 1)

            @block.scalar
            def _(act):
                if not gated:
                    act.sem_inc(up_free, NB)
                with act.Fori(0, E // 2) as k:
                    for u in range(2):
                        e = k * 2 + u
                        for n in range(NH):
                            half, f = n // FC, n % FC
                            o = hT[:, f, half * 512:half * 512 + 512]
                            act.wait_ge(up_mm, e * NH + n + 1)
                            if gated:
                                if n < 2:
                                    act.wait_ge(h_done, e * NH)
                                else:
                                    act.wait_ge(h_done, e * NH + n - 1)
                                nc.scalar.activation(sg[n % 2][:], p_up[n % NB][0:FP, :], func).then_inc(gate_done, 1)
                            else:
                                if f == 0:
                                    act.wait_ge(down_mm, e * 2 + half + 1)
                                bias = b1s[u][:, f:f + 1] if b1 is not None else 0.0
                                nc.scalar.activation(o, p_up[n % NB][0:FP, :], func, bias=bias).then_inc(h_done, 1)
                                act.wait_ge(h_done, e * NH + n + 1)
                                act.sem_inc(up_free, 1)

            @block.vector
            def _(dve):
                dve.sem_inc(down_free, 2)
                if gated:
                    dve.sem_inc(up_free, NB)
                with dve.Fori(0, E // 2) as k:
                    for u in range(2):
                        e = k * 2 + u
                        if gated:
                            for n in range(NH):
                                half, f = n // FC, n % FC
                                o = hT[:, f, half * 512:half * 512 + 512]
                                dve.wait_ge(gate_done, e * NH + n + 1)
                                if f == 0:
                                    dve.wait_ge(down_mm, e * 2 + half + 1)
                                nc.vector.tensor_tensor(o, sg[n % 2][:], p_up[2 + n % NB][0:FP, :], ALU.mult).then_inc(h_done, 1)
                                dve.wait_ge(h_done, e * NH + n + 1)
                                dve.sem_inc(up_free, 1)
                        for half in range(2):
                            dve.wait_ge(down_mm, e * 2 + half + 3)
                            dve.wait_ge(down_free, e * 2 + half + 1)
                            for n in range(4):
                                t = half * 4 + n
                                ins = nc.vector.scalar_tensor_tensor(out=dst[:, t, :], in0=p_dn[half][:, n * P:(n + 1) * P],
                                                                     scalar=wts[:, t, bass.ds(e, 1)], in1=dst[:, t, :],
                                                                     op0=ALU.mult, op1=ALU.add)
                            ins.then_inc(down_free, 1)


def expert_biases(nc, name, g, wts, b2, dst):
    with Space(nc, name) as sb:
        wT = sb("wT", [E, B * T])
        b2s = sb("b2", [E, C])
        with stage(nc, name, "in_", "turned", "kept", "product", "step") as (block, in_, turned, kept, product, step):
            @block.sync
            def _(sp):
                sp.dma_start(b2s[:], b2).then_inc(in_, 16)

            @block.tensor
            def _(pe):
                for n in range(NT):
                    mm = nc.tensor.transpose(g.bank[n // 4][0:E, n % 4 * P:(n % 4 + 1) * P], wts[:, n, :], g.ident[:])
                    mm.then_inc(turned, 1)
                pe.wait_ge(kept, 2)
                pe.wait_ge(in_, 16)
                for n in range(NT):
                    nc.tensor.matmul(g.bank[2 + n // 4][:, n % 4 * P:(n % 4 + 1) * P], wT[:, n * P:(n + 1) * P], b2s[:],
                                     start=True, stop=True).then_inc(product, 1)

            @block.vector
            def _(dve):
                link = Link(dve, step)
                for n in range(2):
                    dve.wait_ge(turned, 4 * n + 4)
                    nc.vector.tensor_copy(wT[:, n * 512:(n + 1) * 512], g.bank[n][0:E, :]).then_inc(kept, 1)
                for n in range(2):
                    dve.wait_ge(product, 4 * n + 4)
                    o = dst[:, 4 * n:4 * n + 4, :]
                    link(nc.vector.tensor_tensor(o, o, g.bank[2 + n][:].rearrange("p (a c) -> p a c", c=C), ALU.add))


class Picks:

    def __init__(self, nc, sb, link, n):
        self.nc, self.link, self.n = nc, link, n
        self.rev = sb("rev", [P, 1, E])
        self.r = sb("r", [P, n, E])
        self.rm = sb("rm", [P, n, 1])
        for e in range(E):
            link(nc.vector.memset(self.rev[:, :, e:e + 1], float(E - e)))

    def wide(self, ap):
        return ap[:].to_broadcast([P, self.n, E])

    def first(self, onehot, top, s):
        nc, link = self.nc, self.link
        link(nc.vector.tensor_reduce(top[:], s[:], AX.X, ALU.max))
        link(nc.vector.tensor_tensor(self.r[:], s[:], self.wide(top), ALU.is_equal))
        link(nc.vector.tensor_tensor(self.r[:], self.r[:], self.wide(self.rev), ALU.mult))
        link(nc.vector.tensor_reduce(self.rm[:], self.r[:], AX.X, ALU.max))
        link(nc.vector.tensor_tensor(onehot[:], self.r[:], self.wide(self.rm), ALU.is_equal))

    def without(self, out, s, onehot):
        nc, link = self.nc, self.link
        link(nc.vector.tensor_scalar(self.r[:], onehot[:], -1.0, 1.0, ALU.mult, ALU.add))
        link(nc.vector.tensor_tensor(out[:], s[:], self.r[:], ALU.mult))
        link(nc.vector.scalar_tensor_tensor(out=out[:], in0=onehot[:], scalar=LOWEST, in1=out[:], op0=ALU.mult, op1=ALU.add))


def router(nc, name, g, kind, srcT, wr, wts, br=None):
    n = B if kind == "batch" else NT
    with Space(nc, name) as sb:
        wrs = sb("wr", [C, E])
        brs = sb("br", [P, 1, E])
        s = sb("s", [P, n, E])
        s2 = sb("s2", [P, n, E])
        oh1, oh2 = sb("oh1", [P, n, E]), sb("oh2", [P, n, E])
        m1, m2 = sb("m1", [P, n, 1]), sb("m2", [P, n, 1])
        d, ex = sb("d", [P, 2, n, E]), sb("ex", [P, 2, n, E])
        t = sb("t", [P, n, E])
        u1, u2 = sb("u1", [P, n, 1]), sb("u2", [P, n, 1])
        mean = sb("mean", [P, B])
        meanw = sb("meanw", [P, B, P])
        with stage(nc, name, "in_", "mean_done", "logits", "exp_in", "exp_out", "step") as (
                block, in_, mean_done, logits, exp_in, exp_out, step):
            @block.sync
            def _(sp):
                sp.dma_start(wrs[:], wr).then_inc(in_, 16)
                if br is not None:
                    sp.dma_start(brs[:].rearrange("p a e -> p (a e)"), rows(br)).then_inc(in_, 16)

            @block.tensor
            def _(pe):
                pe.wait_ge(in_, 16 if br is None else 32)
                if kind == "batch":
                    pe.wait_ge(mean_done, 1)
                for i in range(n):
                    lhsT = meanw[:, i, :] if kind == "batch" else srcT[:, 0, i * P:(i + 1) * P]
                    nc.tensor.matmul(g.bank[0][:, i * E:(i + 1) * E], lhsT, wrs[:], start=True, stop=True).then_inc(logits, 1)

            @block.scalar
            def _(act):
                for k in range({"mixer": 2, "top2": 1, "batch": 2}[kind]):
                    act.wait_ge(exp_in, k + 1)
                    i_, o = (d[:, k], ex[:, k])
                    if kind == "mixer" or (kind == "batch" and k == 0):
                        nc.scalar.activation(o, i_, ACT.Exp).then_inc(exp_out, 1)
                    else:
                        nc.scalar.activation(u2[:], u1[:], ACT.Exp).then_inc(exp_out, 1)

            @block.vector
            def _(dve):
                link = Link(dve, step)
                v = nc.vector
                pick = Picks(nc, sb, link, n)
                wide = pick.wide
                if kind == "batch":
                    link(v.tensor_reduce(mean[:], srcT[:].rearrange("p a (b t) -> p (a b) t", b=B), AX.X, ALU.add))
                    link(v.tensor_scalar(mean[:], mean[:], 1.0 / T, None, ALU.mult))
                    link(v.tensor_copy(meanw[:], mean[:].rearrange("p (b a) -> p b a", a=1).to_broadcast([P, B, P])))
                    dve.sem_inc(mean_done, 1)
                dve.wait_ge(logits, n)
                link(v.tensor_copy(s[:], g.bank[0][:, 0:n * E].rearrange("p (n e) -> p n e", e=E)))
                if kind == "mixer":
                    def near(k, sc, top):
                        link(v.tensor_tensor(d[:, k], sc[:], wide(top), ALU.subtract))
                        dve.sem_inc(exp_in, 1)
                        link(v.scalar_tensor_tensor(out=t[:], in0=s[:], scalar=-1.0, in1=s[:], op0=ALU.mult, op1=ALU.max))
                        link(v.tensor_tensor(t[:], t[:], wide(top), ALU.max))
                        link(v.tensor_scalar(t[:], t[:], 2.0 * 0.01, None, ALU.mult))
                        link(v.tensor_tensor(s2[:], wide(top), s[:], ALU.subtract))
                        link(v.tensor_tensor(t[:], s2[:], t[:], ALU.is_le))

                    def gate(k, u):
                        dve.wait_ge(exp_out, k + 1)
                        link(v.tensor_tensor(t[:], t[:], ex[:, k], ALU.mult))
                        link(v.tensor_reduce(u[:], t[:], AX.X, ALU.add))
                        link(v.reciprocal(u[:], u[:]))
                    pick.first(oh1, m1, s)
                    near(0, s, m1)
                    gate(0, u1)
                    pick.without(s2, s, oh1)
                    pick.first(oh2, m2, s2)
                    near(1, s2, m2)
                    gate(1, u2)
                    link(v.tensor_tensor(oh1[:], oh1[:], wide(u1), ALU.mult))
                    link(v.tensor_tensor(oh2[:], oh2[:], wide(u2), ALU.mult))
                    link(v.tensor_tensor(wts[:], oh1[:], oh2[:], ALU.add))
                    return
                if kind == "batch":
                    link(v.tensor_tensor(s[:], s[:], wide(brs), ALU.add))
                    link(v.tensor_reduce(m1[:], s[:], AX.X, ALU.max))
                    link(v.tensor_tensor(d[:, 0], s[:], wide(m1), ALU.subtract))
                    dve.sem_inc(exp_in, 1)
                    dve.wait_ge(exp_out, 1)
                    link(v.tensor_reduce(u1[:], ex[:, 0], AX.X, ALU.add))
                    link(v.reciprocal(u1[:], u1[:]))
                    link(v.tensor_tensor(s[:], ex[:, 0], wide(u1), ALU.mult))
                pick.first(oh1, m1, s)
                pick.without(s2, s, oh1)
                pick.first(oh2, m2, s2)
                link(v.tensor_tensor(u1[:], m2[:], m1[:], ALU.subtract))
                dve.sem_inc(exp_in, 1)
                dve.wait_ge(exp_out, 2 if kind == "batch" else 1)
                link(v.tensor_scalar(u1[:], u2[:], 1.0, None, ALU.add))
                link(v.reciprocal(u1[:], u1[:]))
                link(v.tensor_tensor(u2[:], u2[:], u1[:], ALU.mult))
                if kind == "top2":
                    link(v.tensor_scalar(u1[:], u1[:], 0.5, None, ALU.mult))
                    link(v.tensor_scalar(u2[:], u2[:], 0.5, None, ALU.mult))
                link(v.tensor_tensor(oh1[:], oh1[:], wide(u1), ALU.mult))
                link(v.tensor_tensor(oh2[:], oh2[:], wide(u2), ALU.mult))
                if kind == "batch":
                    for a in range(QT):
                        link(v.tensor_tensor(wts[:].rearrange("p (b a) e -> p b a e", a=QT)[:, :, a, :], oh1[:], oh2[:], ALU.add))
                else:
                    link(v.tensor_tensor(wts[:], oh1[:], oh2[:], ALU.add))


def expert_choice(nc, name, g, srcT, wr, wts, keep):
    with Space(nc, name) as sb:
        wrs = sb("wr", [C, E])
        s = sb("s", [P, NT, E])
        top = sb("top", [P, NT, 1])
        pr = sb("pr", [P, NT, E])
        prw = sb("prw", [P, 2, E, QT, P])
        prt = sb("prt", [P, 2, E, T])
        before = sb("before", [P, QT, T])
        cmp_ = sb("cmp", [P, 2, T])
        ahead = sb("ahead", [P, 2, E, T])
        rank = sb("rank", [P, NT, E])
        with stage(nc, name, "in_", "logits", "exp_in", "exp_out", "made", "wide", "spread", "compared", "step") as (
                block, in_, logits, exp_in, exp_out, made, wide_done, spread, compared, step):
            @block.sync
            def _(sp):
                sp.dma_start(wrs[:], wr).then_inc(in_, 16)

            @block.gpsimd
            def _(pool):
                nc.gpsimd.memset(before[:], 1.0).then_inc(made, 1)
                pool.wait_ge(made, 1)
                nc.gpsimd.affine_select(out=before[:], in_=before[:], compare_op=ALU.is_gt, fill=0.0, base=0,
                                        pattern=[[P, QT], [-1, T]], channel_multiplier=1).then_inc(made, 1)

            @block.tensor
            def _(pe):
                pe.wait_ge(in_, 16)
                for i in range(NT):
                    nc.tensor.matmul(g.bank[0][:, i * E:(i + 1) * E], srcT[:, 0, i * P:(i + 1) * P], wrs[:],
                                     start=True, stop=True).then_inc(logits, 1)
                for b in range(B):
                    pe.wait_ge(wide_done, b + 1)
                    for e in range(E):
                        i = b * E + e
                        if i >= 4:
                            pe.wait_ge(spread, i - 3)
                        for a in range(QT):
                            mm = nc.tensor.matmul(g.bank[1 + i % 4][:, a * P:(a + 1) * P], prw[:, b % 2, e, a, :], g.ident[:],
                                                  start=True, stop=True)
                        mm.then_inc(compared, 1)

            @block.scalar
            def _(act):
                act.wait_ge(exp_in, 1)
                nc.scalar.activation(pr[:], s[:], ACT.Exp).then_inc(exp_out, 1)
                for i in range(B * E):
                    b, e = i // E, i % E
                    act.wait_ge(compared, i + 1)
                    if b >= 2 and e == 0:
                        act.wait_ge(made, 2 + b - 1)
                    nc.scalar.copy(prt[:, b % 2, e, :], g.bank[1 + i % 4][:, 0:T]).then_inc(spread, 1)

            @block.vector
            def _(dve):
                link = Link(dve, step)
                v = nc.vector
                dve.wait_ge(logits, NT)
                link(v.tensor_copy(s[:], g.bank[0][:, 0:NT * E].rearrange("p (n e) -> p n e", e=E)))
                link(v.tensor_reduce(top[:], s[:], AX.X, ALU.max))
                link(v.tensor_tensor(s[:], s[:], top[:].to_broadcast([P, NT, E]), ALU.subtract))
                dve.sem_inc(exp_in, 1)
                dve.wait_ge(exp_out, 1)
                link(v.tensor_reduce(top[:], pr[:], AX.X, ALU.add))
                link(v.reciprocal(top[:], top[:]))
                link(v.tensor_tensor(pr[:], pr[:], top[:].to_broadcast([P, NT, E]), ALU.mult))
                dve.wait_ge(made, 2)

                def widen(b):
                    for a in range(QT):
                        link(v.tensor_copy(prw[:, b % 2, :, a, :],
                                           pr[:, b * QT + a, :].rearrange("p (e a) -> p e a", a=1).to_broadcast([P, E, P])))
                    dve.sem_inc(wide_done, 1)
                widen(0)
                for b in range(B):
                    if b + 1 < B:
                        widen(b + 1)
                    for a in range(QT):
                        for e in range(E):
                            dve.wait_ge(spread, b * E + e + 1)
                            pc = pr[:, b * QT + a, e:e + 1]
                            link(v.scalar_tensor_tensor(out=cmp_[:, e % 2, :], in0=prt[:, b % 2, e, :], scalar=pc,
                                                        in1=before[:, a, :], op0=ALU.is_equal, op1=ALU.mult))
                            link(v.scalar_tensor_tensor(out=ahead[:, a, e, :], in0=prt[:, b % 2, e, :], scalar=pc,
                                                        in1=cmp_[:, e % 2, :], op0=ALU.is_gt, op1=ALU.add))
                        link(v.tensor_reduce(rank[:, b * QT + a, :], ahead[:, a], AX.X, ALU.add))
                    dve.sem_inc(made, 1)
                link(v.tensor_scalar(rank[:], rank[:], float(keep), None, ALU.is_lt))
                link(v.tensor_tensor(wts[:], rank[:], pr[:], ALU.mult))


def context_norm(nc, name, g, ctx, gain, shift, kvT):
    for b in range(B):
        with Space(nc, f"{name}{b}") as sb:
            c = sb("c", [P, CT, CC])
            z = sb("z", [P, CT, CC])
            zT = sb("zT", [CC, TC])
            cols = sb("cols", [CC, 2])
            with stage(nc, f"{name}{b}_load", "in_") as (block, in_):
                @block.sync
                def _(sp):
                    sp.dma_start(c[:, 0:CT - 1, :], ctx[b, 0:(CT - 1) * P, :].rearrange("(t p) c -> p t c", p=P)).then_inc(in_, 16)
                    sp.dma_start(c[0:LAST, CT - 1, :], ctx[b, (CT - 1) * P:TC, :]).then_inc(in_, 16)
                    sp.wait_ge(in_, 32)
            layernorm(nc, f"{name}{b}_ln", c, z, tiles=CT, width=CC, last=LAST)
            with stage(nc, f"{name}{b}_turn", "in_", "turned", "kept", "stored") as (block, in_, turned, kept, stored):
                @block.sync
                def _(sp):
                    sp.dma_start(cols[:, 0:1], gain.rearrange("(n a) -> n a", a=1)).then_inc(in_, 16)
                    sp.dma_start(cols[:, 1:2], shift.rearrange("(n a) -> n a", a=1)).then_inc(in_, 16)
                    sp.wait_ge(kept, CT)
                    sp.dma_start(kvT[b, :, :], zT[:]).then_inc(stored, 16)
                    sp.wait_ge(stored, 16)

                @block.tensor
                def _(pe):
                    for t in range(CT):
                        r = P if t < CT - 1 else LAST
                        if t >= 4:
                            pe.wait_ge(kept, t - 3)
                        nc.tensor.transpose(g.bank[t % 4][0:CC, 0:r], z[0:r, t, :], g.ident[0:r, 0:r]).then_inc(turned, 1)

                @block.vector
                def _(dve):
                    dve.wait_ge(in_, 32)
                    for t in range(CT):
                        r = P if t < CT - 1 else LAST
                        dve.wait_ge(turned, t + 1)
                        nc.vector.tensor_scalar(zT[0:CC, t * P:t * P + r], g.bank[t % 4][0:CC, 0:r], cols[:, 0:1], cols[:, 1:2],
                                                ALU.mult, ALU.add).then_inc(kept, 1)


class Global:
    pass


def build(nc, a, out, sublayers=8):
    with ExitStack() as es:
        def sb(name, shape):
            return es.enter_context(nc.sbuf_tensor(name, shape, F32))
        g = Global()
        g.bank = [es.enter_context(nc.psum_tensor(f"bank{i}", [P, 512], F32)) for i in range(8)]
        g.ident = sb("ident", [P, P])
        x = sb("x", [P, NT, C])
        xn = sb("xn", [P, NT, C])
        xnT = sb("xnT", [P, 1, B * T])
        wts = sb("wts", [P, NT, E])
        xv = lambda t: t.rearrange("b (a p) c -> p (b a) c", p=P)

        with stage(nc, "start", "in_", "made") as (block, in_, made):
            @block.sync
            def _(sp):
                sp.dma_start(x[:], xv(a["x"])).then_inc(in_, 16)
                sp.wait_ge(in_, 16)

            @block.gpsimd
            def _(pool):
                nc.gpsimd.memset(g.ident[:], 0.0).then_inc(made, 1)
                pool.wait_ge(made, 1)
                nc.gpsimd.affine_select(out=g.ident[:], in_=g.ident[:], compare_op=ALU.not_equal, fill=1.0, base=0,
                                        pattern=[[-1, P]], channel_multiplier=1).then_inc(made, 1)
                pool.wait_ge(made, 2)

        g.ctx = Context(lambda n, shape, dt: es.enter_context(nc.sbuf_tensor(n, shape, dt)))
        split_context(nc, "split", g.ctx, a["cT"])

        def normed(name):
            layernorm(nc, name + "_ln", x, xn)
            transpose_tokens(nc, name + "_xnT", g, xn, [(xnT, None, None)])

        def cross(ctx, name, wq, wkT, bq, wv, y, heads, D, scale, add, key_bias, bv=None):
            V = nc.dram_tensor(name + "_V", [B, heads, P, CT * (D + 1)], F32).ap()
            project_values(nc, name + "v", g, ctx, wv, heads, D, V)
            cross_attention(nc, name + "cross", g, ctx, wq, wkT, bq, V, xnT, y, heads, D, scale, add, key_bias, bv)

        def l0_attention():
            normed("l0a")
            with Space(nc, "l0a") as s:
                y = s("y", [P, NT, C])
                yT = s("yT", [P, 1, B * T])
                self_attention(nc, "l0self", g, a["l0_wq"], a["l0_wk"], a["l0_bq"], a["l0_bk"], a["L0_xattn_Wv"], a["L0_xattn_bv"],
                               xnT, xnT, y, C // H, (C // H) ** -0.5, True)
                cross(g.ctx, "l0", a["l0_wcq"], a["l0_wckT"], a["l0_bcq"], a["L0_xattn_Wcv"], y, H, C // H, (C // H) ** -0.5,
                      True, True, a["L0_xattn_bcv"])
                transpose_tokens(nc, "l0yT", g, y, [(yT, None, None)])
                linear(nc, "l0out", g, yT, 1, a["L0_xattn_Wp"], a["L0_xattn_bp"], x)

        def l0_ffn():
            normed("l0f")
            router(nc, "l0router", g, "mixer", xnT, a["l0_wr"], wts)
            experts(nc, "l0experts", g, xnT, a["l0_w1"], None, a["l0_w2"], wts, x, "silu", 2)

        def l1_attention():
            normed("l1a")
            cross(g.ctx, "l1", a["l1_wq"], a["l1_wkT"], a["l1_bq"], a["L1_xattn_Wv"], x, 1, C, 1.0, True, True, a["L1_xattn_bv"])

        def l1_ffn():
            normed("l1f")
            router(nc, "l1router", g, "top2", xnT, a["L1_ffn_w_gate"], wts)
            expert_biases(nc, "l1bias", g, wts, a["L1_ffn_bu"], x)
            experts(nc, "l1experts", g, xnT, a["L1_ffn_Wd"], a["l1_b1"], a["L1_ffn_Wu"], wts, x, "relu", 1, 64)

        def mlp(name, s, r, pre):
            hT = s(name + "hT", [P, 4, B * T])
            layernorm(nc, name + "_ln3", r, xn)
            transpose_tokens(nc, name + "_ln3T", g, xn, [(xnT, a[pre + "ln3_g"], a[pre + "ln3_b"])])
            hidden(nc, name + "_h", g, xnT, a[pre + "li2_w"], a[pre + "li2_bT"], hT, 4)
            linear(nc, name + "_o", g, hT, 4, a[pre + "li3_w"], a[pre + "li3_b"], r)

        def l2_attention():
            W = H * 32
            with Space(nc, "l2a") as s:
                x1 = s("x1", [P, NT, C])
                r = s("r", [P, NT, C])
                layernorm(nc, "l2_ln0", x, xn)
                layernorm(nc, "l2_ln1", xn, x1, a["L2_xattn_ln1_g"], a["L2_xattn_ln1_b"])
                layernorm(nc, "l2_a1ln", x1, xn)
                with Space(nc, "l2a1") as s1:
                    kvn = s1("kvn", [P, 1, B * T])
                    y = s1("y", [P, NT, W])
                    transpose_tokens(nc, "l2_a1T", g, xn, [(xnT, a["L2_xattn_a1_lnx_g"], a["L2_xattn_a1_lnx_b"]),
                                                           (kvn, a["L2_xattn_a1_lny_g"], a["L2_xattn_a1_lny_b"])])
                    self_attention(nc, "l2self", g, a["L2_xattn_a1_wq"], a["L2_xattn_a1_wk"], None, None, a["l2_a1_wv"], None,
                                   xnT, kvn, y, 32, 32 ** -0.5, False)
                    after_attention("l2a1o", s1, x1, r, y, "L2_xattn_a1_")
                add_tokens(nc, "l2_add1", r, x1)
                layernorm(nc, "l2_ln2", r, x1, a["L2_xattn_ln2_g"], a["L2_xattn_ln2_b"])
                layernorm(nc, "l2_a2ln", x1, xn)
                transpose_tokens(nc, "l2_a2T", g, xn, [(xnT, a["L2_xattn_a2_lnx_g"], a["L2_xattn_a2_lnx_b"])])
                context_norm(nc, "l2ctx", g, a["ctx_512"], a["L2_xattn_a2_lny_g"], a["L2_xattn_a2_lny_b"], g.kvT2)
                with Space(nc, "l2a2") as s1:
                    y = s1("y", [P, NT, W])
                    with Space(nc, "l2c") as s2:
                        ctx = Context(s2)
                        split_context(nc, "l2split", ctx, g.kvT2)
                        cross(ctx, "l2", a["L2_xattn_a2_wq"], a["l2_a2_wkT"], None, a["l2_a2_wv"], y, H, 32, 32 ** -0.5,
                              False, False)
                    after_attention("l2a2o", s1, x1, r, y, "L2_xattn_a2_")
                add_tokens(nc, "l2_add2", x, x1)
                add_tokens(nc, "l2_add3", x, r)

        def after_attention(name, s, x1, r, y, pre):
            with Space(nc, name) as s2:
                yT = s2("yT", [P, 4, B * T])
                with stage(nc, name + "_copy", "copied") as (block, copied):
                    @block.vector
                    def _(dve):
                        nc.vector.tensor_copy(r[:], x1[:]).then_inc(copied, 1)
                        dve.wait_ge(copied, 1)
                transpose_tokens(nc, name + "_yT", g, y, [(yT, None, None)], width=512)
                linear(nc, name + "_lin", g, yT, 4, a[pre + "li1_w"], a[pre + "li1_b"], r)
            with Space(nc, name + "m") as s2:
                mlp(name, s2, r, pre)

        def l2_ffn():
            normed("l2f")
            router(nc, "l2router", g, "batch", xnT, a["L2_ffn_Wr"], wts, a["L2_ffn_br"])
            expert_biases(nc, "l2bias", g, wts, a["L2_ffn_b2"], xn)
            experts(nc, "l2experts", g, xnT, a["L2_ffn_W1"], a["l2_b1"], a["l2_w2"], wts, xn, "gelu", 4)
            with Space(nc, "l2f") as s:
                z = s("z", [P, NT, C])
                layernorm(nc, "l2f_out", xn, z, a["L2_ffn_gamma"], a["L2_ffn_beta"])
                add_tokens(nc, "l2f_add", x, z)

        def l3_attention():
            normed("l3a")
            with Space(nc, "l3a") as s:
                y = s("y", [P, NT, H * 64])
                cross(g.ctx, "l3", a["l3_wq"], a["l3_wkT"], None, a["L3_xattn_Wv"], y, H, 64, 64 ** -0.5, False, False)
                yT = s("yT", [P, 8, B * T])
                transpose_tokens(nc, "l3yT", g, y, [(yT, None, None)], width=H * 64)
                linear(nc, "l3out", g, yT, 8, a["L3_xattn_Wo"], a["L3_xattn_bo"], x)

        def l3_ffn():
            normed("l3f")
            expert_choice(nc, "l3router", g, xnT, a["l3_wr"], wts, int(2.0 * T / E))
            experts(nc, "l3experts", g, xnT, a["L3_ffn_w1"], None, a["l3_w2"], wts, x, "gelu", 4)

        g.kvT2 = nc.dram_tensor("kvT2", [B, CC, TC], F32).ap()
        for f in (l0_attention, l0_ffn, l1_attention, l1_ffn, l2_attention, l2_ffn, l3_attention, l3_ffn)[:sublayers]:
            f()

        with stage(nc, "end", "stored") as (block, stored):
            @block.sync
            def _(sp):
                sp.dma_start(xv(out), x[:]).then_inc(stored, 16)
                sp.wait_ge(stored, 16)


def layout(v, np):
    def f(n):
        return np.asarray(v[n], np.float32)

    def heads(w, D, pad=None):
        w = w.reshape(w.shape[0], -1, D).transpose(1, 0, 2)
        return np.pad(w, ((0, 0), (0, 0), (0, (pad or D) - D)))

    def col(b, D, pad=None):
        b = b.reshape(-1, D, 1)
        return np.pad(b, ((0, 0), (0, (pad or D) - D), (0, 0)))

    def keyT(w, b, D):
        n = w.shape[1] // D
        return np.concatenate([w.T.reshape(n, D, CC), b.reshape(n, D, 1)], 2)

    def down(w, FP):
        return w.reshape(E, -1, FP, C).transpose(0, 2, 1, 3).reshape(E, FP, -1)

    zero = lambda n: np.zeros(n, np.float32)
    a = {n: f(n) for n in v if v[n] is not None}
    a["cT"] = f("ctx_512").transpose(0, 2, 1)
    D = C // H
    a["l0_wq"], a["l0_wk"] = heads(f("L0_xattn_Wq"), D, 32), heads(f("L0_xattn_Wk"), D, 32)
    a["l0_bq"], a["l0_bk"] = col(f("L0_xattn_bq"), D, 32), col(f("L0_xattn_bk"), D, 32)
    a["l0_wcq"], a["l0_bcq"] = heads(f("L0_xattn_Wcq"), D), col(f("L0_xattn_bcq"), D)
    a["l0_wckT"] = keyT(f("L0_xattn_Wck"), f("L0_xattn_bck"), D)
    a["l0_wr"] = f("L0_ffn_router_w").T
    a["l0_w1"] = np.concatenate([f("L0_ffn_w_gate").transpose(0, 2, 1), f("L0_ffn_w_up").transpose(0, 2, 1)], 2)
    a["l0_w2"] = down(f("L0_ffn_w_down").transpose(0, 2, 1), P)
    a["l1_wq"], a["l1_bq"] = heads(f("L1_xattn_Wq"), C), col(f("L1_xattn_bq"), C)
    a["l1_wkT"] = keyT(f("L1_xattn_Wk"), f("L1_xattn_bk"), C)
    a["l1_b1"] = f("L1_ffn_bd").reshape(E, 64, 1)
    a["l2_a1_wv"] = f("L2_xattn_a1_wv").transpose(1, 0, 2).reshape(C, -1)
    a["l2_a2_wkT"] = np.concatenate([f("L2_xattn_a2_wk").transpose(0, 2, 1), zero((H, 32, 1))], 2)
    a["l2_a2_wv"] = f("L2_xattn_a2_wv").transpose(1, 0, 2).reshape(CC, -1)
    for p in ("L2_xattn_a1_", "L2_xattn_a2_"):
        a[p + "li2_bT"] = f(p + "li2_b").reshape(4, P).T
    a["l2_b1"] = f("L2_ffn_b1").reshape(E, 4, P).transpose(0, 2, 1)
    a["l2_w2"] = down(f("L2_ffn_W2"), P)
    a["l3_wq"] = heads(f("L3_xattn_Wq"), 64)
    a["l3_wkT"] = keyT(f("L3_xattn_Wk"), zero(H * 64), 64)
    a["l3_wr"] = f("L3_ffn_gate_w").T
    a["l3_w2"] = down(f("L3_ffn_w2"), P)
    return {n: np.ascontiguousarray(w) for n, w in a.items()}


SUBLAYERS = 8


def kernel(**inputs):
    import numpy as np
    import concourse.bacc as bacc
    from concourse.bass_utils import run_bass_kernel_spmd

    nc = bacc.Bacc("TRN2", target_bir_lowering=False, num_devices=1)
    arrays = layout(inputs, np)
    a = {n: nc.dram_tensor(f"in_{n}", list(w.shape), F32, kind="ExternalInput").ap() for n, w in arrays.items()}
    out = nc.dram_tensor("out", [B, T, C], F32, kind="ExternalOutput").ap()
    build(nc, a, out, SUBLAYERS)
    r = run_bass_kernel_spmd(nc, [{f"in_{n}": w for n, w in arrays.items()}], core_ids=[0])
    return r.results[0]["out"]
```

```python
from contextlib import ExitStack, contextmanager

import concourse.bass as bass
from concourse import mybir

F32 = mybir.dt.float32
F32R = mybir.dt.float32r
ALU = mybir.AluOpType
ACT = mybir.ActivationFunctionType
AX = mybir.AxisListType

P = 128
B, T, C = 4, 256, 128
TC, CC = 1601, 64
KA = CC + 1
TCE = TC + 1
KV = 3 * CC
NT = B * T // P
QT = T // P
H = 16
E = 8
CT = -(-TC // P)
LAST = TC - (CT - 1) * P
EPS = 1e-5
LOWEST = -3.0e38


class Signals:
    last = ExitStack()
    sems = []


@contextmanager
def stage(nc, name, *signals):
    es = ExitStack()
    sems = [es.enter_context(nc.semaphore(f"{name}_{s}")) for s in signals]
    for s in Signals.sems:
        nc.sync.sem_clear(s)
    with nc.Block() as block:
        yield (block, *sems)
    Signals.last.close()
    Signals.last, Signals.sems = es, sems


class Early:

    def __init__(self, nc, sem):
        self.nc, self.sem, self.n = nc, sem, 0

    def load(self, dst, src):
        self.nc.sync.dma_start(dst, src).then_inc(self.sem, 16)
        self.n += 16

    def ready(self, *engines):
        for eng in engines:
            eng.wait_ge(self.sem, self.n)


class Link:

    def __init__(self, eng, sem, base=0):
        self.eng, self.sem, self.base, self.n = eng, sem, base, 0

    def __call__(self, ins):
        ins.then_inc(self.sem, 1)
        self.n += 1
        self.eng.wait_ge(self.sem, self.base + self.n)


class Space:

    def __init__(self, nc, name):
        self.nc, self.name, self.es = nc, name, ExitStack()

    def __enter__(self):
        return self

    def __exit__(self, *a):
        self.es.close()

    def __call__(self, name, shape, dt=F32):
        return self.es.enter_context(self.nc.sbuf_tensor(f"{self.name}_{name}", shape, dt))


def bcast(ap, shape):
    return ap.to_broadcast(shape)


def rows(dram, n=P):
    return dram.rearrange("(a n) -> a n", a=1).to_broadcast([n, dram.shape[0]])


def layernorm(nc, name, src, dst, gain=None, shift=None, width=C, groups=1, last=P, early=None):
    with Space(nc, name) as sb:
        tiles = src.shape[1]
        K = tiles // groups
        stats = sb("stats", [P, tiles, 6])
        mv = sb("mv", [P, tiles, 2])
        std = sb("std", [P, tiles])
        rstd = sb("rstd", [P, tiles])
        gb = sb("gb", [P, 2, width]) if gain is not None else None
        full = lambda ap: ap.rearrange("p (g k) c -> p g k c", k=K)
        mv4, std4, rstd4 = full(mv[:]), std[:].rearrange("p (g k) -> p g k", k=K), rstd[:].rearrange("p (g k) -> p g k", k=K)
        parts = [(slice(0, K), P)] if last == P else [(slice(0, K - 1), P), (slice(K - 1, K), last)]
        with stage(nc, name, "moments", "std", "step", "affine_in") as (block, moments, std_done, step, affine_in):
            @block.sync
            def _(sp):
                if gain is not None:
                    sp.dma_start(gb[:, 0, :], rows(gain)).then_inc(affine_in, 16)
                    sp.dma_start(gb[:, 1, :], rows(shift)).then_inc(affine_in, 16)

            @block.vector
            def _(dve):
                if early is not None:
                    early.ready(dve)
                for n in range(tiles):
                    r = P if n % K < K - 1 else last
                    nc.vector.bn_stats(stats[0:r, n, :], src[0:r, n, :]).then_inc(step, 1)
                dve.wait_ge(step, tiles)
                for n in range(tiles):
                    r = P if n % K < K - 1 else last
                    nc.vector.bn_aggr(mv[0:r, n, :], stats[0:r, n, :]).then_inc(step, 1)
                dve.wait_ge(step, 2 * tiles)
                for s, r in parts:
                    nc.vector.tensor_scalar(rstd4[0:r, :, s], mv4[0:r, :, s, 1], EPS, None, ALU.add).then_inc(moments, 1)
                dve.wait_ge(std_done, len(parts))
                for s, r in parts:
                    nc.vector.reciprocal(rstd4[0:r, :, s], std4[0:r, :, s]).then_inc(step, 1)
                dve.wait_ge(step, 2 * tiles + len(parts))
                for n in range(tiles):
                    r = P if n % K < K - 1 else last
                    nc.vector.tensor_scalar(dst[0:r, n, :], src[0:r, n, :], mv[0:r, n, 0:1],
                                            rstd[0:r, n:n + 1], ALU.subtract, ALU.mult).then_inc(step, 1)
                dve.wait_ge(step, 3 * tiles + len(parts))
                if gain is not None:
                    dve.wait_ge(affine_in, 32)
                    n = 3 * tiles + len(parts)
                    for k, op in ((0, ALU.mult), (1, ALU.add)):
                        for s, r in parts:
                            o = full(dst)[0:r, :, s]
                            row = gb[0:r, k, :].rearrange("p (g k c) -> p g k c", g=1, k=1)
                            nc.vector.tensor_tensor(o, o, row.to_broadcast(list(o.shape)), op).then_inc(step, 1)
                        n += len(parts)
                        dve.wait_ge(step, n)

            @block.scalar
            def _(act):
                act.wait_ge(moments, len(parts))
                for s, r in parts:
                    nc.scalar.activation(std4[0:r, :, s], rstd4[0:r, :, s], ACT.Sqrt).then_inc(std_done, 1)


def transpose_tokens(nc, name, g, src, outs, width=C):
    kc = width // P
    with Space(nc, name) as sb:
        cols = sb("cols", [P, 2 * len(outs)])
        with stage(nc, name, "turned", "kept", "kept_act", "cols_in") as (block, turned, kept, kept_act, cols_in):
            n_cols = sum(gain is not None for _, gain, _ in outs)

            @block.sync
            def _(sp):
                for k, (_, gain, shift) in enumerate(outs):
                    if gain is not None:
                        sp.dma_start(cols[:, 2 * k:2 * k + 1], gain.rearrange("(n a) -> n a", a=1)).then_inc(cols_in, 16)
                        sp.dma_start(cols[:, 2 * k + 1:2 * k + 2], shift.rearrange("(n a) -> n a", a=1)).then_inc(cols_in, 16)

            def done(eng, n):
                if n > 0:
                    eng.wait_ge((kept, kept_act)[(n - 1) % 2], (n + 1) // 2)

            @block.tensor
            def _(pe):
                for i in range(kc * 2):
                    c, half = i // 2, i % 2
                    done(pe, i - 3)
                    for n in range(4):
                        mm = nc.tensor.transpose(g.bank[i % 4][:, n * P:(n + 1) * P],
                                                 src[:, half * 4 + n, c * P:(c + 1) * P], g.ident[:])
                    mm.then_inc(turned, 1)

            @block.vector
            def _(dve):
                if n_cols:
                    dve.wait_ge(cols_in, 32 * n_cols)
                for i in range(0, kc * 2, 2):
                    dve.wait_ge(turned, i + 1)
                    for k, (dst, gain, _) in enumerate(outs):
                        o = dst[:, i // 2, 0:512]
                        if gain is None:
                            ins = nc.vector.tensor_copy(o, g.bank[i % 4][:])
                        else:
                            ins = nc.vector.tensor_scalar(o, g.bank[i % 4][:], cols[:, 2 * k:2 * k + 1],
                                                          cols[:, 2 * k + 1:2 * k + 2], ALU.mult, ALU.add)
                    ins.then_inc(kept, 1)

            @block.scalar
            def _(act):
                if n_cols:
                    act.wait_ge(cols_in, 32 * n_cols)
                for i in range(1, kc * 2, 2):
                    act.wait_ge(turned, i + 1)
                    for k, (dst, gain, _) in enumerate(outs):
                        o = dst[:, i // 2, 512:1024]
                        if gain is None:
                            ins = nc.scalar.copy(o, g.bank[i % 4][:])
                        else:
                            ins = nc.scalar.activation(o, g.bank[i % 4][:], ACT.Identity, bias=cols[:, 2 * k + 1:2 * k + 2],
                                                       scale=cols[:, 2 * k:2 * k + 1])
                    ins.then_inc(kept_act, 1)


class Context:

    def __init__(self, nc, name):
        self.hi_lo = nc.dram_tensor(name + "_hi_lo", [B, P, TCE], F32).ap()
        self.hi_one = nc.dram_tensor(name + "_hi_one", [B, KA, TCE], F32).ap()
        self.tok = nc.dram_tensor(name + "_tok", [B, P, CT, KV], F32).ap()


def load_context(nc, name, g, raw, src):
    with stage(nc, name, "cleared") as (block, cleared):
        @block.gpsimd
        def _(pool):
            nc.gpsimd.memset(raw[:, :, CT - 1, :], 0.0).then_inc(cleared, 1)
            pool.wait_ge(cleared, 1)
    for b in range(B):
        g.early.load(raw[:, b, 0:CT - 1, :], src[b, 0:(CT - 1) * P, :].rearrange("(t p) c -> p t c", p=P))
        g.early.load(raw[0:LAST, b, CT - 1, :], src[b, (CT - 1) * P:TC, :])
        g.early.load(raw[LAST:LAST + 1, b, CT - 1, :], src[b, TC - 1:TC, :])


def split_context(nc, name, g, ctx, raw):
    G = 4
    NU = -(-CT // G)
    with Space(nc, name) as sb:
        hi_lo = [sb(f"hi_lo{s}", [P, TCE], F32R) for s in range(2)]
        hi_one = [sb(f"hi_one{s}", [KA, TCE], F32R) for s in range(2)]
        tok = [sb(f"tok{s}", [P, CT, KV], F32R) for s in range(2)]
        with stage(nc, name, "turned", "hi_done", "lo_done", "tok_hi", "tok_lo", "one_set", "stored0", "stored1") as (
                block, turned, hi_done, lo_done, tok_hi, tok_lo, one_set, stored0, stored1):
            stored = [stored0, stored1]

            def unit(n):
                b, u = n // NU, n % NU
                return b, u * G * P, min(G * P, TCE - u * G * P)

            def slot_free(eng, b):
                if b >= 2:
                    eng.wait_ge(stored[b % 2], 48 * (b // 2))

            @block.sync
            def _(sp):
                sp.wait_ge(one_set, 6)
                for b in range(B):
                    sp.wait_ge(hi_done, 2 * NU * (b + 1))
                    sp.wait_ge(lo_done, NU * (b + 1))
                    sp.dma_start(ctx.hi_lo[b, :, :], hi_lo[b % 2][:].bitcast(F32)).then_inc(stored[b % 2], 16)
                    sp.dma_start(ctx.hi_one[b, :, :], hi_one[b % 2][:].bitcast(F32)).then_inc(stored[b % 2], 16)
                    sp.wait_ge(tok_lo, 2 * b + 2)
                    sp.dma_start(ctx.tok[b, :, :, :], tok[b % 2][:].bitcast(F32)).then_inc(stored[b % 2], 16)
                for s in range(2):
                    sp.wait_ge(stored[s], 48 * (B // 2))

            @block.tensor
            def _(pe):
                g.early.ready(pe)
                for n in range(B * NU):
                    b, c, w = unit(n)
                    if n >= 4:
                        pe.wait_ge(hi_done, 2 * (n - 3))
                        pe.wait_ge(lo_done, n - 3)
                    for k in range(0, w, P):
                        r = min(P, w - k)
                        mm = nc.tensor.transpose(g.bank[n % 4][0:CC, k:k + r], raw[0:r, b, (c + k) // P, :], g.ident[0:r, 0:r])
                    mm.then_inc(turned, 1)

            @block.scalar
            def _(act):
                for n in range(B * NU):
                    b, c, w = unit(n)
                    if n % NU == 0:
                        slot_free(act, b)
                    act.wait_ge(turned, n + 1)
                    nc.scalar.copy(hi_lo[b % 2][0:CC, c:c + w], g.bank[n % 4][0:CC, 0:w]).then_inc(hi_done, 1)
                    nc.scalar.copy(hi_one[b % 2][0:CC, c:c + w], g.bank[n % 4][0:CC, 0:w]).then_inc(hi_done, 1)

            @block.gpsimd
            def _(pool):
                g.early.ready(pool)
                for k in range(2):
                    nc.gpsimd.memset(hi_one[k][CC:KA, :].bitcast(F32), 1.0).then_inc(one_set, 1)
                    pool.wait_ge(one_set, 3 * k + 1)
                    nc.gpsimd.memset(tok[k][:, :, CC:KA].bitcast(F32), 1.0).then_inc(one_set, 1)
                    pool.wait_ge(one_set, 3 * k + 2)
                    nc.gpsimd.memset(tok[k][:, :, 2 * CC:KV].bitcast(F32), 0.0).then_inc(one_set, 1)
                    pool.wait_ge(one_set, 3 * k + 3)
                for b in range(B):
                    slot_free(pool, b)
                    nc.gpsimd.tensor_copy(tok[b % 2][:, :, 0:CC], raw[:, b, :, :]).then_inc(tok_hi, 1)

            @block.vector
            def _(dve):
                g.early.ready(dve)
                for n in range(B * NU):
                    b, c, w = unit(n)
                    dve.wait_ge(hi_done, 2 * n + 2)
                    nc.vector.tensor_tensor(hi_lo[b % 2][CC:2 * CC, c:c + w], g.bank[n % 4][0:CC, 0:w],
                                            hi_lo[b % 2][0:CC, c:c + w].bitcast(F32), ALU.subtract).then_inc(lo_done, 1)
                    if n % NU == NU - 1:
                        dve.wait_ge(tok_hi, b + 1)
                        dve.wait_ge(one_set, 6)
                        for dst, src in ((slice(KA, 2 * CC), slice(0, CC - 1)), (slice(KV - 1, KV), slice(CC - 1, CC))):
                            nc.vector.tensor_tensor(tok[b % 2][:, :, dst], raw[:, b, :, src], tok[b % 2][:, :, src].bitcast(F32),
                                                    ALU.subtract).then_inc(tok_lo, 1)


class Head:

    def __init__(self, b, h, i, turn, u):
        self.b, self.h, self.i, self.turn, self.u = b, h, i, turn, u


def run_heads(eng, heads, step):
    def fixed(b, c):
        def at(d):
            i = b * heads + c + d
            return Head(i // heads, i % heads, i, i // 2, i % 2) if 0 <= i < B * heads else None
        return at

    def looped(b, k, c):
        def at(d):
            return Head(b, k * 2 + c + d, k * 2 + b * heads + c + d, k + (b * heads + c + d) // 2, (c + d) % 2)
        return at

    for c in (-2, -1):
        step(fixed(0, c))
    for b in range(B):
        first = min(heads, 4 if b == 0 else 2)
        for c in range(first):
            step(fixed(b, c))
        if heads > 2:
            with eng.Fori(0, (heads - 2 - first) // 2) as k:
                step(looped(b, k, first))
                step(looped(b, k, first + 1))
            step(fixed(b, heads - 2))
            step(fixed(b, heads - 1))
    for c in range(2):
        step(fixed(B, c))


def after(eng, sem, n):
    if not isinstance(n, int) or n > 0:
        eng.wait_ge(sem, n)


def cross_weights(g, sb, name, w, D):
    heads, WV = w.shape[1], C + KA + 1
    ws, wvs = sb(name + "_w", [D, heads, WV]), sb(name + "_wv", [P, heads, D + 1])
    g.early.load(ws[:], w[0:D, :, 0:WV])
    g.early.load(wvs[:], w[:, :, WV:])
    return ws, wvs


def cross_attention(nc, name, g, ctx, weights, normT, y, heads, D, scale, add, key_bias, query_bias):
    D1 = D + 1
    ws, wvs = weights
    KR = CC + 1 if key_bias else CC
    NG = (CT + 1) // 2
    CW = [402, 400, 400, 400]
    C0 = [0, 402, 802, 1202]
    NJ = QT * len(CW)
    VM = NJ + (1 if key_bias else 2)
    BY_POOL = (1, 2, 3, 4, 5)
    BY_DVE = [n for n in range(NG) if n not in BY_POOL]
    NS = 2 if heads > 4 else B
    WV = C + KA + 1
    with Space(nc, name) as sb:
        hi_lo = [sb(f"hi_lo{s}", [P, TCE], F32R) for s in range(NS)]
        hi_one = [sb(f"hi_one{s}", [KA, TCE], F32R) for s in range(NS)]
        tok = [sb(f"tok{s}", [P, CT, KV], F32R) for s in range(NS)]
        ms = sb("m", [C, heads, KA])
        bms = sb("bm", [KA, heads]) if query_bias else None
        mst = [sb(f"mst{s}", [C, KA]) for s in range(2)]
        q_hi = [sb(f"q_hi{s}", [P, T], F32R) for s in range(2)]
        q_lo = [sb(f"q_lo{s}", [KA, T], F32R) for s in range(2)]
        kb = [sb(f"kb{s}", [KA, T]) for s in range(2)] if key_bias else None
        top = sb("top", [KA, T]) if key_bias else None
        mx = [sb(f"mx{s}", [P, NJ]) for s in range(2)]
        negm = [sb(f"negm{s}", [P, QT]) for s in range(2)]
        PT = sb("PT", [P, CT, T])
        PH = [sb(f"PH{s}", [P, CT, T], F32R) for s in range(2)]
        PL = [sb(f"PL{s}", [P, CT, T], F32R) for s in range(2)]
        zT = [sb(f"zT{s}", [P, T]) for s in range(2)]
        rl = [sb(f"rl{s}", [P, QT]) for s in range(2)]
        p_qk = g.bank[0][:, T:2 * T]
        p_m = g.bank[0][CC:KA, 0:T]
        p_s, p_st = [g.bank[2], g.bank[3]], [g.bank[4], g.bank[5]]
        p_z = [g.bank[6 + s][:, 0:T] for s in range(2)]
        p_o = g.bank[1][:, 0:QT * D1].rearrange("p (a d) -> p a d", d=D1)

        names = ["ctx_in0", "ctx_in1", "ctx_in2", "ctx_in3", "pair_mm", "pair_sb", "w_set", "waits_taken", "qk_mm", "kb_done", "q_hi_done", "q_lo_done",
                 "s_mm", "max_done", "negm_done", "m_mm", "top_done", "m_done", "st_mm", "exp_done", "high_done", "low_dve", "low_pool", "z_mm", "z_sb",
                 "o_mm", "recip_done", "y_done"]
        with stage(nc, name, *names) as (
                block, ctx_in0, ctx_in1, ctx_in2, ctx_in3, pair_mm, pair_sb, w_set, waits_taken, qk_mm, kb_done, q_hi_done, q_lo_done, s_mm,
                max_done, negm_done, m_mm, top_done, m_done, st_mm, exp_done, high_done, low_dve, low_pool, z_mm, z_sb, o_mm, recip_done, y_done):

            ctx_in = [ctx_in0, ctx_in1, ctx_in2, ctx_in3]

            def low_done(eng, i, n):
                if n in BY_POOL:
                    after(eng, low_pool, i * len(BY_POOL) + BY_POOL.index(n) + 1)
                else:
                    after(eng, low_dve, i * len(BY_DVE) + BY_DVE.index(n) + 1)

            def group(at_, n):
                k = min(2, CT - 2 * n)
                r = P if k == 2 else LAST
                return at_[0:r, 2 * n:2 * n + k, :].rearrange("p t q -> p (t q)")

            GM = min(heads, 4)
            NM = heads // GM

            @block.sync
            def _(sp):
                for b in range(B):
                    if b >= NS:
                        sp.wait_ge(z_mm, (b - NS + 1) * heads)
                    sp.dma_start(hi_lo[b % NS][:].bitcast(F32), ctx.hi_lo[b, :, :]).then_inc(ctx_in[b % NS], 16)
                    sp.dma_start(hi_one[b % NS][:].bitcast(F32), ctx.hi_one[b, :, :]).then_inc(ctx_in[b % NS], 16)
                    sp.dma_start(tok[b % NS][:].bitcast(F32), ctx.tok[b, :, :, :]).then_inc(ctx_in[b % NS], 16)

            @block.gpsimd
            def _(pool):
                pool.wait_ge(pair_sb, NM)

                def step(at):
                    q, m = at(2), at(0)
                    if q:
                        after(pool, qk_mm, q.i - 1)
                        nc.gpsimd.tensor_copy(mst[q.u][:], ms[:, bass.ds(q.h, 1), :].rearrange("p a d -> p (a d)")).then_inc(w_set, 1)
                    if m:
                        for n in BY_POOL:
                            pool.wait_ge(high_done, m.i * NG + n + 1)
                            nc.gpsimd.tensor_tensor(group(PL[m.u], n), group(PT, n), group(PH[m.u], n).bitcast(F32),
                                                    ALU.subtract).then_inc(low_pool, 1)
                run_heads(pool, heads, step)

            @block.tensor
            def _(pe):
                g.early.ready(pe)
                for n in range(NM):
                    for k in range(GM):
                        h = n * GM + k
                        mm = nc.tensor.matmul(g.bank[2 + n][:, k * KA:(k + 1) * KA], ws[0:D, h, 0:C], ws[0:D, h, C:C + KA],
                                              start=True, stop=True)
                        if query_bias:
                            mm = nc.tensor.matmul(g.bank[2 + n][0:KA, GM * KA + k:GM * KA + k + 1], ws[0:D, h, C:C + KA],
                                                  ws[0:D, h, C + KA:WV], start=True, stop=True)
                    mm.then_inc(pair_mm, 1)
                pe.wait_ge(pair_sb, NM)

                def step(at):
                    q, f, m, v, o = at(2), at(1), at(0), at(-1), at(-2)

                    def scores(j):
                        a, c = j // len(CW), j % len(CW)
                        if j == 0:
                            pe.wait_ge(q_hi_done, 2 * f.i + 2)
                            if isinstance(f.h, int) and f.h == 0:
                                pe.wait_ge(ctx_in[f.b % NS], 48 * (f.b // NS + 1))
                        after(pe, max_done, f.i * NJ + j - 1)
                        nc.tensor.matmul(p_s[j % 2][:, 0:CW[c]], q_hi[f.u][:, a * P:(a + 1) * P],
                                         hi_lo[f.b % NS][:, C0[c]:C0[c] + CW[c]], start=True, stop=True).then_inc(s_mm, 1)

                    def scores_t(n):
                        if n == 0:
                            pe.wait_ge(m_done, m.i + 1)
                        after(pe, exp_done, m.i * NG + (n - 1 if n >= 2 else -n))
                        for t in range(2 * n, min(2 * n + 2, CT)):
                            r = P if t < CT - 1 else LAST
                            out = p_st[n % 2][0:r, (t % 2) * T:(t % 2 + 1) * T]
                            nc.tensor.matmul(out, hi_lo[m.b % NS][:, t * P:t * P + r], q_hi[m.u][:], start=True, stop=False)
                            mm = nc.tensor.matmul(out, hi_one[m.b % NS][:, t * P:t * P + r], q_lo[m.u][:], start=False, stop=True)
                        mm.then_inc(st_mm, 1)

                    def values(t):
                        if t == 0:
                            after(pe, z_sb, v.i - 1)
                        if t % 2 == 0:
                            low_done(pe, v.i, t // 2)
                        r = P if t < CT - 1 else LAST
                        tk, hi, lo = tok[v.b % NS], PH[v.u][0:r, t, :], PL[v.u][0:r, t, :]
                        nc.tensor.matmul(p_z[v.u], tk[0:r, t, 0:2 * CC], hi, start=(t == 0), stop=(t == CT - 1), skip_group_check=True)
                        nc.tensor.matmul(p_z[v.u][0:CC, :], tk[0:r, t, 2 * CC:KV], hi, start=False, stop=False, skip_group_check=True)
                        mm = nc.tensor.matmul(p_z[v.u][0:KA, :], tk[0:r, t, 0:KA], lo, start=False, stop=(t == CT - 1), skip_group_check=True)
                        if t == CT - 1:
                            mm.then_inc(z_mm, 1)

                    for j in range(NJ):
                        if f:
                            scores(j)
                        if m and j < NG:
                            scores_t(j)
                        if v and j >= 2:
                            values(j - 2)
                        if o and j == 3:
                            pe.wait_ge(z_sb, o.i + 1)
                            after(pe, y_done, o.i)
                            pe.sem_inc(waits_taken, 1)
                            for a in range(QT):
                                mm = nc.tensor.matmul(p_o[:, a, :], zT[o.u][:, a * P:(a + 1) * P],
                                                      wvs[:, bass.ds(o.h, 1), :].rearrange("p a d -> p (a d)"), start=True, stop=True)
                            mm.then_inc(o_mm, 1)
                        if q and j == 4:
                            after(pe, m_done, q.i - 1)
                            after(pe, q_lo_done, q.i)
                            pe.wait_ge(w_set, q.i + 1)
                            pe.sem_inc(waits_taken, 1)
                            nc.tensor.matmul(p_qk[0:KR, :], mst[q.u][:, 0:KR], normT[:, 0, q.b * T:(q.b + 1) * T],
                                             start=True, stop=True).then_inc(qk_mm, 1)
                    if v:
                        for t in range(NJ - 2, VM):
                            values(t)
                    if f:
                        pe.wait_ge(negm_done, f.i + 1)
                        if key_bias and q:
                            pe.wait_ge(kb_done, q.i + 1)
                        for a in range(QT):
                            mm = nc.tensor.matmul(p_m[:, a * P:(a + 1) * P], negm[f.u][:, a:a + 1], g.ident[:], start=True, stop=True)
                        mm.then_inc(m_mm, 1)
                    if v:
                        for t in range(VM, CT):
                            values(t)
                run_heads(pe, heads, step)

            @block.scalar
            def _(act):
                def step(at):
                    q, m, o = at(2), at(0), at(-2)

                    def exps(n):
                        act.wait_ge(st_mm, m.i * NG + n + 1)
                        low_done(act, m.i - 1, n)
                        k = min(2, CT - 2 * n)
                        nc.scalar.activation(group(PT, n), p_st[n % 2][0:(P if k == 2 else LAST), 0:k * T], ACT.Exp,
                                             scale=scale).then_inc(exp_done, 1)

                    def high(n):
                        act.wait_ge(exp_done, m.i * NG + n + 1)
                        nc.scalar.copy(group(PH[m.u], n), group(PT, n)).then_inc(high_done, 1)
                    if m:
                        exps(0)
                    if o:
                        act.wait_ge(z_mm, o.i + 1)
                        nc.scalar.copy(zT[o.u][:], p_z[o.u]).then_inc(z_sb, 1)
                    if m:
                        after(act, z_mm, m.i - 1)
                        for n in range(1, NG):
                            exps(n)
                            if n < NG - 1:
                                high(n - 1)
                    if q:
                        act.wait_ge(qk_mm, q.i + 1)
                        after(act, st_mm, (q.i - 1) * NG)
                        for s in range(2):
                            dst = q_hi[q.u][s * CC:(s + 1) * CC, :]
                            if query_bias:
                                nc.scalar.activation(dst, p_qk[0:CC, :], ACT.Identity, bias=bms[0:CC, bass.ds(q.h, 1)]).then_inc(q_hi_done, 1)
                            else:
                                nc.scalar.copy(dst, p_qk[0:CC, :]).then_inc(q_hi_done, 1)
                    if m:
                        high(NG - 2)
                        high(NG - 1)
                run_heads(act, heads, step)

            @block.vector
            def _(dve):
                for n in range(NM):
                    dve.wait_ge(pair_mm, n + 1)
                    hs = slice(n * GM, (n + 1) * GM)
                    ins = nc.vector.tensor_copy(ms[:, hs, :], g.bank[2 + n][:, 0:GM * KA].rearrange("p (h k) -> p h k", k=KA))
                    if query_bias:
                        ins = nc.vector.tensor_copy(bms[:, hs], g.bank[2 + n][0:KA, GM * KA:GM * KA + GM])
                    ins.then_inc(pair_sb, 1)
                dve.wait_ge(pair_sb, NM)

                def step(at):
                    q, f, m, o = at(2), at(1), at(0), at(-2)

                    def low(n):
                        dve.wait_ge(high_done, m.i * NG + n + 1)
                        nc.vector.tensor_tensor(group(PL[m.u], n), group(PT, n), group(PH[m.u], n).bitcast(F32),
                                                ALU.subtract).then_inc(low_dve, 1)
                    for j in range(NJ):
                        if f:
                            dve.wait_ge(s_mm, f.i * NJ + j + 1)
                            nc.vector.tensor_reduce(mx[f.u][:, j:j + 1], p_s[j % 2][:, 0:CW[j % len(CW)]], AX.X,
                                                    ALU.max).then_inc(max_done, 1)
                        if o and j == 5:
                            dve.wait_ge(o_mm, o.i + 1)
                            nc.vector.reciprocal(rl[o.u][:], p_o[:, :, D]).then_inc(recip_done, 1)
                            dve.wait_ge(recip_done, o.i + 1)
                            for a in range(QT):
                                dst = y[:, o.b * QT + a, bass.ds(o.h * D, D)]
                                if add:
                                    ins = nc.vector.scalar_tensor_tensor(out=dst, in0=p_o[:, a, 0:D], scalar=rl[o.u][:, a:a + 1],
                                                                         in1=dst, op0=ALU.mult, op1=ALU.add)
                                else:
                                    ins = nc.vector.tensor_scalar(dst, p_o[:, a, 0:D], rl[o.u][:, a:a + 1], None, ALU.mult)
                            ins.then_inc(y_done, 1)
                        if m and j == 3:
                            low(BY_DVE[0])
                        if q and key_bias and j == 5:
                            dve.wait_ge(qk_mm, q.i + 1)
                            nc.vector.tensor_scalar(kb[q.u][CC:KA, :], p_qk[CC:KA, :], bms[CC:KA, bass.ds(q.h, 1)], None,
                                                    ALU.add).then_inc(kb_done, 1)
                    if f:
                        dve.wait_ge(max_done, f.i * NJ + NJ)
                        nc.vector.tensor_reduce(negm[f.u][:], mx[f.u][:].rearrange("p (a c) -> p a c", a=QT), AX.X,
                                                ALU.max, negate=True).then_inc(negm_done, 1)
                        dve.wait_ge(m_mm, f.i + 1)
                        row = q_lo[f.u][CC:KA, :]
                        if key_bias:
                            dve.wait_ge(kb_done, f.i + 1)
                            nc.vector.tensor_tensor(top[CC:KA, :], p_m, kb[f.u][CC:KA, :], ALU.subtract).then_inc(top_done, 1)
                            dve.wait_ge(top_done, f.i + 1)
                            nc.vector.tensor_tensor(row, top[CC:KA, :], kb[f.u][CC:KA, :], ALU.add).then_inc(m_done, 1)
                        else:
                            nc.vector.tensor_copy(row, p_m).then_inc(m_done, 1)
                    if q:
                        dve.wait_ge(q_hi_done, 2 * q.i + 2)
                        o, hi = q_lo[q.u][0:CC, :], q_hi[q.u][0:CC, :].bitcast(F32)
                        if query_bias:
                            nc.vector.scalar_tensor_tensor(out=o, in0=p_qk[0:CC, :], scalar=bms[0:CC, bass.ds(q.h, 1)], in1=hi,
                                                           op0=ALU.add, op1=ALU.subtract).then_inc(q_lo_done, 1)
                        else:
                            nc.vector.tensor_tensor(o, p_qk[0:CC, :], hi, ALU.subtract).then_inc(q_lo_done, 1)
                    if m:
                        low(BY_DVE[1])
                run_heads(dve, heads, step)
                dve.wait_ge(y_done, B * heads)


def self_weights(g, sb, name, bqk, wv, bv, D):
    wvs = sb(name + "_wv", [C, H * D])
    g.early.load(wvs[:], wv)
    bvs = bs = None
    if bv is not None:
        bvs, bs = sb(name + "_bv", [P, H * D]), sb(name + "_b", [96, H, 2])
        g.early.load(bvs[:], rows(bv))
        g.early.load(bs[:], bqk)
    return wvs, bvs, bs


def self_attention(nc, name, g, wqk, weights, qsrcT, kvsrcT, y, D, scale, causal):
    D1 = D + 1
    DP = 32
    R = 3 * DP
    wvs, bvs, bs = weights
    with Space(nc, name) as sb:
        V = sb("V", [P, NT, H, D1])
        sums = sb("sums", [P, D1])
        mask = sb("mask", [P, 2, P]) if causal else None
        mask_r = sb("mask_r", [P, 2, P], F32R) if causal else None
        ident_r = sb("ident_r", [P, P], F32R) if causal else None
        wst = [sb(f"wst{s}", [C, 2, R]) for s in range(2)]
        vst = [sb(f"vst{s}", [P, QT, D1]) for s in range(2)]
        qst = [sb(f"qst{s}", [R + 1, T], F32R) for s in range(2)]
        kst = [sb(f"kst{s}", [R + 1, T], F32R) for s in range(2)]
        negm = [sb(f"negm{s}", [P, QT]) for s in range(2)]
        PT = [sb(f"PT{s}", [P, QT, T]) for s in range(2)]
        PM = [sb(f"PM{s}", [P, QT, P]) for s in range(2)] if not causal else None
        PS = [sb(f"PS{s}", [P, T]) for s in range(2)] if not causal else None
        zT = [sb(f"zT{s}", [D1, T]) for s in range(2)]
        rl = [sb(f"rl{s}", [P, QT]) for s in range(2)]
        p_qk = [[g.bank[n][0:R, k * T:(k + 1) * T] for k in range(2)] for n in (0, 3)]
        p_m = [g.bank[6 + s][64:65, T:2 * T] for s in range(2)]
        p_o = g.bank[1][:, T:T + QT * D1].rearrange("p (a d) -> p a d", d=D1)
        p_s, p_st = g.bank[2], [g.bank[4], g.bank[5]]
        p_z = [g.bank[6 + s][0:D1, 0:T] for s in range(2)]
        names = ["wqk_in0", "wqk_in1", "consts", "v_mm", "v_sb", "v_set", "waits_taken", "qk_mm", "hi_done", "lo_done", "s_mm",
                 "negm_done", "m_mm", "m_done", "st_mm", "exp_done", "select_done", "z_mm", "z_sb", "o_mm", "recip_done", "y_done"]
        with stage(nc, name, *names) as (
                block, wqk_in0, wqk_in1, consts, v_mm, v_sb, v_set, waits_taken, qk_mm, hi_done, lo_done, s_mm,
                negm_done, m_mm, m_done, st_mm, exp_done, select_done, z_mm, z_sb, o_mm, recip_done, y_done):
            wqk_in = [wqk_in0, wqk_in1]

            @block.sync
            def _(sp):
                def step(at):
                    q = at(2)
                    if q:
                        after(sp, qk_mm, q.i - 1)
                        sp.dma_start(wst[q.u][:], wqk[bass.ds(q.h, 1), :, :, :].rearrange("a c k r -> (a c) k r")).then_inc(wqk_in[q.u], 16)
                run_heads(sp, H, step)

            @block.gpsimd
            def _(pool):
                nc.gpsimd.memset(sums[:, 0:D], 0.0).then_inc(consts, 1)
                pool.wait_ge(consts, 1)
                nc.gpsimd.memset(sums[:, D:D1], 1.0).then_inc(consts, 1)
                pool.wait_ge(consts, 2)
                if causal:
                    nc.gpsimd.memset(mask[:], 0.0).then_inc(consts, 1)
                    pool.wait_ge(consts, 3)
                    for k, sign in ((0, 1), (1, -1)):
                        nc.gpsimd.affine_select(out=mask[:, k, :], in_=mask[:, k, :], compare_op=ALU.is_ge, fill=-1e30, base=0,
                                                pattern=[[-sign, P]], channel_multiplier=sign).then_inc(consts, 1)
                        pool.wait_ge(consts, 4 + k)
                    nc.gpsimd.tensor_copy(mask_r[:], mask[:]).then_inc(consts, 1)
                    pool.wait_ge(consts, 6)
                    nc.gpsimd.tensor_copy(ident_r[:], g.ident[:]).then_inc(consts, 1)
                    pool.wait_ge(consts, 7)
                pool.wait_ge(v_sb, NT)

                def step(at):
                    m = at(0)
                    if m:
                        after(pool, z_mm, m.i - 1)
                        nc.gpsimd.tensor_copy(vst[m.u][:], V[:, m.b * QT:(m.b + 1) * QT, bass.ds(m.h, 1), :]
                                              .rearrange("p t a d -> p t (a d)")).then_inc(v_set, 1)
                        if not causal:
                            pool.wait_ge(exp_done, m.i + 1)
                            pool.sem_inc(waits_taken, 1)
                            for t in range(QT):
                                nc.gpsimd.affine_select(out=PM[m.u][:, t, :], in_=PT[m.u][:, t, t * P:(t + 1) * P], compare_op=ALU.is_gt,
                                                        fill=0.0, base=0, pattern=[[-1, P]], channel_multiplier=1).then_inc(select_done, 1)
                            nc.gpsimd.tensor_tensor(PS[m.u][:], PT[m.u][:, 0, :], PT[m.u][:, 1, :], ALU.add).then_inc(select_done, 1)
                run_heads(pool, H, step)

            @block.tensor
            def _(pe):
                g.early.ready(pe)
                for n in range(NT):
                    if n >= 2:
                        pe.wait_ge(v_sb, n - 1)
                    nc.tensor.matmul(g.bank[2 + n % 2][:, 0:H * D], kvsrcT[:, 0, n * P:(n + 1) * P], wvs[:],
                                     start=True, stop=True).then_inc(v_mm, 1)
                pe.wait_ge(v_sb, NT + 2)
                pe.wait_ge(consts, 7 if causal else 2)

                def step(at):
                    q, f, m, v, o = at(2), at(1), at(0), at(-1), at(-2)
                    if q:
                        pe.wait_ge(wqk_in[q.u], q.turn * 16 + 16)
                        after(pe, lo_done, 2 * q.i - 2)
                        pe.sem_inc(waits_taken, 1)
                        for k, src in ((0, qsrcT), (1, kvsrcT)):
                            mm = nc.tensor.matmul(p_qk[q.u][k], wst[q.u][:, k, :], src[:, 0, q.b * T:(q.b + 1) * T], start=True, stop=True)
                        mm.then_inc(qk_mm, 1)
                    if m:
                        pe.wait_ge(negm_done, m.i + 1)
                        after(pe, m_done, m.i - 1)
                        pe.sem_inc(waits_taken, 1)
                        for a in range(QT):
                            mm = nc.tensor.matmul(p_m[m.u][:, a * P:(a + 1) * P], negm[m.u][:, a:a + 1], g.ident[:], start=True, stop=True)
                        mm.then_inc(m_mm, 1)
                    if v:
                        pe.wait_ge(v_set, v.i + 1)
                        pe.wait_ge(exp_done, v.i + 1)
                        if not causal:
                            pe.wait_ge(select_done, 3 * v.i + 2)
                        after(pe, z_sb, v.i - 1)
                        pe.sem_inc(waits_taken, 1)
                        z = p_z[v.u]
                        if causal:
                            nc.tensor.matmul(z[:, P:T], vst[v.u][:, 1, :], PT[v.u][:, 1, P:T], start=True, stop=False,
                                             skip_group_check=True)
                            mm = nc.tensor.matmul(z, vst[v.u][:, 0, :], PT[v.u][:, 0, :], start=False, stop=True, skip_group_check=True)
                        else:
                            nc.tensor.matmul(z[:, 0:P], vst[v.u][:, 0, :], PM[v.u][:, 0, :], start=True, stop=False, skip_group_check=True)
                            nc.tensor.matmul(z[:, 0:P], vst[v.u][:, 1, :], PT[v.u][:, 1, 0:P], start=False, stop=False, skip_group_check=True)
                            nc.tensor.matmul(z[:, P:T], vst[v.u][:, 1, :], PM[v.u][:, 1, :], start=False, stop=False, skip_group_check=True)
                            pe.wait_ge(select_done, 3 * v.i + 3)
                            pe.sem_inc(waits_taken, 1)
                            mm = nc.tensor.matmul(z, sums[:], PS[v.u][:], start=False, stop=True, skip_group_check=True)
                        mm.then_inc(z_mm, 1)
                    if m:
                        pe.wait_ge(m_done, m.i + 1)
                        after(pe, exp_done, m.i - 1)
                        pe.sem_inc(waits_taken, 1)
                        for t in range(QT):
                            q0 = t * P if causal else 0
                            out = p_st[m.u][:, t * T + q0:(t + 1) * T]
                            if causal:
                                nc.tensor.matmul(out[:, 0:P], ident_r[:], mask_r[:, 1, :], start=True, stop=False,
                                                 skip_group_check=True)
                            mm = nc.tensor.matmul(out, kst[m.u][:, t * P:(t + 1) * P], qst[m.u][:, q0:T],
                                                  start=not causal, stop=True, skip_group_check=True)
                        mm.then_inc(st_mm, 1)
                    if f:
                        pe.wait_ge(lo_done, 2 * f.i + 2)
                        after(pe, negm_done, f.i)
                        pe.sem_inc(waits_taken, 1)
                        for a in range(QT):
                            w = (a + 1) * P if causal else T
                            out = p_s[:, a * T:a * T + w]
                            if causal:
                                nc.tensor.matmul(out[:, a * P:w], ident_r[:], mask_r[:, 0, :], start=True, stop=False,
                                                 skip_group_check=True)
                            mm = nc.tensor.matmul(out, qst[f.u][0:R, a * P:(a + 1) * P], kst[f.u][0:R, 0:w],
                                                  start=not causal, stop=True, skip_group_check=True)
                        mm.then_inc(s_mm, 1)
                    if o:
                        pe.wait_ge(z_sb, o.i + 1)
                        after(pe, y_done, o.i)
                        pe.sem_inc(waits_taken, 1)
                        for a in range(QT):
                            mm = nc.tensor.transpose(p_o[:, a, :], zT[o.u][:, a * P:(a + 1) * P], g.ident[0:D1, 0:D1])
                        mm.then_inc(o_mm, 1)
                run_heads(pe, H, step)

            @block.scalar
            def _(act):
                g.early.ready(act)

                def step(at):
                    q, m = at(2), at(0)
                    if m:
                        act.wait_ge(st_mm, m.i + 1)
                        after(act, z_mm, m.i - 1)
                        if not causal:
                            after(act, select_done, 3 * (m.i - 1))
                            nc.scalar.activation(PT[m.u][:].rearrange("p t q -> p (t q)"), p_st[m.u][:], ACT.Exp, scale=scale)\
                                .then_inc(exp_done, 1)
                        else:
                            nc.scalar.activation(PT[m.u][:, 0, :], p_st[m.u][:, 0:T], ACT.Exp, scale=scale)
                            nc.scalar.activation(PT[m.u][:, 1, P:T], p_st[m.u][:, T + P:2 * T], ACT.Exp, scale=scale)\
                                .then_inc(exp_done, 1)
                    if q:
                        act.wait_ge(qk_mm, q.i + 1)
                        after(act, st_mm, q.i - 1)
                        for k, dst in ((0, qst), (1, kst)):
                            if bs is None:
                                nc.scalar.copy(dst[q.u][0:R, :], p_qk[q.u][k]).then_inc(hi_done, 1)
                            else:
                                nc.scalar.activation(dst[q.u][0:R, :], p_qk[q.u][k], ACT.Identity,
                                                     bias=bs[:, bass.ds(q.h, 1), k]).then_inc(hi_done, 1)
                run_heads(act, H, step)

            @block.vector
            def _(dve):
                nc.vector.memset(V[:, :, :, D:D1], 1.0 if causal else 0.0)
                g.early.ready(dve)
                for n in range(NT):
                    dve.wait_ge(v_mm, n + 1)
                    o = V[:, n, :, 0:D]
                    i_ = g.bank[2 + n % 2][:, 0:H * D].rearrange("p (h d) -> p h d", d=D)
                    if bvs is None:
                        nc.vector.tensor_copy(o, i_).then_inc(v_sb, 1)
                    else:
                        nc.vector.tensor_tensor(o, i_, bvs[:].rearrange("p (h d) -> p h d", d=D), ALU.add).then_inc(v_sb, 1)
                for s in range(2):
                    nc.vector.memset(kst[s][R:R + 1, :].bitcast(F32), 1.0).then_inc(v_sb, 1)

                def step(at):
                    f, m, o = at(1), at(0), at(-2)
                    if m:
                        dve.wait_ge(m_mm, m.i + 1)
                        nc.vector.tensor_copy(qst[m.u][R:R + 1, :], p_m[m.u]).then_inc(m_done, 1)
                    if f:
                        dve.wait_ge(hi_done, 2 * f.i + 2)
                        for k, dst, blk in ((0, qst, slice(DP, 2 * DP)), (1, kst, slice(2 * DP, R))):
                            hi = dst[f.u][blk, :].bitcast(F32)
                            if bs is None:
                                nc.vector.tensor_tensor(dst[f.u][blk, :], p_qk[f.u][k][blk, :], hi, ALU.subtract).then_inc(lo_done, 1)
                            else:
                                nc.vector.scalar_tensor_tensor(out=dst[f.u][blk, :], in0=p_qk[f.u][k][blk, :],
                                                               scalar=bs[blk, bass.ds(f.h, 1), k], in1=hi,
                                                               op0=ALU.add, op1=ALU.subtract).then_inc(lo_done, 1)
                    if o:
                        dve.wait_ge(z_mm, o.i + 1)
                        nc.vector.tensor_copy(zT[o.u][:], p_z[o.u]).then_inc(z_sb, 1)
                    if f:
                        dve.wait_ge(s_mm, f.i + 1)
                        if causal:
                            nc.vector.tensor_reduce(negm[f.u][:, 0:1], p_s[:, 0:P], AX.X, ALU.max, negate=True)
                            nc.vector.tensor_reduce(negm[f.u][:, 1:2], p_s[:, T:2 * T], AX.X, ALU.max,
                                                    negate=True).then_inc(negm_done, 1)
                        else:
                            nc.vector.tensor_reduce(negm[f.u][:], p_s[:].rearrange("p (a t) -> p a t", t=T), AX.X,
                                                    ALU.max, negate=True).then_inc(negm_done, 1)
                    if o:
                        dve.wait_ge(o_mm, o.i + 1)
                        nc.vector.reciprocal(rl[o.u][:], p_o[:, :, D]).then_inc(recip_done, 1)
                        dve.wait_ge(recip_done, o.i + 1)
                        dst = y[:, o.b * QT:(o.b + 1) * QT, bass.ds(o.h * D, D)]
                        nc.vector.tensor_tensor(dst, p_o[:, :, 0:D], rl[o.u][:].rearrange("p (a d) -> p a d", d=1).to_broadcast([P, QT, D]),
                                                ALU.mult).then_inc(y_done, 1)
                run_heads(dve, H, step)
                dve.wait_ge(y_done, B * H)


def add_tokens(nc, name, dst, src):
    with stage(nc, name, "added") as (block, added):
        @block.vector
        def _(dve):
            nc.vector.tensor_tensor(dst[:], dst[:], src[:], ALU.add).then_inc(added, 1)
            dve.wait_ge(added, 1)


def linear_weights(g, sb, name, kc, w, bias):
    ws, bs = sb(name + "_w", [P, kc, C]), sb(name + "_b", [P, C])
    g.early.load(ws[:], w.rearrange("(k p) c -> p k c", p=P))
    g.early.load(bs[:], rows(bias))
    return ws, bs


def linear(nc, name, g, srcT, kc, weights, dst):
    ws, bs = weights
    with stage(nc, name, "product", "step") as (block, product, step):
        @block.tensor
        def _(pe):
            g.early.ready(pe)
            for n in range(NT):
                for k in range(kc):
                    mm = nc.tensor.matmul(g.bank[n // 4][:, n % 4 * P:(n % 4 + 1) * P], srcT[:, k, n * P:(n + 1) * P],
                                          ws[:, k, :], start=(k == 0), stop=(k == kc - 1))
                if n % 4 == 3:
                    mm.then_inc(product, 1)

        @block.vector
        def _(dve):
            link = Link(dve, step)
            g.early.ready(dve)
            link(nc.vector.tensor_tensor(dst[:], dst[:], bs[:].rearrange("p (a c) -> p a c", a=1).to_broadcast([P, NT, C]), ALU.add))
            for n in range(2):
                dve.wait_ge(product, n + 1)
                o = dst[:, 4 * n:4 * n + 4, :]
                link(nc.vector.tensor_tensor(o, o, g.bank[n][:].rearrange("p (a c) -> p a c", c=C), ALU.add))


def hidden_weights(g, sb, name, fc, w, bias):
    ws, bs = sb(name + "_w", [P, fc * P]), sb(name + "_b", [P, fc])
    g.early.load(ws[:], w)
    g.early.load(bs[:], bias)
    return ws, bs


def hidden(nc, name, g, srcT, weights, dstT, fc):
    ws, bs = weights
    with stage(nc, name, "product", "done") as (block, product, done):
        @block.tensor
        def _(pe):
            g.early.ready(pe)
            for n in range(2 * fc):
                f, half = n // 2, n % 2
                if n >= 4:
                    pe.wait_ge(done, n - 3)
                nc.tensor.matmul(g.bank[n % 4][:], ws[:, f * P:(f + 1) * P], srcT[:, 0, half * 512:half * 512 + 512],
                                 start=True, stop=True).then_inc(product, 1)

        @block.scalar
        def _(act):
            g.early.ready(act)
            for n in range(2 * fc):
                f, half = n // 2, n % 2
                act.wait_ge(product, n + 1)
                nc.scalar.activation(dstT[:, f, half * 512:half * 512 + 512], g.bank[n % 4][:], ACT.Gelu,
                                     bias=bs[:, f:f + 1]).then_inc(done, 1)


def experts(nc, name, g, srcT, w1, b1, w2, wts, dst, kind, FC, FP=P):
    gated = kind == "silu"
    func = {"silu": ACT.Silu, "relu": ACT.Relu, "gelu": ACT.Gelu}[kind]
    W1 = FC * FP * (2 if gated else 1)
    NW = 32 if b1 is None else 48
    NB = 2 if gated else 4
    with Space(nc, name) as sb:
        w1s = [sb(f"w1_{s}", [P, W1]) for s in range(2)]
        w2s = [sb(f"w2_{s}", [FP, FC * C]) for s in range(2)]
        b1s = [sb(f"b1_{s}", [FP, FC]) for s in range(2)] if b1 is not None else None
        hT = sb("hT", [FP, FC, B * T])
        sg = [sb(f"sg{s}", [FP, 512]) for s in range(2)] if gated else None
        p_up = [g.bank[s] for s in range(4)]
        p_dn = [g.bank[4], g.bank[5]]
        with stage(nc, name, "w_in0", "w_in1", "up_mm", "up_free", "gate_done", "h_done", "down_mm", "down_free") as (
                block, w_in0, w_in1, up_mm, up_free, gate_done, h_done, down_mm, down_free):
            w_in = [w_in0, w_in1]
            NH = 2 * FC

            @block.sync
            def _(sp):
                with sp.Fori(0, E // 2) as k:
                    for u in range(2):
                        sp.wait_ge(down_mm, k * 4 + 2 * u + 1)
                        e = bass.ds(k * 2 + u, 1)
                        sp.dma_start(w1s[u][:], w1[e, :, :].rearrange("a k t -> (a k) t")).then_inc(w_in[u], 16)
                        sp.dma_start(w2s[u][:], w2[e, :, :].rearrange("a k t -> (a k) t")).then_inc(w_in[u], 16)
                        if b1 is not None:
                            sp.dma_start(b1s[u][:], b1[e, :, :].rearrange("a k t -> (a k) t")).then_inc(w_in[u], 16)

            @block.tensor
            def _(pe):
                pe.sem_inc(down_mm, 3)
                with pe.Fori(0, E // 2) as k:
                    for u in range(2):
                        e = k * 2 + u
                        pe.wait_ge(w_in[u], (k + 1) * NW)
                        for n in range(NH):
                            half, f = n // FC, n % FC
                            x = srcT[:, 0, half * 512:half * 512 + 512]
                            pe.wait_ge(up_free, e * NH + n + 1)
                            s = n % NB
                            mm = nc.tensor.matmul(p_up[s][0:FP, :], w1s[u][:, f * FP:(f + 1) * FP], x, start=True, stop=True)
                            if gated:
                                mm = nc.tensor.matmul(p_up[2 + s][0:FP, :], w1s[u][:, (FC + f) * FP:(FC + f + 1) * FP], x,
                                                      start=True, stop=True)
                            mm.then_inc(up_mm, 1)
                        for half in range(2):
                            pe.wait_ge(h_done, e * NH + (half + 1) * FC + 1)
                            pe.wait_ge(down_free, e * 2 + half + 1)
                            for n in range(4):
                                for f in range(FC):
                                    t = (half * 4 + n) * P
                                    mm = nc.tensor.matmul(p_dn[half][:, n * P:(n + 1) * P], hT[:, f, t:t + P],
                                                          w2s[u][:, f * C:(f + 1) * C], start=(f == 0), stop=(f == FC - 1))
                            mm.then_inc(down_mm, 1)

            @block.scalar
            def _(act):
                if not gated:
                    act.sem_inc(up_free, NB)
                    act.sem_inc(h_done, 1)
                with act.Fori(0, E // 2) as k:
                    for u in range(2):
                        e = k * 2 + u
                        for n in range(NH):
                            half, f = n // FC, n % FC
                            o = hT[:, f, half * 512:half * 512 + 512]
                            act.wait_ge(up_mm, e * NH + n + 1)
                            if gated:
                                if n < 2:
                                    act.wait_ge(h_done, e * NH + 1)
                                else:
                                    act.wait_ge(h_done, e * NH + n)
                                nc.scalar.activation(sg[n % 2][:], p_up[n % NB][0:FP, :], func).then_inc(gate_done, 1)
                            else:
                                if f == 0:
                                    act.wait_ge(down_mm, e * 2 + half + 2)
                                bias = b1s[u][:, f:f + 1] if b1 is not None else 0.0
                                nc.scalar.activation(o, p_up[n % NB][0:FP, :], func, bias=bias).then_inc(h_done, 1)
                                act.wait_ge(h_done, e * NH + n + 2)
                                act.sem_inc(up_free, 1)

            @block.vector
            def _(dve):
                dve.sem_inc(down_free, 2)
                if gated:
                    dve.sem_inc(up_free, NB)
                    dve.sem_inc(h_done, 1)
                with dve.Fori(0, E // 2) as k:
                    for u in range(2):
                        e = k * 2 + u
                        if gated:
                            for n in range(NH):
                                half, f = n // FC, n % FC
                                o = hT[:, f, half * 512:half * 512 + 512]
                                dve.wait_ge(gate_done, e * NH + n + 1)
                                if f == 0:
                                    dve.wait_ge(down_mm, e * 2 + half + 2)
                                nc.vector.tensor_tensor(o, sg[n % 2][:], p_up[2 + n % NB][0:FP, :], ALU.mult).then_inc(h_done, 1)
                                dve.wait_ge(h_done, e * NH + n + 2)
                                dve.sem_inc(up_free, 1)
                        for half in range(2):
                            dve.wait_ge(down_mm, e * 2 + half + 4)
                            dve.wait_ge(down_free, e * 2 + half + 1)
                            for n in range(4):
                                t = half * 4 + n
                                ins = nc.vector.scalar_tensor_tensor(out=dst[:, t, :], in0=p_dn[half][:, n * P:(n + 1) * P],
                                                                     scalar=wts[:, t, bass.ds(e, 1)], in1=dst[:, t, :],
                                                                     op0=ALU.mult, op1=ALU.add)
                            ins.then_inc(down_free, 1)


def expert_biases(nc, name, g, wts, b2, dst):
    with Space(nc, name) as sb:
        wT = sb("wT", [E, B * T])
        b2s = sb("b2", [E, C])
        with stage(nc, name, "in_", "turned", "kept", "product", "step") as (block, in_, turned, kept, product, step):
            @block.sync
            def _(sp):
                sp.dma_start(b2s[:], b2).then_inc(in_, 16)

            @block.tensor
            def _(pe):
                for n in range(NT):
                    mm = nc.tensor.transpose(g.bank[n // 4][0:E, n % 4 * P:(n % 4 + 1) * P], wts[:, n, :], g.ident[:])
                    mm.then_inc(turned, 1)
                pe.wait_ge(kept, 2)
                pe.wait_ge(in_, 16)
                for n in range(NT):
                    nc.tensor.matmul(g.bank[2 + n // 4][:, n % 4 * P:(n % 4 + 1) * P], wT[:, n * P:(n + 1) * P], b2s[:],
                                     start=True, stop=True).then_inc(product, 1)

            @block.vector
            def _(dve):
                link = Link(dve, step)
                for n in range(2):
                    dve.wait_ge(turned, 4 * n + 4)
                    nc.vector.tensor_copy(wT[:, n * 512:(n + 1) * 512], g.bank[n][0:E, :]).then_inc(kept, 1)
                for n in range(2):
                    dve.wait_ge(product, 4 * n + 4)
                    o = dst[:, 4 * n:4 * n + 4, :]
                    link(nc.vector.tensor_tensor(o, o, g.bank[2 + n][:].rearrange("p (a c) -> p a c", c=C), ALU.add))


class Picks:

    def __init__(self, nc, sb, link, n):
        self.nc, self.link, self.n = nc, link, n
        self.rev = sb("rev", [P, 1, E])
        self.r = sb("r", [P, n, E])
        self.rm = sb("rm", [P, n, 1])
        for e in range(E):
            link(nc.vector.memset(self.rev[:, :, e:e + 1], float(E - e)))

    def wide(self, ap):
        return ap[:].to_broadcast([P, self.n, E])

    def first(self, onehot, top, s):
        nc, link = self.nc, self.link
        link(nc.vector.tensor_reduce(top[:], s[:], AX.X, ALU.max))
        link(nc.vector.tensor_tensor(self.r[:], s[:], self.wide(top), ALU.is_equal))
        link(nc.vector.tensor_tensor(self.r[:], self.r[:], self.wide(self.rev), ALU.mult))
        link(nc.vector.tensor_reduce(self.rm[:], self.r[:], AX.X, ALU.max))
        link(nc.vector.tensor_tensor(onehot[:], self.r[:], self.wide(self.rm), ALU.is_equal))

    def without(self, out, s, onehot):
        nc, link = self.nc, self.link
        link(nc.vector.tensor_scalar(self.r[:], onehot[:], -1.0, 1.0, ALU.mult, ALU.add))
        link(nc.vector.tensor_tensor(out[:], s[:], self.r[:], ALU.mult))
        link(nc.vector.scalar_tensor_tensor(out=out[:], in0=onehot[:], scalar=LOWEST, in1=out[:], op0=ALU.mult, op1=ALU.add))


def router(nc, name, g, kind, srcT, weights, wts):
    n = B if kind == "batch" else NT
    with Space(nc, name) as sb:
        wrs, brs = weights
        s = sb("s", [P, n, E])
        s2 = sb("s2", [P, n, E])
        oh1, oh2 = sb("oh1", [P, n, E]), sb("oh2", [P, n, E])
        m1, m2 = sb("m1", [P, n, 1]), sb("m2", [P, n, 1])
        d, ex = sb("d", [P, 2, n, E]), sb("ex", [P, 2, n, E])
        t = sb("t", [P, n, E])
        u1, u2 = sb("u1", [P, n, 1]), sb("u2", [P, n, 1])
        mean = sb("mean", [P, B])
        meanw = sb("meanw", [P, B, P])
        with stage(nc, name, "mean_done", "logits", "exp_in", "exp_out", "step") as (
                block, mean_done, logits, exp_in, exp_out, step):
            @block.tensor
            def _(pe):
                g.early.ready(pe)
                if kind == "batch":
                    pe.wait_ge(mean_done, 1)
                for i in range(n):
                    lhsT = meanw[:, i, :] if kind == "batch" else srcT[:, 0, i * P:(i + 1) * P]
                    nc.tensor.matmul(g.bank[0][:, i * E:(i + 1) * E], lhsT, wrs[:], start=True, stop=True).then_inc(logits, 1)

            @block.scalar
            def _(act):
                for k in range({"mixer": 2, "top2": 1, "batch": 2}[kind]):
                    act.wait_ge(exp_in, k + 1)
                    i_, o = (d[:, k], ex[:, k])
                    if kind == "mixer" or (kind == "batch" and k == 0):
                        nc.scalar.activation(o, i_, ACT.Exp).then_inc(exp_out, 1)
                    else:
                        nc.scalar.activation(u2[:], u1[:], ACT.Exp).then_inc(exp_out, 1)

            @block.vector
            def _(dve):
                link = Link(dve, step)
                v = nc.vector
                pick = Picks(nc, sb, link, n)
                wide = pick.wide
                if kind == "batch":
                    link(v.tensor_reduce(mean[:], srcT[:].rearrange("p a (b t) -> p (a b) t", b=B), AX.X, ALU.add))
                    link(v.tensor_scalar(mean[:], mean[:], 1.0 / T, None, ALU.mult))
                    link(v.tensor_copy(meanw[:], mean[:].rearrange("p (b a) -> p b a", a=1).to_broadcast([P, B, P])))
                    dve.sem_inc(mean_done, 1)
                dve.wait_ge(logits, n)
                link(v.tensor_copy(s[:], g.bank[0][:, 0:n * E].rearrange("p (n e) -> p n e", e=E)))
                if kind == "mixer":
                    def near(k, sc, top):
                        link(v.tensor_tensor(d[:, k], sc[:], wide(top), ALU.subtract))
                        dve.sem_inc(exp_in, 1)
                        link(v.scalar_tensor_tensor(out=t[:], in0=s[:], scalar=-1.0, in1=s[:], op0=ALU.mult, op1=ALU.max))
                        link(v.tensor_tensor(t[:], t[:], wide(top), ALU.max))
                        link(v.tensor_scalar(t[:], t[:], 2.0 * 0.01, None, ALU.mult))
                        link(v.tensor_tensor(s2[:], wide(top), s[:], ALU.subtract))
                        link(v.tensor_tensor(t[:], s2[:], t[:], ALU.is_le))

                    def gate(k, u):
                        dve.wait_ge(exp_out, k + 1)
                        link(v.tensor_tensor(t[:], t[:], ex[:, k], ALU.mult))
                        link(v.tensor_reduce(u[:], t[:], AX.X, ALU.add))
                        link(v.reciprocal(u[:], u[:]))
                    pick.first(oh1, m1, s)
                    near(0, s, m1)
                    gate(0, u1)
                    pick.without(s2, s, oh1)
                    pick.first(oh2, m2, s2)
                    near(1, s2, m2)
                    gate(1, u2)
                    link(v.tensor_tensor(oh1[:], oh1[:], wide(u1), ALU.mult))
                    link(v.tensor_tensor(oh2[:], oh2[:], wide(u2), ALU.mult))
                    link(v.tensor_tensor(wts[:], oh1[:], oh2[:], ALU.add))
                    return
                if kind == "batch":
                    g.early.ready(dve)
                    link(v.tensor_tensor(s[:], s[:], wide(brs), ALU.add))
                    link(v.tensor_reduce(m1[:], s[:], AX.X, ALU.max))
                    link(v.tensor_tensor(d[:, 0], s[:], wide(m1), ALU.subtract))
                    dve.sem_inc(exp_in, 1)
                    dve.wait_ge(exp_out, 1)
                    link(v.tensor_reduce(u1[:], ex[:, 0], AX.X, ALU.add))
                    link(v.reciprocal(u1[:], u1[:]))
                    link(v.tensor_tensor(s[:], ex[:, 0], wide(u1), ALU.mult))
                pick.first(oh1, m1, s)
                pick.without(s2, s, oh1)
                pick.first(oh2, m2, s2)
                link(v.tensor_tensor(u1[:], m2[:], m1[:], ALU.subtract))
                dve.sem_inc(exp_in, 1)
                dve.wait_ge(exp_out, 2 if kind == "batch" else 1)
                link(v.tensor_scalar(u1[:], u2[:], 1.0, None, ALU.add))
                link(v.reciprocal(u1[:], u1[:]))
                link(v.tensor_tensor(u2[:], u2[:], u1[:], ALU.mult))
                if kind == "top2":
                    link(v.tensor_scalar(u1[:], u1[:], 0.5, None, ALU.mult))
                    link(v.tensor_scalar(u2[:], u2[:], 0.5, None, ALU.mult))
                link(v.tensor_tensor(oh1[:], oh1[:], wide(u1), ALU.mult))
                link(v.tensor_tensor(oh2[:], oh2[:], wide(u2), ALU.mult))
                if kind == "batch":
                    for a in range(QT):
                        link(v.tensor_tensor(wts[:].rearrange("p (b a) e -> p b a e", a=QT)[:, :, a, :], oh1[:], oh2[:], ALU.add))
                else:
                    link(v.tensor_tensor(wts[:], oh1[:], oh2[:], ALU.add))


def expert_choice(nc, name, g, srcT, wrs, wts, keep):
    with Space(nc, name) as sb:
        s = sb("s", [P, NT, E])
        top = sb("top", [P, NT, 1])
        pr = sb("pr", [P, NT, E])
        prw = sb("prw", [P, 2, E, QT, P])
        prt = sb("prt", [P, 2, E, T])
        before = sb("before", [P, QT, T])
        cmp_ = sb("cmp", [P, 3, T])
        ahead = sb("ahead", [P, 2, E, T])
        rank = sb("rank", [P, NT, E])
        with stage(nc, name, "logits", "exp_in", "exp_out", "made", "wide", "spread", "compared", "compares", "step") as (
                block, logits, exp_in, exp_out, made, wide_done, spread, compared, compares, step):
            @block.gpsimd
            def _(pool):
                nc.gpsimd.memset(before[:], 1.0).then_inc(made, 1)
                pool.wait_ge(made, 1)
                nc.gpsimd.affine_select(out=before[:], in_=before[:], compare_op=ALU.is_gt, fill=0.0, base=0,
                                        pattern=[[P, QT], [-1, T]], channel_multiplier=1).then_inc(made, 1)

            @block.tensor
            def _(pe):
                g.early.ready(pe)
                for i in range(NT):
                    nc.tensor.matmul(g.bank[0][:, i * E:(i + 1) * E], srcT[:, 0, i * P:(i + 1) * P], wrs[:],
                                     start=True, stop=True).then_inc(logits, 1)
                for b in range(B):
                    pe.wait_ge(wide_done, b + 1)
                    for e in range(E):
                        i = b * E + e
                        if i >= 4:
                            pe.wait_ge(spread, i - 3)
                        for a in range(QT):
                            mm = nc.tensor.matmul(g.bank[1 + i % 4][:, a * P:(a + 1) * P], prw[:, b % 2, e, a, :], g.ident[:],
                                                  start=True, stop=True)
                        mm.then_inc(compared, 1)

            @block.scalar
            def _(act):
                act.wait_ge(exp_in, 1)
                nc.scalar.activation(pr[:], s[:], ACT.Exp).then_inc(exp_out, 1)
                for i in range(B * E):
                    b, e = i // E, i % E
                    act.wait_ge(compared, i + 1)
                    if b >= 2 and e == 0:
                        act.wait_ge(made, 2 + b - 1)
                    nc.scalar.copy(prt[:, b % 2, e, :], g.bank[1 + i % 4][:, 0:T]).then_inc(spread, 1)

            @block.vector
            def _(dve):
                link = Link(dve, step)
                v = nc.vector
                dve.wait_ge(logits, NT)
                link(v.tensor_copy(s[:], g.bank[0][:, 0:NT * E].rearrange("p (n e) -> p n e", e=E)))
                link(v.tensor_reduce(top[:], s[:], AX.X, ALU.max))
                link(v.tensor_tensor(s[:], s[:], top[:].to_broadcast([P, NT, E]), ALU.subtract))
                dve.sem_inc(exp_in, 1)
                dve.wait_ge(exp_out, 1)
                link(v.tensor_reduce(top[:], pr[:], AX.X, ALU.add))
                link(v.reciprocal(top[:], top[:]))
                link(v.tensor_tensor(pr[:], pr[:], top[:].to_broadcast([P, NT, E]), ALU.mult))
                dve.wait_ge(made, 2)

                def widen(b):
                    for a in range(QT):
                        link(v.tensor_copy(prw[:, b % 2, :, a, :],
                                           pr[:, b * QT + a, :].rearrange("p (e a) -> p e a", a=1).to_broadcast([P, E, P])))
                    dve.sem_inc(wide_done, 1)
                widen(0)
                for b in range(B):
                    if b + 1 < B:
                        widen(b + 1)
                    for a in range(QT):
                        for e in range(E + 1):
                            if e < E:
                                dve.wait_ge(spread, b * E + e + 1)
                                if e >= 3:
                                    dve.wait_ge(compares, (b * QT + a) * 2 * E + 2 * e - 3)
                                v.scalar_tensor_tensor(out=cmp_[:, e % 3, :], in0=prt[:, b % 2, e, :], scalar=pr[:, b * QT + a, e:e + 1],
                                                       in1=before[:, a, :], op0=ALU.is_equal, op1=ALU.mult).then_inc(compares, 1)
                            if e >= 1:
                                k = e - 1
                                dve.wait_ge(compares, (b * QT + a) * 2 * E + max(1, 2 * k))
                                v.scalar_tensor_tensor(out=ahead[:, a, k, :], in0=prt[:, b % 2, k, :], scalar=pr[:, b * QT + a, k:k + 1],
                                                       in1=cmp_[:, k % 3, :], op0=ALU.is_gt, op1=ALU.add).then_inc(compares, 1)
                        dve.wait_ge(compares, (b * QT + a + 1) * 2 * E)
                        link(v.tensor_reduce(rank[:, b * QT + a, :], ahead[:, a], AX.X, ALU.add))
                    dve.sem_inc(made, 1)
                link(v.tensor_scalar(rank[:], rank[:], float(keep), None, ALU.is_lt))
                link(v.tensor_tensor(wts[:], rank[:], pr[:], ALU.mult))


class Global:
    pass


def build(nc, a, out, sublayers=8):
    with ExitStack() as es:
        def sb(name, shape):
            return es.enter_context(nc.sbuf_tensor(name, shape, F32))
        g = Global()
        g.bank = [es.enter_context(nc.psum_tensor(f"bank{i}", [P, 512], F32)) for i in range(8)]
        g.ident = sb("ident", [P, P])
        x = sb("x", [P, NT, C])
        xn = sb("xn", [P, NT, C])
        xnT = sb("xnT", [P, 1, B * T])
        wts = sb("wts", [P, NT, E])
        g.early = Early(nc, es.enter_context(nc.semaphore("early")))
        wr = {l: sb(l + "_wr", [C, E]) for l in ("l0", "l1", "l2", "l3")}
        br = sb("l2_br", [P, 1, E])
        for l, w in (("l0", a["l0_wr"]), ("l1", a["L1_ffn_w_gate"]), ("l2", a["L2_ffn_Wr"]), ("l3", a["l3_wr"])):
            g.early.load(wr[l][:], w)
        g.early.load(br[:].rearrange("p a e -> p (a e)"), rows(a["L2_ffn_br"]))
        xv = lambda t: t.rearrange("b (a p) c -> p (b a) c", p=P)

        with stage(nc, "start", "in_", "made") as (block, in_, made):
            @block.sync
            def _(sp):
                sp.dma_start(x[:], xv(a["x"])).then_inc(in_, 16)
                sp.wait_ge(in_, 16)

            @block.gpsimd
            def _(pool):
                nc.gpsimd.memset(g.ident[:], 0.0).then_inc(made, 1)
                pool.wait_ge(made, 1)
                nc.gpsimd.affine_select(out=g.ident[:], in_=g.ident[:], compare_op=ALU.not_equal, fill=1.0, base=0,
                                        pattern=[[-1, P]], channel_multiplier=1).then_inc(made, 1)
                pool.wait_ge(made, 2)

        g.ctx = Context(nc, "ctx")

        def normed(name):
            layernorm(nc, name + "_ln", x[:], xn[:])
            transpose_tokens(nc, name + "_xnT", g, xn, [(xnT, None, None)])

        def cross(ctx, name, w, y, heads, D, scale, add, key_bias, bq=True):
            cross_attention(nc, name + "cross", g, ctx, w, xnT, y, heads, D, scale, add, key_bias, bq)

        def l0_attention():
            with Space(nc, "context") as s:
                raw = s("raw", [P, B, CT, CC])
                load_context(nc, "load", g, raw, a["ctx_512"])
                normed("l0a")
                split_context(nc, "split", g, g.ctx, raw)
            with Space(nc, "l0a") as s:
                ws = self_weights(g, s, "l0self", a["l0_bqk"], a["L0_xattn_Wv"], a["L0_xattn_bv"], C // H)
                wc = cross_weights(g, s, "l0cross", a["l0_wc"], C // H)
                y = s("y", [P, NT, C])
                yT = s("yT", [P, 1, B * T])
                self_attention(nc, "l0self", g, a["l0_wqk"], ws,
                               xnT, xnT, y, C // H, (C // H) ** -0.5, True)
                cross(g.ctx, "l0", wc, y, H, C // H, (C // H) ** -0.5, True, True)
                w = linear_weights(g, s, "l0out", 1, a["L0_xattn_Wp"], a["L0_xattn_bp"])
                transpose_tokens(nc, "l0yT", g, y, [(yT, None, None)])
                linear(nc, "l0out", g, yT, 1, w, x)

        def l0_ffn():
            normed("l0f")
            router(nc, "l0router", g, "mixer", xnT, (wr["l0"], None), wts)
            experts(nc, "l0experts", g, xnT, a["l0_w1"], None, a["l0_w2"], wts, x, "silu", 2)

        def l1_attention():
            with Space(nc, "l1a") as s:
                wc = cross_weights(g, s, "l1cross", a["l1_wc"], C)
                normed("l1a")
                cross(g.ctx, "l1", wc, x, 1, C, 1.0, True, True)

        def l1_ffn():
            normed("l1f")
            router(nc, "l1router", g, "top2", xnT, (wr["l1"], None), wts)
            expert_biases(nc, "l1bias", g, wts, a["L1_ffn_bu"], x)
            experts(nc, "l1experts", g, xnT, a["L1_ffn_Wd"], a["l1_b1"], a["L1_ffn_Wu"], wts, x, "relu", 1, 64)

        def mlp(name, s, r, pre):
            hT = s(name + "hT", [P, 4, B * T])
            w2 = hidden_weights(g, s, name + "_h", 4, a[pre + "li2_w"], a[pre + "li2_bT"])
            w3 = linear_weights(g, s, name + "_o", 4, a[pre + "li3_w"], a[pre + "li3_b"])
            layernorm(nc, name + "_ln3", r[:], xn[:])
            transpose_tokens(nc, name + "_ln3T", g, xn, [(xnT, a[pre + "ln3_g"], a[pre + "ln3_b"])])
            hidden(nc, name + "_h", g, xnT, w2, hT, 4)
            linear(nc, name + "_o", g, hT, 4, w3, r)

        def l2_attention():
            W = H * 32
            with Space(nc, "l2a") as s:
                x1 = s("x1", [P, NT, C])
                r = s("r", [P, NT, C])
                layernorm(nc, "l2_ln0", x[:], xn[:])
                layernorm(nc, "l2_ln1", xn[:], x1[:], a["L2_xattn_ln1_g"], a["L2_xattn_ln1_b"])
                layernorm(nc, "l2_a1ln", x1[:], xn[:])
                with Space(nc, "l2a1") as s1:
                    kvn = s1("kvn", [P, 1, B * T])
                    y = s1("y", [P, NT, W])
                    ws = self_weights(g, s1, "l2self", None, a["l2_a1_wv"], None, 32)
                    transpose_tokens(nc, "l2_a1T", g, xn, [(xnT, a["L2_xattn_a1_lnx_g"], a["L2_xattn_a1_lnx_b"]),
                                                           (kvn, a["L2_xattn_a1_lny_g"], a["L2_xattn_a1_lny_b"])])
                    self_attention(nc, "l2self", g, a["l2_wqk"], ws,
                                   xnT, kvn, y, 32, 32 ** -0.5, False)
                    after_attention("l2a1o", s1, x1, r, y, "L2_xattn_a1_")
                ctx2 = Context(nc, "ctx2")
                wc = cross_weights(g, s, "l2cross", a["l2_wc"], 32)
                with Space(nc, "l2context") as s1:
                    raw = s1("raw", [P, B, CT, CC])
                    load_context(nc, "l2load", g, raw, a["ctx_512"])
                    add_tokens(nc, "l2_add1", r, x1)
                    layernorm(nc, "l2_ln2", r[:], x1[:], a["L2_xattn_ln2_g"], a["L2_xattn_ln2_b"])
                    layernorm(nc, "l2_a2ln", x1[:], xn[:])
                    transpose_tokens(nc, "l2_a2T", g, xn, [(xnT, a["L2_xattn_a2_lnx_g"], a["L2_xattn_a2_lnx_b"])])
                    flat = raw[:].rearrange("p b t c -> p (b t) c")
                    layernorm(nc, "l2ctx_ln", flat, flat, a["L2_xattn_a2_lny_g"], a["L2_xattn_a2_lny_b"], width=CC, groups=B,
                              last=LAST + 1, early=g.early)
                    split_context(nc, "l2split", g, ctx2, raw)
                with Space(nc, "l2a2") as s1:
                    y = s1("y", [P, NT, W])
                    cross(ctx2, "l2", wc, y, H, 32, 32 ** -0.5, False, False, bq=False)
                    after_attention("l2a2o", s1, x1, r, y, "L2_xattn_a2_")
                add_tokens(nc, "l2_add2", x, x1)
                add_tokens(nc, "l2_add3", x, r)

        def after_attention(name, s, x1, r, y, pre):
            with Space(nc, name) as s2:
                yT = s2("yT", [P, 4, B * T])
                w = linear_weights(g, s2, name + "_lin", 4, a[pre + "li1_w"], a[pre + "li1_b"])
                with stage(nc, name + "_copy", "copied") as (block, copied):
                    @block.vector
                    def _(dve):
                        nc.vector.tensor_copy(r[:], x1[:]).then_inc(copied, 1)
                        dve.wait_ge(copied, 1)
                transpose_tokens(nc, name + "_yT", g, y, [(yT, None, None)], width=512)
                linear(nc, name + "_lin", g, yT, 4, w, r)
            with Space(nc, name + "m") as s2:
                mlp(name, s2, r, pre)

        def l2_ffn():
            normed("l2f")
            router(nc, "l2router", g, "batch", xnT, (wr["l2"], br), wts)
            expert_biases(nc, "l2bias", g, wts, a["L2_ffn_b2"], xn)
            experts(nc, "l2experts", g, xnT, a["L2_ffn_W1"], a["l2_b1"], a["l2_w2"], wts, xn, "gelu", 4)
            with Space(nc, "l2f") as s:
                z = s("z", [P, NT, C])
                layernorm(nc, "l2f_out", xn[:], z[:], a["L2_ffn_gamma"], a["L2_ffn_beta"])
                add_tokens(nc, "l2f_add", x, z)

        def l3_attention():
            with Space(nc, "l3a") as s:
                y = s("y", [P, NT, H * 64])
                wc = cross_weights(g, s, "l3cross", a["l3_wc"], 64)
                normed("l3a")
                cross(g.ctx, "l3", wc, y, H, 64, 64 ** -0.5, False, False, bq=False)
                yT = s("yT", [P, 8, B * T])
                w = linear_weights(g, s, "l3out", 8, a["L3_xattn_Wo"], a["L3_xattn_bo"])
                transpose_tokens(nc, "l3yT", g, y, [(yT, None, None)], width=H * 64)
                linear(nc, "l3out", g, yT, 8, w, x)

        def l3_ffn():
            normed("l3f")
            expert_choice(nc, "l3router", g, xnT, wr["l3"], wts, int(2.0 * T / E))
            experts(nc, "l3experts", g, xnT, a["L3_ffn_w1"], None, a["l3_w2"], wts, x, "gelu", 4)

        for f in (l0_attention, l0_ffn, l1_attention, l1_ffn, l2_attention, l2_ffn, l3_attention, l3_ffn)[:sublayers]:
            f()

        with stage(nc, "end", "stored") as (block, stored):
            @block.sync
            def _(sp):
                sp.dma_start(xv(out), x[:]).then_inc(stored, 16)
                sp.wait_ge(stored, 16)
        for s in Signals.sems:
            nc.sync.sem_clear(s)
        Signals.last.close()
        Signals.last, Signals.sems = ExitStack(), []


def layout(v, np):
    def f(n):
        return np.asarray(v[n], np.float32)

    def pairs(wq, wk):
        w = np.stack([wq.reshape(len(wq), H, -1), wk.reshape(len(wk), H, -1)], 2)
        return np.tile(np.pad(w, ((0, 0), (0, 0), (0, 0), (0, 32 - w.shape[3]))), 3)

    def cross(wq, bq, wk, bk, wv, bv, D):
        n = wq.shape[1] // D
        w = np.zeros((P, n, C + KA + 1 + D + 1), np.float32)
        w[0:D, :, 0:C] = wq.reshape(C, n, D).transpose(2, 1, 0)
        w[0:D, :, C:C + CC] = wk.reshape(CC, n, D).transpose(2, 1, 0)
        w[0:D, :, C + CC] = bk.reshape(n, D).T
        w[0:D, :, C + KA] = bq.reshape(n, D).T
        w[0:CC, :, -1 - D:-1] = wv.reshape(CC, n, D)
        w[CC, :, -1 - D:-1] = bv.reshape(n, D)
        w[KA:P, :, -1 - D:-1] = wv.reshape(CC, n, D)[:-1]
        w[CC, :, -1] = 1.0
        return w

    def down(w, FP):
        return w.reshape(E, -1, FP, C).transpose(0, 2, 1, 3).reshape(E, FP, -1)

    zero = lambda n: np.zeros(n, np.float32)
    a = {n: f(n) for n in v if v[n] is not None}
    D = C // H
    a["l0_wqk"] = pairs(f("L0_xattn_Wq"), f("L0_xattn_Wk")).transpose(1, 0, 2, 3)
    a["l0_bqk"] = pairs(f("L0_xattn_bq")[None], f("L0_xattn_bk")[None])[0].transpose(2, 0, 1)
    a["l0_wc"] = cross(f("L0_xattn_Wcq"), f("L0_xattn_bcq"), f("L0_xattn_Wck"), f("L0_xattn_bck"),
                       f("L0_xattn_Wcv"), f("L0_xattn_bcv"), D)
    a["l0_wr"] = f("L0_ffn_router_w").T
    a["l0_w1"] = np.concatenate([f("L0_ffn_w_gate").transpose(0, 2, 1), f("L0_ffn_w_up").transpose(0, 2, 1)], 2)
    a["l0_w2"] = down(f("L0_ffn_w_down").transpose(0, 2, 1), P)
    a["l1_wc"] = cross(f("L1_xattn_Wq"), f("L1_xattn_bq"), f("L1_xattn_Wk"), f("L1_xattn_bk"),
                       f("L1_xattn_Wv"), f("L1_xattn_bv"), C)
    a["l1_b1"] = f("L1_ffn_bd").reshape(E, 64, 1)
    a["l2_a1_wv"] = f("L2_xattn_a1_wv").transpose(1, 0, 2).reshape(C, -1)
    flat = lambda n: f(n).transpose(1, 0, 2).reshape(f(n).shape[1], -1)
    a["l2_wqk"] = pairs(flat("L2_xattn_a1_wq"), flat("L2_xattn_a1_wk")).transpose(1, 0, 2, 3)
    a["l2_wc"] = cross(flat("L2_xattn_a2_wq"), zero(H * 32), flat("L2_xattn_a2_wk"), zero(H * 32),
                       flat("L2_xattn_a2_wv"), zero(H * 32), 32)
    for p in ("L2_xattn_a1_", "L2_xattn_a2_"):
        a[p + "li2_bT"] = f(p + "li2_b").reshape(4, P).T
    a["l2_b1"] = f("L2_ffn_b1").reshape(E, 4, P).transpose(0, 2, 1)
    a["l2_w2"] = down(f("L2_ffn_W2"), P)
    a["l3_wc"] = cross(f("L3_xattn_Wq"), zero(H * 64), f("L3_xattn_Wk"), zero(H * 64),
                       f("L3_xattn_Wv"), zero(H * 64), 64)
    a["l3_wr"] = f("L3_ffn_gate_w").T
    a["l3_w2"] = down(f("L3_ffn_w2"), P)
    return {n: np.ascontiguousarray(w) for n, w in a.items()}


SUBLAYERS = 8


def kernel(**inputs):
    import numpy as np
    import concourse.bacc as bacc
    from concourse.bass_utils import run_bass_kernel_spmd

    nc = bacc.Bacc("TRN2", target_bir_lowering=False, num_devices=1)
    arrays = layout(inputs, np)
    a = {n: nc.dram_tensor(f"in_{n}", list(w.shape), F32, kind="ExternalInput").ap() for n, w in arrays.items()}
    out = nc.dram_tensor("out", [B, T, C], F32, kind="ExternalOutput").ap()
    build(nc, a, out, SUBLAYERS)
    r = run_bass_kernel_spmd(nc, [{f"in_{n}": w for n, w in arrays.items()}], core_ids=[0])
    return r.results[0]["out"]
```
